# Optimizing a Trainium2 kernel written in Bass

```python
import numpy as np
import jax
import jax.numpy as jnp

def _softmax(x, axis=-1):
    return jax.nn.softmax(x, axis=axis)

def _gelu(x):
    return jax.nn.gelu(x, approximate=True)

def _silu(x):
    return jax.nn.silu(x)

def _sigmoid(x):
    return jax.nn.sigmoid(x)

def _layernorm(x, axis=-1, eps=1e-05):
    m = jnp.mean(x, axis=axis, keepdims=True)
    v = jnp.var(x, axis=axis, keepdims=True)
    return (x - m) / jnp.sqrt(v + eps)

def _scatter_add(tgt, idx, src, axis=0):
    return tgt.at[idx].add(src)

def _segment_sum(src, seg, n):
    return jax.ops.segment_sum(src, seg, n)
kernel_name = 'mk_gnn_preln_d4_gnn_r16_99913b'

def setup_inputs(seed: int=0):
    np.random.seed(seed)
    _w = jnp.asarray

    def _rec_inputs():
        import jax
        import jax.numpy as jnp
        _gk = jax.random.key(seed)
        x = -0.000202 + 1 * jax.random.normal(jax.random.fold_in(_gk, 1), (6250, 128), jnp.float32)
        src = jax.random.randint(jax.random.fold_in(_gk, 2), (200000,), 0, 6250, jnp.int32)
        dst = jnp.minimum((6250 * jax.random.uniform(jax.random.fold_in(_gk, 3), (200000,)) ** 2.0).astype(jnp.int32), 99999)
        _o = jnp.argsort(dst, stable=True)
        src = src[_o]
        dst = dst[_o]
        edge_attr_16 = 0.000254156 + 0.999948 * jax.random.normal(jax.random.fold_in(_gk, 11), (200000, 16), jnp.float32)
        edge_weight = jax.random.uniform(jax.random.fold_in(_gk, 13), (200000,), jnp.float32, 0.0, 0.999999)
        return (x, src, dst, edge_attr_16, edge_weight)
    x, src, dst, edge_attr_16, edge_weight = _rec_inputs()

    def _L0_gnn_setup():
        import jax, jax.numpy as jnp
        import numpy as np
        N = 3125
        E = 50000
        D = 128
        H = 8
        DH = D // H
        DE = 16
        SCALE = 1.0 / np.sqrt(DH)
        key = jax.random.key(seed)
        ks = jax.random.split(key, 9)
        s = 1.0 / np.sqrt(D)
        x = jax.random.normal(ks[0], (N, D), dtype=jnp.float32)
        edge_index = jax.random.randint(ks[1], (2, E), 0, N, dtype=jnp.int64)
        edge_attr = jax.random.normal(ks[2], (E, DE), dtype=jnp.float32)
        w_q = jax.random.normal(ks[3], (D, D), dtype=jnp.float32) * s
        w_k = jax.random.normal(ks[4], (D, D), dtype=jnp.float32) * s
        w_v = jax.random.normal(ks[5], (D, D), dtype=jnp.float32) * s
        w_o = jax.random.normal(ks[6], (D, D), dtype=jnp.float32) * s
        b_o = jax.random.normal(ks[7], (D,), dtype=jnp.float32) * 0.01
        return {'x': x, 'edge_index': edge_index, 'edge_attr': edge_attr, 'w_q': w_q, 'w_k': w_k, 'w_v': w_v, 'w_o': w_o, 'b_o': b_o}
    _L0_gnn_all = _L0_gnn_setup()
    _L0_gnn_in = {k: v for k, v in _L0_gnn_all.items() if k in ('w_q', 'w_k', 'w_v', 'w_o', 'b_o')}
    del _L0_gnn_all

    def _L1_gnn_setup():
        import jax, jax.numpy as jnp
        import numpy as np
        N_NODES = 3125
        N_EDGES = 50000
        D_IN = 128
        D_OUT = 128
        key = jax.random.key(seed)
        k1, k2, k3, k4, k5 = jax.random.split(key, 5)
        x = jax.random.normal(k1, (N_NODES, D_IN), dtype=jnp.float32)
        edge_index = jax.random.randint(k2, (2, N_EDGES), 0, N_NODES, dtype=jnp.int64)
        scale = 1.0 / np.sqrt(D_IN)
        W_rel = jax.random.normal(k3, (D_OUT, D_IN), dtype=jnp.float32) * scale
        b_rel = jax.random.normal(k4, (D_OUT,), dtype=jnp.float32) * scale
        W_root = jax.random.normal(k5, (D_OUT, D_IN), dtype=jnp.float32) * scale
        return {'x': x, 'edge_index': edge_index, 'W_rel': W_rel, 'b_rel': b_rel, 'W_root': W_root}
    _L1_gnn_all = _L1_gnn_setup()
    _L1_gnn_in = {k: v for k, v in _L1_gnn_all.items() if k in ('W_rel', 'b_rel', 'W_root')}
    del _L1_gnn_all

    def _L2_gnn_setup():
        import jax, jax.numpy as jnp
        import numpy as np
        N_NODES = 3125
        N_EDGES = 100000
        D = 128
        N_LAYERS = 2
        NEG_SLOPE = 0.2

        def _gcn_layer(x, src, dst, ew, Ws, bs, Wn, bn, bias):
            n = x.shape[0]
            msg = x[src] * ew[:, None]
            agg = jax.ops.segment_sum(msg, dst, num_segments=n)
            agg = agg + x
            cnt = jax.ops.segment_sum(jnp.ones_like(ew), dst, num_segments=n) + 1.0
            neigh = agg / cnt[:, None]
            out = x @ Ws.T + bs + neigh @ Wn.T + bn + bias
            return jnp.where(out > 0, out, NEG_SLOPE * out)
        key = jax.random.key(seed)
        ks = jax.random.split(key, 10)
        user_embeddings = jax.random.normal(ks[0], (N_NODES, D), dtype=jnp.float32)
        social_edge_index = jax.random.randint(ks[1], (2, N_EDGES), 0, N_NODES, dtype=jnp.int64)
        social_edge_weights = jax.random.uniform(ks[2], (N_EDGES,), dtype=jnp.float32)
        s = 1.0 / np.sqrt(D)
        W_self = jax.random.uniform(ks[3], (N_LAYERS, D, D), minval=-s, maxval=s, dtype=jnp.float32)
        b_self = jax.random.uniform(ks[4], (N_LAYERS, D), minval=-s, maxval=s, dtype=jnp.float32)
        W_neigh = jax.random.uniform(ks[5], (N_LAYERS, D, D), minval=-s, maxval=s, dtype=jnp.float32)
        b_neigh = jax.random.uniform(ks[6], (N_LAYERS, D), minval=-s, maxval=s, dtype=jnp.float32)
        layer_bias = jnp.zeros((N_LAYERS, D), dtype=jnp.float32)
        W_agg = jax.random.uniform(ks[7], (D, D), minval=-s, maxval=s, dtype=jnp.float32)
        b_agg = jax.random.uniform(ks[8], (D,), minval=-s, maxval=s, dtype=jnp.float32)
        return {'user_embeddings': user_embeddings, 'social_edge_index': social_edge_index, 'social_edge_weights': social_edge_weights, 'W_self': W_self, 'b_self': b_self, 'W_neigh': W_neigh, 'b_neigh': b_neigh, 'layer_bias': layer_bias, 'W_agg': W_agg, 'b_agg': b_agg}
    _L2_gnn_all = _L2_gnn_setup()
    _L2_gnn_in = {k: v for k, v in _L2_gnn_all.items() if k in ('W_self', 'b_self', 'W_neigh', 'b_neigh', 'layer_bias', 'W_agg', 'b_agg')}
    del _L2_gnn_all

    def _L3_gnn_setup():
        import jax, jax.numpy as jnp
        import numpy as np
        N = 6250
        E = 100000
        IN_F = 128
        OUT_F = 32
        H = 4
        NEG_SLOPE = 0.2
        key = jax.random.key(seed)
        ks = jax.random.split(key, 7)
        x = jax.random.normal(ks[0], (N, IN_F), dtype=jnp.float32)
        edge_index = jax.random.randint(ks[1], (2, E), 0, N, dtype=jnp.int64)
        edge_weight = jax.random.uniform(ks[2], (E,), dtype=jnp.float32)
        gain = np.sqrt(2.0)
        w_bound = gain * np.sqrt(6.0 / (IN_F + OUT_F))
        a_bound = gain * np.sqrt(6.0 / (OUT_F + 1))
        W = jax.random.uniform(ks[3], (H, IN_F, OUT_F), dtype=jnp.float32, minval=-w_bound, maxval=w_bound)
        a_l = jax.random.uniform(ks[4], (H, OUT_F, 1), dtype=jnp.float32, minval=-a_bound, maxval=a_bound)
        a_r = jax.random.uniform(ks[5], (H, OUT_F, 1), dtype=jnp.float32, minval=-a_bound, maxval=a_bound)
        bias = jnp.zeros((H * OUT_F,), dtype=jnp.float32)
        return {'x': x, 'edge_index': edge_index, 'edge_weight': edge_weight, 'W': W, 'a_l': a_l, 'a_r': a_r, 'bias': bias}
    _L3_gnn_all = _L3_gnn_setup()
    _L3_gnn_in = {k: v for k, v in _L3_gnn_all.items() if k in ('W', 'a_l', 'a_r', 'bias')}
    del _L3_gnn_all
    return {'x': x, 'src': src, 'dst': dst, 'edge_attr_16': edge_attr_16, 'edge_weight': edge_weight, 'L0_gnn_w_q': _L0_gnn_in['w_q'], 'L0_gnn_w_k': _L0_gnn_in['w_k'], 'L0_gnn_w_v': _L0_gnn_in['w_v'], 'L0_gnn_w_o': _L0_gnn_in['w_o'], 'L0_gnn_b_o': _L0_gnn_in['b_o'], 'L1_gnn_W_rel': _L1_gnn_in['W_rel'], 'L1_gnn_b_rel': _L1_gnn_in['b_rel'], 'L1_gnn_W_root': _L1_gnn_in['W_root'], 'L2_gnn_W_self': _L2_gnn_in['W_self'], 'L2_gnn_b_self': _L2_gnn_in['b_self'], 'L2_gnn_W_neigh': _L2_gnn_in['W_neigh'], 'L2_gnn_b_neigh': _L2_gnn_in['b_neigh'], 'L2_gnn_layer_bias': _L2_gnn_in['layer_bias'], 'L2_gnn_W_agg': _L2_gnn_in['W_agg'], 'L2_gnn_b_agg': _L2_gnn_in['b_agg'], 'L3_gnn_W': _L3_gnn_in['W'], 'L3_gnn_a_l': _L3_gnn_in['a_l'], 'L3_gnn_a_r': _L3_gnn_in['a_r'], 'L3_gnn_bias': _L3_gnn_in['bias']}

def reference(x, src, dst, edge_attr_16, edge_weight, L0_gnn_w_q, L0_gnn_w_k, L0_gnn_w_v, L0_gnn_w_o, L0_gnn_b_o, L1_gnn_W_rel, L1_gnn_b_rel, L1_gnn_W_root, L2_gnn_W_self, L2_gnn_b_self, L2_gnn_W_neigh, L2_gnn_b_neigh, L2_gnn_layer_bias, L2_gnn_W_agg, L2_gnn_b_agg, L3_gnn_W, L3_gnn_a_l, L3_gnn_a_r, L3_gnn_bias):
    import jax
    import jax.numpy as jnp

    def _L0_gnn_ref(x, edge_index, edge_attr, w_q, w_k, w_v, w_o, b_o):
        import jax, jax.numpy as jnp
        import numpy as np
        N = 3125
        E = 50000
        D = 128
        H = 8
        DH = D // H
        DE = 16
        SCALE = 1.0 / np.sqrt(DH)
        n = x.shape[0]
        Q = (x @ w_q).reshape(n, H, DH)
        K = (x @ w_k).reshape(n, H, DH)
        V = (x @ w_v).reshape(n, H, DH)
        src, dst = (edge_index[0], edge_index[1])
        scores = jnp.einsum('ehd,ehd->eh', Q[src], K[dst]) * SCALE
        ew = jax.nn.sigmoid(jnp.sum(edge_attr, axis=-1, keepdims=True))
        scores = scores * ew
        weighted = V[dst] * scores[..., None]
        sums = jax.ops.segment_sum(weighted, dst, num_segments=n)
        cnt = jax.ops.segment_sum(jnp.ones((scores.shape[0],), jnp.float32), dst, num_segments=n)
        out = sums / jnp.maximum(cnt, 1.0)[:, None, None]
        return out.reshape(n, D) @ w_o + b_o

    def _L1_gnn_ref(x, edge_index, W_rel, b_rel, W_root):
        import jax, jax.numpy as jnp
        import numpy as np
        N_NODES = 3125
        N_EDGES = 50000
        D_IN = 128
        D_OUT = 128
        src = edge_index[0]
        dst = edge_index[1]
        n = x.shape[0]
        agg = jax.ops.segment_sum(x[src], dst, num_segments=n)
        out = agg @ W_rel.T + b_rel + x @ W_root.T
        return jax.nn.relu(out)

    def _L2_gnn_ref(user_embeddings, social_edge_index, social_edge_weights, W_self, b_self, W_neigh, b_neigh, layer_bias, W_agg, b_agg):
        import jax, jax.numpy as jnp
        import numpy as np
        N_NODES = 3125
        N_EDGES = 100000
        D = 128
        N_LAYERS = 2
        NEG_SLOPE = 0.2

        def _gcn_layer(x, src, dst, ew, Ws, bs, Wn, bn, bias):
            n = x.shape[0]
            msg = x[src] * ew[:, None]
            agg = jax.ops.segment_sum(msg, dst, num_segments=n)
            agg = agg + x
            cnt = jax.ops.segment_sum(jnp.ones_like(ew), dst, num_segments=n) + 1.0
            neigh = agg / cnt[:, None]
            out = x @ Ws.T + bs + neigh @ Wn.T + bn + bias
            return jnp.where(out > 0, out, NEG_SLOPE * out)
        src = social_edge_index[0]
        dst = social_edge_index[1]
        x = user_embeddings
        for l in range(N_LAYERS):
            x = _gcn_layer(x, src, dst, social_edge_weights, W_self[l], b_self[l], W_neigh[l], b_neigh[l], layer_bias[l])
        return x @ W_agg.T + b_agg

    def _L3_gnn_ref(x, edge_index, edge_weight, W, a_l, a_r, bias):
        import jax, jax.numpy as jnp
        import numpy as np
        N = 6250
        E = 100000
        IN_F = 128
        OUT_F = 32
        H = 4
        NEG_SLOPE = 0.2
        n = x.shape[0]
        row, col = (edge_index[0], edge_index[1])
        Wh = jnp.einsum('ni,hio->hno', x, W)
        e_l = jnp.einsum('hno,ho->hn', Wh, a_l[..., 0])
        e_r = jnp.einsum('hno,ho->hn', Wh, a_r[..., 0])
        e = e_l[:, row] + e_r[:, col]
        e = jax.nn.leaky_relu(e, negative_slope=NEG_SLOPE)
        e = e + jnp.log(jnp.clip(edge_weight, 1e-08, None))[None, :]
        eT = e.T
        e_max = jax.ops.segment_max(eT, col, num_segments=n)
        alpha = jnp.exp(eT - e_max[col])
        alpha_sum = jax.ops.segment_sum(alpha, col, num_segments=n)
        alpha = alpha / (alpha_sum[col] + 1e-08)
        msgs = alpha[:, :, None] * jnp.transpose(Wh, (1, 0, 2))[row]
        out = jax.ops.segment_sum(msgs, col, num_segments=n)
        out = out.reshape(n, -1) + bias
        return out
    edge_index = jnp.stack([src, dst])
    h = jnp.maximum(_layernorm(x, axis=-1), 0.0)
    x = x + _L0_gnn_ref(h, edge_index, edge_attr_16, L0_gnn_w_q, L0_gnn_w_k, L0_gnn_w_v, L0_gnn_w_o, L0_gnn_b_o)
    h = jnp.maximum(_layernorm(x, axis=-1), 0.0)
    x = x + _L1_gnn_ref(h, edge_index, L1_gnn_W_rel, L1_gnn_b_rel, L1_gnn_W_root)
    h = jnp.maximum(_layernorm(x, axis=-1), 0.0)
    x = x + _L2_gnn_ref(h, edge_index, edge_weight, L2_gnn_W_self, L2_gnn_b_self, L2_gnn_W_neigh, L2_gnn_b_neigh, L2_gnn_layer_bias, L2_gnn_W_agg, L2_gnn_b_agg)
    h = jnp.maximum(_layernorm(x, axis=-1), 0.0)
    x = x + _L3_gnn_ref(h, edge_index, edge_weight, L3_gnn_W, L3_gnn_a_l, L3_gnn_a_r, L3_gnn_bias)
    return x

_drawn_inputs = setup_inputs


def setup_inputs(seed=0):
    import zlib

    import numpy as np

    out = dict(_drawn_inputs(seed))
    spreads = {'L2_gnn_layer_bias': (0.0, 0.8), 'L3_gnn_bias': (0.0, 2.0)}
    factors = {'edge_attr_16': 200.0,
     'edge_weight': 8.0,
     'L0_gnn_b_o': 3.469,
     'L1_gnn_b_rel': 8.0,
     'L2_gnn_W_self': 8.0,
     'L2_gnn_b_self': 8.0,
     'L2_gnn_W_neigh': 8.0,
     'L2_gnn_b_neigh': 8.0,
     'L2_gnn_W_agg': 7.234,
     'L2_gnn_b_agg': 200.0,
     'L3_gnn_a_l': 200.0,
     'L3_gnn_a_r': 200.0,
     'L3_gnn_W': 26.746}
    for name, (base, spread) in spreads.items():
        noise = np.random.default_rng([zlib.crc32(name.encode()), seed]).standard_normal(out[name].shape)
        drawn = base * np.exp(spread * noise) if base else spread * noise
        out[name] = jnp.asarray(drawn.astype(out[name].dtype))
    for name, factor in factors.items():
        out[name] = (out[name] * factor).astype(out[name].dtype)
    return out
```

```python
from contextlib import ExitStack

import concourse.bass as bass
from concourse import mybir

P = 128
N = 6250
E = 200000
D = 128
EDGE_ATTRS = 16
TILES = -(-E // P)
BLOCKS = -(-N // P)
GROUP = 7
GROUPS = BLOCKS // GROUP
RING = 16
HALF = RING // 2
STEPS = -(-(TILES + BLOCKS - 1) // RING) * RING
ITERS = STEPS // RING
CHUNKS = -(-(STEPS + RING) // P)
COLS = CHUNKS * P
AGG_W = 132
HEADS0, DH0 = 8, 16
HEADS3, DH3 = 4, 32
SCALE0 = DH0 ** -0.5
EPS = 1e-5
SLOPE = 0.2
ROW3 = HEADS3 * (DH3 + 2)
SPAN = -(-E // (P * RING)) * RING
SPAN_ITERS = SPAN // RING
BIG = 1e38
PAD_DST = 20000.0
assert GROUPS * GROUP == BLOCKS and TILES <= COLS

ALU = mybir.AluOpType
ACT = mybir.ActivationFunctionType
AX = mybir.AxisListType.X
F32 = mybir.dt.float32
I32 = mybir.dt.int32
DVE_ONLY = (mybir.EngineType.DVE,)
SP_ONLY = (mybir.EngineType.SP,)

(KV, QUERY, OUT0, ROOT, REL, SELF2A, NEIGH2A, SELF2B, NEIGH2B, AGG2, HEADS) = range(11)
PASSES = 11


def build(nc, x, src, dst, edge_attr, edge_weight, w, out, debug=None):
    ctx = ExitStack()
    with ctx:
        def sb(name, shape, dt=F32):
            return ctx.enter_context(nc.sbuf_tensor(name, shape, dt))

        def sem(name):
            return ctx.enter_context(nc.semaphore(name))

        def dram(name, shape, dt=F32):
            return nc.dram_tensor(name, shape, dt, kind="Internal").ap()

        tile_rows = dram("tile_rows", [COLS, 4 * P])
        step_block_d = dram("step_block_d", [1, COLS], I32)
        tables = [dram(f"table{i}", [BLOCKS * P, D]) for i in range(4)]
        head_table = dram("head_table", [BLOCKS * P, ROW3])
        right_table = dram("right_table", [BLOCKS * P, HEADS3])
        right_edges = dram("right_edges", [P * SPAN, HEADS3])
        edge_rows = dram("edge_rows", [P * SPAN, ROW3])
        alphas_d = dram("alphas", [SPAN, P * HEADS3])
        step_tile_d = dram("step_tile_d", [1, COLS], I32)

        X = sb("X", [P, BLOCKS, D])
        H = sb("H", [P, BLOCKS, D])
        scratch = sb("scratch", [P, BLOCKS * D + BLOCKS * AGG_W])
        R = scratch[:, 0:BLOCKS * D].rearrange("p (b f) -> p b f", f=D)
        AGG = scratch[:, BLOCKS * D:].rearrange("p (b f) -> p b f", f=AGG_W)
        step_table = sb("step_table", [P, 4, COLS])
        S_SRC, S_PLACE, S_W, S_W0 = range(4)
        step_block = sb("step_block", [1, COLS], I32)
        idx_stage = sb("idx_stage", [P, RING], I32)
        rows = sb("rows", [P, RING, ROW3])
        scaled = sb("scaled", [P, HALF, AGG_W])
        onehot = sb("onehot", [P, HALF, P])
        work = sb("work", [P, 4, GROUP * D])
        stage, turned, cen, sq = (work[:, i, :].rearrange("p (j f) -> p j f", f=D) for i in range(4))
        small = sb("small", [P, 8, GROUP * HEADS0])
        iota = sb("iota", [P, P])
        pidx = sb("pidx", [P, 1])
        ident = sb("ident", [P, P])
        ones = sb("ones", [P, P])
        epst = sb("epst", [P, 1])
        cnt = sb("cnt", [P, BLOCKS])
        inv_mean0 = sb("inv_mean0", [P, BLOCKS])
        inv_mean2 = sb("inv_mean2", [P, BLOCKS])
        W = {k: sb(f"w_{k}", [P, D]) for k in
             ("q", "k", "v", "o", "rel", "root", "self0", "self1", "neigh0", "neigh1", "agg", "heads", "left", "right")}
        bias = {k: sb(f"b_{k}", [P, D]) for k in
                ("o", "rel", "self0", "neigh0", "layer0", "self1", "neigh1", "layer1", "agg", "out")}
        bsum = sb("bsum", [P, 2, D])
        chunk_i = work[:, :, :].rearrange("p i f -> p (i f)")[:, 0:2 * COLS].bitcast(I32).rearrange("p (k e) -> p k e", k=2)
        block_edge = sb("block_edge", [P, BLOCKS - 1])
        block_no = sb("block_no", [P, BLOCKS - 1])
        step_no = sb("step_no", [P, CHUNKS])
        cmp = sb("cmp", [P, (BLOCKS - 1) * CHUNKS])
        first_tile = sb("first_tile", [P, BLOCKS - 1])
        step_b = sb("step_b", [P, CHUNKS])
        step_t = sb("step_t", [P, CHUNKS])
        step_off = sb("step_off", [P, CHUNKS])
        step_b_i = sb("step_b_i", [P, CHUNKS], I32)
        step_t_i = sb("step_t_i", [P, CHUNKS], I32)
        step_tc_i = sb("step_tc_i", [P, CHUNKS], I32)
        step_tile = sb("step_tile", [1, COLS], I32)
        tri = sb("tri", [P, P])
        before = sb("before", [P, 3, BLOCKS])
        first_edge = sb("first_edge", [P, BLOCKS], I32)
        w_lr = sb("w_lr", [P, 2 * HEADS3])
        right = sb("right", [P, BLOCKS, HEADS3])
        right0 = sb("right0", [P, HEADS3])
        zeros = sb("zeros", [P, SPAN * HEADS3 // 16])
        dst0 = sb("dst0", [P, 1], I32)
        carry = sb("carry", [P, 6, HEADS3])
        carry_in = sb("carry_in", [P, 2, HEADS3])
        chain = sb("chain", [HEADS3, 6, P])
        chain_out = sb("chain_out", [HEADS3, 4, P])
        HT = scratch[:, 0:BLOCKS * ROW3].rearrange("p (b h f) -> p b h f", h=HEADS3, f=DH3 + 2)
        Hflat = H[:, :, :].rearrange("p b f -> p (b f)")
        score = Hflat.rearrange("p (t h) -> p t h", h=HEADS3)
        right_e = scratch[:, 0:SPAN * HEADS3].rearrange("p (t h) -> p t h", h=HEADS3)
        _o = SPAN * HEADS3
        dst_x = scratch[:, _o:_o + SPAN + 2]
        same = scratch[:, _o + SPAN + 2:_o + 2 * SPAN + 3]
        keep = scratch[:, _o + 2 * SPAN + 3:_o + 3 * SPAN + 4]
        tmp = scratch[:, _o + 3 * SPAN + 4:_o + 4 * SPAN + 4]
        run_src = step_table[:, 0, 0:SPAN + RING].bitcast(I32)
        dst_xi = step_table[:, 2, 0:SPAN + 2].bitcast(I32)
        logw = step_table[:, 3, 0:SPAN]
        place2 = Hflat[:, 0:COLS]
        alpha_s = step_table[:, :, :].rearrange("p k c -> p (k c)").rearrange("p (c h) -> p c h", h=HEADS3)

        ps = [ctx.enter_context(nc.psum_tensor(f"ps{i}", [P, 1024], F32)) for i in range(4)]

        loaded_x = sem("loaded_x")
        loaded_edges = sem("loaded_edges")
        loaded_attr = [sem(f"loaded_attr{i}") for i in range(5)]
        loaded_w = sem("loaded_w")
        consts = sem("consts")
        cleared = sem("cleared")
        attr_used = sem("attr_used")
        logits_ready = sem("logits_ready")
        sigmoid_ready = sem("sigmoid_ready")
        tile_rows_ready = sem("tile_rows_ready")
        tile_rows_stored = sem("tile_rows_stored")
        counted = sem("counted")
        summed = sem("summed")
        step_index_ready = sem("step_index_ready")
        step_rows_landed = [sem(f"step_rows_landed{i}") for i in range(2)]
        step_rows_ready = sem("step_rows_ready")
        step_turned = sem("step_turned")
        step_table_ready = sem("step_table_ready")
        blocks_stored = sem("blocks_stored")
        blocks_loaded = sem("blocks_loaded")
        ve = sem("ve")
        norm_sum = sem("norm_sum")
        norm_root = sem("norm_root")
        table_ready = sem("table_ready")
        table_stored = sem("table_stored")
        lin_staged = sem("lin_staged")
        lin_transposed = sem("lin_transposed")
        lin_turned = sem("lin_turned")
        lin_product = sem("lin_product")
        lin_used = sem("lin_used")
        idx_staged = sem("idx_staged")
        row_landed = [sem(f"row_landed{j}") for j in range(RING)]
        row_scaled = sem("row_scaled")
        onehot_ready = sem("onehot_ready")
        partial_ready = sem("partial_ready")
        block_added = sem("block_added")
        agg_cleared = sem("agg_cleared")
        agg_done = sem("agg_done")
        out_stored = sem("out_stored")
        out_ready = sem("out_ready")
        zeroed = sem("zeroed")
        right_cleared = sem("right_cleared")
        starts_summed = sem("starts_summed")
        starts_ready = sem("starts_ready")
        heads_ready = sem("heads_ready")
        heads_stored = sem("heads_stored")
        right_stored = sem("right_stored")
        runs_padded = sem("runs_padded")
        runs_loaded = sem("runs_loaded")
        rows_stored = [sem(f"rows_stored{i}") for i in range(2)]
        score_taken = sem("score_taken")
        round_open = sem("round_open")
        right_scattered = sem("right_scattered")
        right0_loaded = sem("right0_loaded")
        right_loaded = sem("right_loaded")
        dst0_ready = sem("dst0_ready")
        logw_ready = sem("logw_ready")
        carries_ready = sem("carries_ready")
        carries_turned = sem("carries_turned")
        chains_ready = sem("chains_ready")
        chains_turned = sem("chains_turned")
        exponents_ready = sem("exponents_ready")
        alphas_ready = sem("alphas_ready")
        alphas_stored = sem("alphas_stored")
        alpha_rows_landed = [sem(f"alpha_rows_landed{i}") for i in range(2)]
        alpha_turned = sem("alpha_turned")
        alpha_copied = sem("alpha_copied")
        place_moved = sem("place_moved")
        tile_landed = [sem(f"tile_landed{j}") for j in range(RING)]
        row_weighted = sem("row_weighted")

        SCALED0, PARTIAL0, ADDED0 = RING, HALF, 4

        full_tiles = E // P
        fullc = full_tiles // P
        rest = full_tiles - fullc * P
        tail = E - full_tiles * P

        def tiled(a, width):
            yield slice(0, P), slice(0, fullc), a[0:fullc * P * P * width].rearrange("(c p e) -> p c e", p=P, e=P * width)
            yield slice(0, rest), fullc, a[fullc * P * P * width:full_tiles * P * width].rearrange("(p e) -> p e", e=P * width)
            yield slice(rest, rest + 1), fullc, a[full_tiles * P * width:].rearrange("(p e) -> p e", p=1)

        TR = step_table[:, :, :].rearrange("p k c -> p (k c)").rearrange("p (c k e) -> p c k e", k=4, e=P)
        WLOADS = len(W) + len(bias)
        attr = edge_attr.rearrange("e a -> (e a)")
        EAW = P * EDGE_ATTRS
        LOGITS = H[:, 0:CHUNKS, :]
        ATTR = [(slice(3 * i, 3 * i + 3), (i % 2) * 3 * EAW) for i in range(4)] + [(slice(12, 13), 0)]
        GATHER_STEPS = scratch[:, 0:CHUNKS * 4 * P].rearrange("p (c k e) -> p c k e", k=4, e=P)

        def grp_of(t, g):
            return t[:, bass.ds(g * GROUP, GROUP), :]

        def every_span(first):
            return bass.AP(tensor=dst.tensor, offset=first, ap=[[SPAN, E // SPAN], [1, 1]])

        block = ctx.enter_context(nc.Block())

        @block.sync
        def _(sp):
            sp.wait_ge(cleared, 2)
            for k, a in ((0, src), (1, dst)):
                for pp, cc, s in tiled(a, 1):
                    n = s.shape[-1]
                    t = chunk_i[pp, k, :].rearrange("p (c e) -> p c e", e=P)
                    sp.dma_start(t[:, cc, 0:n], s).then_inc(loaded_edges, 16)
            for pp, cc, s in tiled(edge_weight, 1):
                sp.dma_start(TR[pp, cc, 2, 0:s.shape[-1]], s).then_inc(loaded_edges, 16)
            sp.dma_start(X[:, 0:BLOCKS - 1, :], x[0:(BLOCKS - 1) * P, :].rearrange("(b p) f -> p b f", p=P))\
                .then_inc(loaded_x, 16)
            last = N - (BLOCKS - 1) * P
            sp.dma_start(X[0:last, BLOCKS - 1, :], x[(BLOCKS - 1) * P:, :]).then_inc(loaded_x, 16)
            for i, (cc, at) in enumerate(ATTR):
                if i >= 2:
                    sp.wait_ge(attr_used, i - 1)
                dst_ = scratch[:, at:at + 3 * EAW].rearrange("p (c e) -> p c e", c=3)
                if i < 4:
                    s = attr[cc.start * P * EAW:cc.stop * P * EAW].rearrange("(c p e) -> p c e", p=P, e=EAW)
                    sp.dma_start(dst_, s).then_inc(loaded_attr[i], 16)
                else:
                    s = attr[fullc * P * EAW:full_tiles * EAW].rearrange("(p e) -> p e", e=EAW)
                    sp.dma_start(dst_[0:rest, 0, :], s).then_inc(loaded_attr[i], 16)
                    s = attr[full_tiles * EAW:].rearrange("(p e) -> p e", p=1)
                    sp.dma_start(dst_[rest:rest + 1, 0, 0:tail * EDGE_ATTRS], s).then_inc(loaded_attr[i], 16)
            for k in ("q", "k", "v", "o", "rel", "root", "self0", "self1", "neigh0", "neigh1", "agg", "heads"):
                sp.dma_start(W[k][:, :], w[k]).then_inc(loaded_w, 16)
            for k, t in (("left", W["left"]), ("right", W["right"])):
                sp.dma_start(t[:, :], w[k].rearrange("(a f) -> a f", a=1).to_broadcast([P, D])).then_inc(loaded_w, 16)
            for k in ("o", "rel", "self0", "neigh0", "layer0", "self1", "neigh1", "layer1", "agg", "out"):
                sp.dma_start(bias[k][:, :], w["b_" + k].rearrange("(a f) -> a f", a=1).to_broadcast([P, D]))\
                    .then_inc(loaded_w, 16)
            sp.wait_ge(zeroed, 1)
            sp.dma_start(right_edges.rearrange("(p r t) h -> p r (t h)", p=P, r=16),
                         zeros[:, :].rearrange("p (a t) -> p a t", a=1).to_broadcast([P, 16, SPAN * HEADS3 // 16]))\
                .then_inc(right_cleared, 16)
            sp.wait_ge(tile_rows_ready, 2)
            sp.wait_ge(loaded_edges, 16 * 9)
            sp.dma_start(tile_rows.rearrange("(c p) e -> p c e", p=P), TR.rearrange("p c k e -> p c (k e)"))\
                .then_inc(tile_rows_stored, 16)
            sp.wait_ge(step_index_ready, 1)
            sp.dma_start(step_block_d.rearrange("a (c p) -> p (a c)", p=P), step_b_i[:, :],
                         allow_slow_non_contiguous=True).then_inc(blocks_stored, 16)
            sp.wait_ge(blocks_stored, 16)
            sp.dma_start(step_block[:, :], step_block_d).then_inc(blocks_loaded, 16)
            sp.dma_start(step_tile_d.rearrange("a (c p) -> p (a c)", p=P), step_tc_i[:, :],
                         allow_slow_non_contiguous=True).then_inc(blocks_stored, 16)
            sp.wait_ge(blocks_stored, 32)
            sp.dma_start(step_tile[:, :], step_tile_d).then_inc(blocks_loaded, 16)

            for layer in range(4):
                rows_d = tables[layer].rearrange("(g j p) f -> g p j f", p=P, j=GROUP)
                with sp.Fori(0, GROUPS) as g:
                    sp.wait_ge(table_ready, g + (GROUPS * layer + 1))
                    sp.dma_start(rows_d[bass.ds(g, 1), :, :, :].rearrange("a p j f -> (a p) j f"),
                                 H[:, bass.ds(g * GROUP, GROUP), :]).then_inc(table_stored, 16)
            heads_d = head_table.rearrange("(g j p) f -> g p j f", p=P, j=GROUP)
            with sp.Fori(0, GROUPS) as g:
                sp.wait_ge(heads_ready, g + 1)
                sp.dma_start(heads_d[bass.ds(g, 1), :, :, :].rearrange("a p j f -> (a p) j f"),
                             HT[:, bass.ds(g * GROUP, GROUP), :, :].rearrange("p j h f -> p j (h f)")).then_inc(heads_stored, 16)
            sp.wait_ge(heads_ready, GROUPS)
            sp.dma_start(right_table.rearrange("(b p) h -> p b h", p=P), right[:, :, :]).then_inc(right_stored, 16)
            sp.wait_ge(runs_padded, 1)
            fullp = E // SPAN
            more = E - fullp * SPAN
            for a_, t_, o_ in ((src, run_src, 0), (dst, dst_xi, 1), (edge_weight, logw, 0)):
                sp.dma_start(t_[0:fullp, o_:o_ + SPAN], a_[0:fullp * SPAN].rearrange("(p t) -> p t", t=SPAN)).then_inc(runs_loaded, 16)
                sp.dma_start(t_[fullp:fullp + 1, o_:o_ + more], a_[fullp * SPAN:].rearrange("(p t) -> p t", p=1)).then_inc(runs_loaded, 16)
            sp.dma_start(dst_xi[1:P, 0:1], every_span(SPAN - 1),
                         allow_slow_non_contiguous=True).then_inc(runs_loaded, 16)
            sp.dma_start(dst_xi[0:fullp, SPAN + 1:SPAN + 2], every_span(SPAN), allow_slow_non_contiguous=True).then_inc(runs_loaded, 16)
            rows_d = edge_rows.rearrange("(p t) f -> p t f", p=P)
            with sp.Fori(0, SPAN_ITERS) as k:
                for half in range(2):
                    for j in range(half * HALF, (half + 1) * HALF):
                        sp.wait_ge(row_landed[j], k * 16 + (16 * (ITERS * 4 + 1)))
                    sp.dma_start(rows_d[:, bass.ds(k * RING + half * HALF, HALF), :].rearrange("p t f -> p (t f)"),
                                 rows[:, half * HALF:(half + 1) * HALF, :].rearrange("p t f -> p (t f)"))\
                        .then_inc(rows_stored[half], 16)
            sp.wait_ge(right_scattered, 16 * BLOCKS)
            sp.wait_ge(heads_stored, 16 * GROUPS)
            sp.dma_start(right_e.rearrange("p t h -> p (t h)"), right_edges.rearrange("(p t) h -> p (t h)", p=P))\
                .then_inc(right_loaded, 16)
            sp.wait_ge(alphas_ready, 1)
            sp.dma_start(alphas_d.rearrange("(a t) f -> a (t f)", a=1).rearrange("a (p f) -> p (a f)", p=P),
                         Hflat).then_inc(alphas_stored, 16)
            for half in range(2):
                sp.wait_ge(rows_stored[half], 16 * SPAN_ITERS)
            tiles_d = edge_rows.rearrange("(t p) f -> t p f", p=P)
            sp.wait_ge(blocks_loaded, 32)
            sp.wait_ge(score_taken, SPAN_ITERS * 2)
            with sp.Fori(0, ITERS) as k:
                _, at = nc.values_load_multi_w_load_instructions(
                    step_tile[0:1, bass.ds(k * RING, RING)], engines=SP_ONLY, min_val=0, max_val=SPAN - 1,
                    skip_runtime_bounds_check_because="a step's tile is below SPAN by construction")
                for j in range(RING):
                    sp.wait_ge(partial_ready, k * RING + (STEPS * 4 + j + 1 - RING + HALF))
                    sp.dma_start(rows[:, j, :], tiles_d[bass.ds(at[j], 1), :, :].rearrange("a p f -> (a p) f"))\
                        .then_inc(tile_landed[j], 16)
            with sp.Fori(0, GROUPS - 1) as g:
                sp.wait_ge(out_ready, g + 1)
                sp.dma_start(out[0:(BLOCKS - GROUP) * P, :].rearrange("(g j p) f -> g p j f", p=P, j=GROUP)[bass.ds(g, 1), :, :, :]
                             .rearrange("a p j f -> (a p) j f"), grp_of(X, g)).then_inc(out_stored, 16)
            sp.wait_ge(out_ready, GROUPS)
            sp.dma_start(out[(BLOCKS - GROUP) * P:(BLOCKS - 1) * P, :].rearrange("(b p) f -> p b f", p=P),
                         X[:, BLOCKS - GROUP:BLOCKS - 1, :]).then_inc(out_stored, 16)
            sp.dma_start(out[(BLOCKS - 1) * P:, :], X[0:last, BLOCKS - 1, :]).then_inc(out_stored, 16)
            sp.wait_ge(out_stored, 16 * (GROUPS + 1))

        @block.gpsimd
        def _(pool):
            pool.memset(chunk_i[:, 0, :], 0).then_inc(consts, 1)
            pool.iota(iota[:, :], [[1, P]], base=0, channel_multiplier=0,
                      allow_small_or_imprecise_dtypes=True).then_inc(consts, 1)
            pool.iota(pidx[:, :], [[1, 1]], base=0, channel_multiplier=1,
                      allow_small_or_imprecise_dtypes=True).then_inc(consts, 1)
            pool.iota(block_edge[:, :], [[P, BLOCKS - 1]], base=P, channel_multiplier=0,
                      allow_small_or_imprecise_dtypes=True).then_inc(consts, 1)
            pool.iota(block_no[:, :], [[1, BLOCKS - 1]], base=1, channel_multiplier=0,
                      allow_small_or_imprecise_dtypes=True).then_inc(consts, 1)
            pool.iota(step_no[:, :], [[P, CHUNKS]], base=0, channel_multiplier=1,
                      allow_small_or_imprecise_dtypes=True).then_inc(consts, 1)
            pool.memset(ones[:, :], 1.0).then_inc(consts, 1)
            pool.memset(epst[:, :], EPS).then_inc(consts, 1)
            pool.memset(zeros[:, :], 0.0).then_inc(zeroed, 1)
            pool.memset(scaled[:, :, D:AGG_W], 1.0).then_inc(consts, 1)
            pool.wait_ge(tile_rows_stored, 16)
            pool.wait_ge(step_index_ready, 1)
            pool.wait_ge(attr_used, 5)
            for c in range(CHUNKS):
                pool.indirect_dma_start(out=GATHER_STEPS[:, c, :, :].rearrange("p k e -> p (k e)"), out_offset=None,
                                        in_=tile_rows, in_offset=bass.IndirectOffsetOnAxis(ap=step_t_i[:, c:c + 1], axis=0))\
                    .then_inc(step_rows_landed[c >= 6], 16)

            def gathers(layer, table):
                pool.wait_ge(table_stored, 16 * GROUPS * (layer + 1))
                with pool.Fori(0, ITERS) as k:
                    for j in range(RING):
                        if j % HALF == 0:
                            pool.wait_ge(idx_staged, k * 2 + (2 * (ITERS + 1) * layer + j // HALF + 1))
                            pool.wait_ge(row_scaled, k * RING + (STEPS * layer + j + HALF))
                            pool.sem_inc(round_open, 1)
                        pool.indirect_dma_start(out=rows[:, j, 0:D], out_offset=None, in_=table,
                                                in_offset=bass.IndirectOffsetOnAxis(ap=idx_stage[:, j:j + 1], axis=0))\
                            .then_inc(row_landed[j], 16)

            for layer in range(4):
                gathers(layer, tables[layer])

            pool.wait_ge(right_stored, 16)
            pool.wait_ge(right_cleared, 16)
            pool.wait_ge(starts_ready, 1)
            for b in range(BLOCKS):
                pool.indirect_dma_start(out=right_edges, out_offset=bass.IndirectOffsetOnAxis(ap=first_edge[:, b:b + 1], axis=0),
                                        in_=right[:, b, :], in_offset=None, bounds_check=P * SPAN - 1, oob_is_err=False)\
                    .then_inc(right_scattered, 16)
            pool.wait_ge(dst0_ready, 1)
            pool.indirect_dma_start(out=right0[:, :], out_offset=None, in_=right_table,
                                    in_offset=bass.IndirectOffsetOnAxis(ap=dst0[:, 0:1], axis=0)).then_inc(right0_loaded, 16)
            pool.wait_ge(heads_stored, 16 * GROUPS)

            def run_gathers(k):
                for j in range(RING):
                    if j % HALF == 0:
                        half = j // HALF
                        pool.wait_ge(idx_staged, k * 2 + (2 * (ITERS + 1) * 4 + half + 1))
                        if not isinstance(k, int):
                            pool.wait_ge(rows_stored[half], k * 16)
                            pool.wait_ge(score_taken, k * 2 + (half - 1))
                        pool.sem_inc(round_open, 1)
                    pool.indirect_dma_start(out=rows[:, j, :], out_offset=None, in_=head_table,
                                            in_offset=bass.IndirectOffsetOnAxis(ap=idx_stage[:, j:j + 1], axis=0))\
                        .then_inc(row_landed[j], 16)

            run_gathers(0)
            with pool.Fori(1, SPAN_ITERS) as k:
                run_gathers(k)
            pool.wait_ge(alphas_stored, 16)
            for c in range(CHUNKS):
                pool.indirect_dma_start(out=scratch[:, c * 4 * P:(c + 1) * 4 * P], out_offset=None, in_=alphas_d,
                                        in_offset=bass.IndirectOffsetOnAxis(ap=step_tc_i[:, c:c + 1], axis=0))\
                    .then_inc(alpha_rows_landed[c >= 6], 16)
            pool.wait_ge(alpha_copied, CHUNKS)
            with pool.Fori(0, ITERS) as k:
                for half in range(2):
                    for j in range(half * HALF, (half + 1) * HALF):
                        pool.wait_ge(tile_landed[j], k * 16 + 16)
                    pool.sem_inc(round_open, 1)
                    for j in range(half * HALF, (half + 1) * HALF):
                        r = rows[:, j, :].rearrange("p (h f) -> p h f", h=HEADS3)[:, :, 0:DH3 + 1]
                        al = alpha_s[:, bass.ds(k * RING + j, 1), :].rearrange("p a h -> p h a").to_broadcast([P, HEADS3, DH3 + 1])
                        pool.tensor_tensor(r, r, al, ALU.mult).then_inc(row_weighted, 1)

        @block.scalar
        def _(act):
            act.sem_inc(row_scaled, SCALED0)
            for s in (lin_staged, lin_turned):
                act.sem_inc(s, 1)

            def root(g, n):
                act.wait_ge(norm_sum, g + (GROUPS * n + 1))
                act.activation(small[:, 3, 0:GROUP], small[:, 2, 0:GROUP], ACT.Sqrt, bias=epst[:, 0:1],
                               scale=1.0 / D).then_inc(norm_root, 1)

            def turn(p, source, ready, base, roots=None):
                with act.Fori(0, GROUPS) as g:
                    act.wait_ge(ready, g + (base + 1))
                    act.wait_ge(lin_transposed, g + (GROUPS * p + 1))
                    act.copy(stage, source[:, bass.ds(g * GROUP, GROUP), 0:D]).then_inc(lin_staged, 1)
                    act.wait_ge(lin_transposed, g + (GROUPS * p + 2))
                    act.wait_ge(lin_product, g + (GROUPS * p + 1))
                    act.copy(turned.rearrange("p j f -> p (j f)"), ps[0][:, 0:GROUP * D]).then_inc(lin_turned, 1)
                    if roots is not None:
                        root(g, roots)

            def turn_agg(p, layers, roots=None):
                act.wait_ge(agg_done, layers)
                turn(p, AGG, lin_used, GROUPS * p, roots)

            def stage_indices(layer, k, half):
                act.copy(idx_stage[:, half * HALF:(half + 1) * HALF],
                         step_table[:, S_SRC, bass.ds(k * RING + half * HALF, HALF)] if not isinstance(k, int)
                         else step_table[:, S_SRC, k * RING + half * HALF:k * RING + (half + 1) * HALF])\
                    .then_inc(idx_staged, 1)

            def scale(layer, weights):
                act.wait_ge(step_table_ready, CHUNKS)
                stage_indices(layer, 0, 0)
                stage_indices(layer, 0, 1)
                with act.Fori(0, ITERS) as k:
                    for j in range(RING):
                        act.wait_ge(row_landed[j], k * 16 + (16 * (ITERS * layer + 1)))
                        act.wait_ge(partial_ready, k * RING + (STEPS * layer + j + 1))
                        by = 1.0 if weights is None else step_table[:, weights, bass.ds(k * RING + j, 1)]
                        act.activation(scaled[:, j % HALF, 0:D], rows[:, j, 0:D], ACT.Copy, scale=by)\
                            .then_inc(row_scaled, 1)
                        if j % HALF == HALF - 1:
                            stage_indices(layer, k + 1, j // HALF)

            act.wait_ge(logits_ready, 5)
            act.activation(TR[:, :, 3, :], LOGITS, ACT.Sigmoid).then_inc(sigmoid_ready, 1)
            act.wait_ge(sigmoid_ready, 1)
            act.sem_inc(tile_rows_ready, 1)
            with act.Fori(0, GROUPS) as g:
                root(g, 0)
            act.wait_ge(tile_rows_stored, 16)
            for c in range(CHUNKS):
                act.wait_ge(step_turned, c + 1)
                act.copy(step_table[:, :, c * P:(c + 1) * P],
                         ps[c % 2][:, 0:4 * P].rearrange("p (k s) -> p k s", k=4)).then_inc(step_table_ready, 1)
            turn(KV, H, table_ready, 0)
            scale(0, S_W0)
            turn_agg(QUERY, 1)
            turn(OUT0, H, lin_used, GROUPS * QUERY + 1, roots=1)
            turn(ROOT, H, table_ready, GROUPS)
            scale(1, None)
            turn_agg(REL, 2, roots=2)
            turn(SELF2A, H, table_ready, 2 * GROUPS)
            scale(2, S_W)
            turn_agg(NEIGH2A, 3)
            turn(SELF2B, H, table_ready, 3 * GROUPS)
            scale(3, S_W)
            turn_agg(NEIGH2B, 4)
            turn(AGG2, H, lin_used, GROUPS * (NEIGH2B) + 1, roots=3)
            turn(HEADS, H, table_ready, 4 * GROUPS)
            act.wait_ge(runs_loaded, 16 * 8)
            act.wait_ge(logw_ready, 1)
            act.activation(logw, logw, ACT.Ln).then_inc(logw_ready, 1)
            act.wait_ge(lin_used, GROUPS * PASSES + 1)

            def stage_run(k, half):
                n = k * RING + half * HALF
                act.copy(idx_stage[:, half * HALF:(half + 1) * HALF],
                         run_src[:, n:n + HALF] if isinstance(k, int) else run_src[:, bass.ds(n, HALF)]).then_inc(idx_staged, 1)

            stage_run(0, 0)
            stage_run(0, 1)
            with act.Fori(0, SPAN_ITERS) as k:
                for half in range(2):
                    for j in range(half * HALF, (half + 1) * HALF):
                        act.wait_ge(row_landed[j], k * 16 + (16 * (ITERS * 4 + 1)))
                    act.copy(score[:, bass.ds(k * RING + half * HALF, HALF), :],
                             rows[:, half * HALF:(half + 1) * HALF, :].rearrange("p t (h f) -> p t h f", h=HEADS3)[:, :, :, DH3 + 1])\
                        .then_inc(score_taken, 1)
                    stage_run(k + 1, half)
            act.wait_ge(exponents_ready, 1)
            act.activation(Hflat, Hflat, ACT.Exp).then_inc(alphas_ready, 1)
            act.wait_ge(alphas_stored, 16)
            act.copy(place2, step_table[:, S_PLACE, :]).then_inc(place_moved, 1)
            act.wait_ge(place_moved, 1)
            for c in range(CHUNKS):
                act.wait_ge(alpha_turned, c + 1)
                act.copy(alpha_s[:, c * P:(c + 1) * P, :].rearrange("p s h -> p h s"),
                         ps[c % 2][:, 0:4 * P].rearrange("p (h s) -> p h s", h=4)).then_inc(alpha_copied, 1)

        @block.tensor
        def _(pe):
            pe.sem_inc(partial_ready, PARTIAL0)
            for s in (lin_transposed, lin_product):
                pe.sem_inc(s, 1)
            pe.wait_ge(consts, 9)
            pe.wait_ge(counted, 1)
            pe.matmul(ps[2][:, 0:BLOCKS - 1], ones[:, :], first_tile[:, :], start=True, stop=True).then_inc(summed, 1)
            for c in range(CHUNKS):
                pe.wait_ge(step_rows_ready, c + 1)
                if c >= 2:
                    pe.wait_ge(step_table_ready, c - 1)
                for k in range(4):
                    mm = pe.transpose(ps[c % 2][:, k * P:(k + 1) * P], GATHER_STEPS[:, c, k, :], ident[:, :])
                mm.then_inc(step_turned, 1)

            pe.wait_ge(loaded_w, 16 * WLOADS)
            pe.wait_ge(step_table_ready, CHUNKS)

            def linear(p, weights):
                with pe.Fori(0, GROUPS) as g:
                    pe.wait_ge(lin_staged, g + (GROUPS * p + 2))
                    pe.wait_ge(lin_turned, g + (GROUPS * p + 1))
                    for j in range(GROUP):
                        mm = pe.transpose(ps[0][:, j * D:(j + 1) * D], stage[:, j, :], ident[:, :])
                    mm.then_inc(lin_transposed, 1)
                    pe.wait_ge(lin_turned, g + (GROUPS * p + 2))
                    pe.wait_ge(lin_used, g + (GROUPS * p + 1))
                    for j in range(GROUP):
                        for i, m in enumerate(weights):
                            n = m.shape[-1]
                            mm = pe.matmul(ps[1 + i][:, j * n:(j + 1) * n], turned[:, j, :], m[:, :], start=True, stop=True)
                    mm.then_inc(lin_product, 1)

            def partials(layer, width):
                with pe.Fori(0, ITERS) as k:
                    for j in range(RING):
                        n = k * RING + (STEPS * layer + j + 1)
                        pe.wait_ge(onehot_ready, n)
                        pe.wait_ge(row_scaled, n + SCALED0)
                        pe.wait_ge(block_added, n)
                        pe.matmul(ps[j % 4][:, 0:width], onehot[:, j % HALF, :], scaled[:, j % HALF, 0:width],
                                  start=True, stop=True).then_inc(partial_ready, 1)

            linear(KV, [W["k"], W["v"]])
            pe.wait_ge(lin_used, GROUPS * (KV + 1) + 1)
            partials(0, D + 1)
            pe.wait_ge(agg_done, 1)
            linear(QUERY, [W["q"]])
            linear(OUT0, [W["o"]])
            linear(ROOT, [W["root"]])
            pe.wait_ge(consts, 9)
            pe.matmul(ps[3][:, 0:BLOCKS], tri[:, :], cnt[:, :], start=True, stop=True)
            pe.matmul(ps[3][:, 512:512 + BLOCKS], ones[:, :], cnt[:, :], start=True, stop=True).then_inc(starts_summed, 1)
            pe.wait_ge(starts_ready, 1)
            pe.wait_ge(lin_used, GROUPS * (ROOT + 1) + 1)
            partials(1, D)
            pe.wait_ge(agg_done, 2)
            linear(REL, [W["rel"]])
            linear(SELF2A, [W["neigh0"], W["self0"]])
            pe.wait_ge(lin_used, GROUPS * (SELF2A + 1) + 1)
            partials(2, D)
            pe.wait_ge(agg_done, 3)
            linear(NEIGH2A, [W["neigh0"]])
            linear(SELF2B, [W["neigh1"], W["self1"]])
            pe.wait_ge(lin_used, GROUPS * (SELF2B + 1) + 1)
            partials(3, D)
            pe.wait_ge(agg_done, 4)
            linear(NEIGH2B, [W["neigh1"]])
            linear(AGG2, [W["agg"]])
            pe.wait_ge(starts_ready, 2)
            linear(HEADS, [W["heads"], w_lr])
            pe.wait_ge(lin_used, GROUPS * PASSES + 1)
            pe.wait_ge(carries_ready, 1)
            for i in range(6):
                mm = pe.transpose(ps[1 + i // 4][0:HEADS3, (i % 4) * P:(i % 4 + 1) * P], carry[:, i, :], ident[:, :])
            mm.then_inc(carries_turned, 1)
            pe.wait_ge(chains_ready, 1)
            for i in range(2):
                mm = pe.transpose(ps[3][:, i * HEADS3:(i + 1) * HEADS3], chain_out[:, i, :], ident[0:HEADS3, 0:HEADS3])
            mm.then_inc(chains_turned, 1)
            for c in range(CHUNKS):
                pe.wait_ge(alpha_rows_landed[c >= 6], 16 * (6 if c < 6 else CHUNKS - 6))
                if c >= 2:
                    pe.wait_ge(alpha_copied, c - 1)
                for h in range(HEADS3):
                    mm = pe.transpose(ps[c % 2][:, h * P:(h + 1) * P],
                                      scratch[:, c * 4 * P:(c + 1) * 4 * P].rearrange("p (e h) -> p h e", h=HEADS3)[:, h, :],
                                      ident[:, :])
                mm.then_inc(alpha_turned, 1)
            pe.wait_ge(alpha_copied, CHUNKS)
            with pe.Fori(0, ITERS) as k:
                for j in range(RING):
                    n = k * RING + (STEPS * 4 + j + 1)
                    pe.wait_ge(onehot_ready, n)
                    pe.wait_ge(row_weighted, k * RING + (j + 1))
                    pe.wait_ge(block_added, n)
                    pe.matmul(ps[j % 4][:, 0:AGG_W], onehot[:, j % HALF, :],
                              rows[:, j, :].rearrange("p (h f) -> p h f", h=HEADS3)[:, :, 0:DH3 + 1],
                              start=True, stop=True).then_inc(partial_ready, 1)

        @block.vector
        def _(dve):
            done = [0]

            class Chain:
                def __init__(self, per=0, g=None):
                    self.base, self.n, self.per, self.g = done[0], 0, per, g

                def then(self, ins):
                    ins.then_inc(ve, 1)
                    self.n += 1
                    if self.g is None:
                        done[0] += 1
                        dve.wait_ge(ve, self.base + self.n)
                    else:
                        dve.wait_ge(ve, self.g * self.per + (self.base + self.n))

                def close(self):
                    assert self.n == self.per
                    done[0] += self.per * GROUPS

            def bc(a, n):
                return a.rearrange("p (j a) -> p j a", a=1).to_broadcast([P, a.shape[-1], n])

            def flat(a):
                return a.rearrange("p j f -> p (j f)")

            def grp(t, g, w=D):
                return t[:, bass.ds(g * GROUP, GROUP), 0:w]

            def pg(i, w=D):
                return ps[i][:, 0:GROUP * w].rearrange("p (j f) -> p j f", f=w)

            def rowbc(t):
                return t.rearrange("p (a f) -> p a f", a=1).to_broadcast([P, GROUP, D])

            NORM_OPS = 7

            def norm(c, g, n):
                s = small
                c.then(dve.tensor_reduce(s[:, 0, 0:GROUP], grp(X, g), AX, ALU.add))
                c.then(dve.tensor_scalar(s[:, 1, 0:GROUP], s[:, 0, 0:GROUP], 1.0 / D, None, ALU.mult))
                c.then(dve.tensor_tensor(cen, grp(X, g), bc(s[:, 1, 0:GROUP], D), ALU.subtract))
                c.then(dve.tensor_tensor(flat(sq), flat(cen), flat(cen), ALU.mult))
                c.then(dve.tensor_reduce(s[:, 2, 0:GROUP], sq, AX, ALU.add))
                dve.sem_inc(norm_sum, 1)
                dve.wait_ge(norm_root, g + (GROUPS * n + 1))
                c.then(dve.reciprocal(s[:, 4, 0:GROUP], s[:, 3, 0:GROUP]))
                c.then(dve.scalar_tensor_tensor(out=grp(H, g), in0=cen, scalar=0.0, in1=bc(s[:, 4, 0:GROUP], D),
                                                op0=ALU.max, op1=ALU.mult))
                dve.sem_inc(table_ready, 1)

            def sums(layer, width, place):
                dve.memset(AGG[:, :, :].rearrange("p b f -> p (b f)"), 0.0).then_inc(agg_cleared, 1)
                dve.wait_ge(agg_cleared, layer + 1)
                dve.wait_ge(step_table_ready, CHUNKS)
                dve.wait_ge(blocks_loaded, 32)
                with dve.Fori(0, ITERS) as k:
                    _, at = nc.values_load_multi_w_load_instructions(
                        step_block[0:1, bass.ds(k * RING, RING)], engines=DVE_ONLY, min_val=0, max_val=BLOCKS - 1,
                        skip_runtime_bounds_check_because="a step's block is below BLOCKS by construction")
                    for half in range(2):
                        for j in range(half * HALF, (half + 1) * HALF):
                            dve.wait_ge(partial_ready, k * RING + (STEPS * layer + j + 1))
                            dve.tensor_scalar(onehot[:, j % HALF, :], iota[:, :],
                                              place[:, bass.ds(k * RING + j, 1)], None, ALU.is_equal)\
                                .then_inc(onehot_ready, 1)
                        for j in range(half * HALF, (half + 1) * HALF):
                            dve.wait_ge(partial_ready, k * RING + (STEPS * layer + j + 1 + PARTIAL0))
                            dve.wait_ge(block_added, k * RING + (STEPS * layer + j + ADDED0))
                            s = AGG[:, bass.ds(at[j], 1), 0:width].rearrange("p a f -> p (a f)")
                            dve.tensor_tensor(s, s, ps[j % 4][:, 0:width], ALU.add).then_inc(block_added, 1)
                dve.wait_ge(block_added, STEPS * (layer + 1) + ADDED0)
                dve.sem_inc(agg_done, 1)

            dve.sem_inc(block_added, ADDED0)
            dve.sem_inc(lin_used, 1)
            c = Chain()
            c.then(dve.memset(chunk_i[:, 1, :], int(PAD_DST)))
            c.then(dve.memset(TR[:, :, 2, :], 0.0))
            c.then(dve.memset(LOGITS, 0.0))
            c.then(dve.memset(X[:, BLOCKS - 1, :], 0.0))
            dve.wait_ge(consts, 1)
            dve.sem_inc(cleared, 2)
            dve.wait_ge(consts, 9)
            c.then(dve.tensor_scalar(ident[:, :], iota[:, :], pidx[:, 0:1], None, ALU.is_equal))
            c.then(dve.tensor_scalar(tri[:, :], iota[:, :], pidx[:, 0:1], None, ALU.is_gt))
            dve.wait_ge(loaded_edges, 16 * 9)
            for k in range(2):
                c.then(dve.tensor_copy(TR[:, :, k, :], chunk_i[:, k, :].rearrange("p (c e) -> p c e", e=P)))
            dve.sem_inc(tile_rows_ready, 1)
            c.then(dve.tensor_tensor(cmp[:, :].rearrange("p (b c) -> p b c", c=CHUNKS),
                                     TR[:, :, 1, P - 1:P].rearrange("p c a -> p a c").to_broadcast([P, BLOCKS - 1, CHUNKS]),
                                     block_edge[:, :].rearrange("p (b a) -> p b a", a=1).to_broadcast([P, BLOCKS - 1, CHUNKS]),
                                     ALU.is_lt))
            c.then(dve.tensor_reduce(first_tile[:, :], cmp[:, :].rearrange("p (b c) -> p b c", c=CHUNKS), AX, ALU.add))
            dve.sem_inc(counted, 1)
            dve.wait_ge(summed, 1)
            c.then(dve.tensor_tensor(block_edge[:, :], ps[2][:, 0:BLOCKS - 1], block_no[:, :], ALU.add))
            c.then(dve.tensor_tensor(cmp[:, :].rearrange("p (c b) -> p c b", c=CHUNKS),
                                     block_edge[:, :].rearrange("p (a b) -> p a b", a=1).to_broadcast([P, CHUNKS, BLOCKS - 1]),
                                     step_no[:, :].rearrange("p (c a) -> p c a", a=1).to_broadcast([P, CHUNKS, BLOCKS - 1]),
                                     ALU.is_le))
            c.then(dve.tensor_reduce(step_b[:, :], cmp[:, :].rearrange("p (c b) -> p c b", c=CHUNKS), AX, ALU.add))
            c.then(dve.tensor_tensor(step_t[:, :], step_no[:, :], step_b[:, :], ALU.subtract))
            c.then(dve.tensor_scalar(step_off[:, :], step_b[:, :], -float(P), None, ALU.mult))
            c.then(dve.tensor_copy(step_b_i[:, :], step_b[:, :]))
            c.then(dve.tensor_copy(step_t_i[:, :], step_t[:, :]))
            c.then(dve.tensor_scalar(step_tc_i[:, :], step_t[:, :], float(SPAN - 1), None, ALU.min))
            dve.sem_inc(step_index_ready, 1)
            for i, (cc, at) in enumerate(ATTR):
                dve.wait_ge(loaded_attr[i], 16 if i < 4 else 32)
                n = cc.stop - cc.start
                a = scratch[:, at:at + n * EAW].rearrange("p (c e a) -> p c e a", c=n, a=EDGE_ATTRS)
                if i < 4:
                    dve.tensor_reduce(LOGITS[:, cc, :], a, AX, ALU.add).then_inc(logits_ready, 1)
                else:
                    c.then(dve.tensor_reduce(LOGITS[0:rest + 1, 12, 0:tail], a[0:rest + 1, 0, 0:tail, :], AX, ALU.add))
                    dve.tensor_reduce(LOGITS[0:rest, 12, tail:P], a[0:rest, 0, tail:P, :], AX, ALU.add)\
                        .then_inc(logits_ready, 1)
                dve.wait_ge(logits_ready, i + 1)
                dve.sem_inc(attr_used, 1)
            dve.wait_ge(loaded_x, 32)
            dve.wait_ge(sigmoid_ready, 1)
            with dve.Fori(0, GROUPS) as g:
                c = Chain(NORM_OPS, g)
                norm(c, g, 0)
            c.close()
            c = Chain()
            for ch in range(CHUNKS):
                dve.wait_ge(step_rows_landed[ch >= 6], 16 * (6 if ch < 6 else CHUNKS - 6))
                c.then(dve.tensor_scalar(GATHER_STEPS[:, ch, 1, :], GATHER_STEPS[:, ch, 1, :], step_off[:, ch:ch + 1],
                                         None, ALU.add))
                dve.sem_inc(step_rows_ready, 1)
            dve.wait_ge(loaded_w, 16 * WLOADS)
            for i in range(2):
                c.then(dve.tensor_tensor(bsum[:, i, :], bias[f"self{i}"][:, :], bias[f"neigh{i}"][:, :], ALU.add))
                c.then(dve.tensor_tensor(bsum[:, i, :], bsum[:, i, :], bias[f"layer{i}"][:, :], ALU.add))
            dve.wait_ge(step_turned, CHUNKS)
            dve.wait_ge(table_stored, 16 * GROUPS)

            def products(p, g):
                dve.wait_ge(lin_product, g + (GROUPS * p + 2))

            with dve.Fori(0, GROUPS) as g:
                c = Chain(3, g)
                products(KV, g)
                c.then(dve.tensor_copy(grp(R, g), pg(1)))
                c.then(dve.tensor_copy(grp(H, g), pg(2)))
                dve.sem_inc(lin_used, 1)
                c.then(dve.tensor_tensor(grp(X, g), grp(X, g), rowbc(bias["o"][:, :]), ALU.add))
            c.close()
            sums(0, D + 1, step_table[:, S_PLACE, :])
            c = Chain()
            c.then(dve.tensor_copy(cnt[:, :], AGG[:, :, D]))
            c.then(dve.tensor_scalar(inv_mean0[:, :], cnt[:, :], 1.0, None, ALU.max))
            c.then(dve.reciprocal(inv_mean0[:, :], inv_mean0[:, :]))
            c.then(dve.tensor_scalar(inv_mean0[:, :], inv_mean0[:, :], SCALE0, None, ALU.mult))
            c.then(dve.tensor_scalar(inv_mean2[:, :], cnt[:, :], 1.0, None, ALU.add))
            c.then(dve.reciprocal(inv_mean2[:, :], inv_mean2[:, :]))
            with dve.Fori(0, GROUPS) as g:
                c = Chain(4, g)
                products(QUERY, g)
                c.then(dve.tensor_tensor(cen, pg(1), grp(R, g), ALU.mult))
                sc = small[:, 5, 0:GROUP * HEADS0]
                c.then(dve.tensor_reduce(sc, flat(cen).rearrange("p (h d) -> p h d", d=DH0), AX, ALU.add))
                c.then(dve.tensor_tensor(sc.rearrange("p (j h) -> p j h", h=HEADS0), sc.rearrange("p (j h) -> p j h", h=HEADS0),
                                         bc(inv_mean0[:, bass.ds(g * GROUP, GROUP)], HEADS0), ALU.mult))
                v = flat(grp(H, g)).rearrange("p (h d) -> p h d", d=DH0)
                c.then(dve.tensor_tensor(v, v, bc(sc, DH0), ALU.mult))
                dve.sem_inc(lin_used, 1)
            c.close()
            with dve.Fori(0, GROUPS) as g:
                c = Chain(1 + NORM_OPS, g)
                products(OUT0, g)
                c.then(dve.tensor_tensor(grp(X, g), grp(X, g), pg(1), ALU.add))
                dve.sem_inc(lin_used, 1)
                norm(c, g, 1)
            c.close()
            with dve.Fori(0, GROUPS) as g:
                c = Chain(1, g)
                products(ROOT, g)
                c.then(dve.tensor_tensor(grp(R, g), pg(1), rowbc(bias["rel"][:, :]), ALU.add))
                dve.sem_inc(lin_used, 1)
            c.close()
            dve.wait_ge(starts_summed, 1)
            c = Chain()
            c.then(dve.tensor_copy(before[:, 0, :], ps[3][:, 512:512 + BLOCKS]))
            c.then(dve.tensor_tensor_scan(before[:, 1, :], before[:, 0, :], zeros[:, 0:BLOCKS], 0.0, ALU.add, ALU.add))
            c.then(dve.tensor_tensor(before[:, 1, :], before[:, 1, :], before[:, 0, :], ALU.subtract))
            c.then(dve.tensor_tensor(before[:, 1, :], before[:, 1, :], ps[3][:, 0:BLOCKS], ALU.add))
            c.then(dve.tensor_scalar(before[:, 2, :], cnt[:, :], 0.0, float(2 * P * SPAN), ALU.is_equal, ALU.mult))
            c.then(dve.tensor_tensor(first_edge[:, :], before[:, 1, :], before[:, 2, :], ALU.add))
            dve.sem_inc(starts_ready, 1)
            for i, k_ in enumerate(("left", "right")):
                c.then(dve.tensor_tensor(W[k_][:, :], W[k_][:, :], W["heads"][:, :], ALU.mult))
                c.then(dve.tensor_reduce(w_lr[:, i * HEADS3:(i + 1) * HEADS3], W[k_][:, :].rearrange("p (h o) -> p h o", o=DH3),
                                         AX, ALU.add))
            dve.sem_inc(starts_ready, 1)
            sums(1, D, step_table[:, S_PLACE, :])
            with dve.Fori(0, GROUPS) as g:
                c = Chain(2 + NORM_OPS, g)
                products(REL, g)
                c.then(dve.tensor_tensor(cen, pg(1), grp(R, g), ALU.add))
                c.then(dve.scalar_tensor_tensor(out=grp(X, g), in0=cen, scalar=0.0, in1=grp(X, g), op0=ALU.max, op1=ALU.add))
                dve.sem_inc(lin_used, 1)
                norm(c, g, 2)
            c.close()

            def self_terms(p, i, with_bias):
                with dve.Fori(0, GROUPS) as g:
                    c = Chain(3 + with_bias, g)
                    products(p, g)
                    c.then(dve.tensor_tensor(cen, pg(1), bc(inv_mean2[:, bass.ds(g * GROUP, GROUP)], D), ALU.mult))
                    c.then(dve.tensor_tensor(cen, cen, pg(2), ALU.add))
                    dve.sem_inc(lin_used, 1)
                    c.then(dve.tensor_tensor(grp(R, g), cen, rowbc(bsum[:, i, :]), ALU.add))
                    if with_bias:
                        c.then(dve.tensor_tensor(grp(X, g), grp(X, g), rowbc(bias["agg"][:, :]), ALU.add))
                c.close()

            def neighbours(p, table):
                with dve.Fori(0, GROUPS) as g:
                    c = Chain(3, g)
                    products(p, g)
                    c.then(dve.tensor_tensor(cen, pg(1), bc(inv_mean2[:, bass.ds(g * GROUP, GROUP)], D), ALU.mult))
                    c.then(dve.tensor_tensor(cen, cen, grp(R, g), ALU.add))
                    c.then(dve.scalar_tensor_tensor(out=grp(H, g), in0=cen, scalar=SLOPE, in1=cen, op0=ALU.mult, op1=ALU.max))
                    dve.sem_inc(lin_used, 1)
                    if table:
                        dve.sem_inc(table_ready, 1)
                c.close()

            self_terms(SELF2A, 0, 1)
            sums(2, D, step_table[:, S_PLACE, :])
            neighbours(NEIGH2A, True)
            self_terms(SELF2B, 1, 0)
            sums(3, D, step_table[:, S_PLACE, :])
            neighbours(NEIGH2B, False)
            with dve.Fori(0, GROUPS) as g:
                c = Chain(1 + NORM_OPS, g)
                products(AGG2, g)
                c.then(dve.tensor_tensor(grp(X, g), grp(X, g), pg(1), ALU.add))
                dve.sem_inc(lin_used, 1)
                norm(c, g, 3)
            c.close()

            c = Chain()
            c.then(dve.memset(HT[:, :, :, DH3:DH3 + 1], 1.0))
            with dve.Fori(0, GROUPS) as g:
                c = Chain(4, g)
                products(HEADS, g)
                ht = HT[:, bass.ds(g * GROUP, GROUP), :, :]
                c.then(dve.tensor_copy(ht[:, :, :, 0:DH3], pg(1).rearrange("p j (h f) -> p j h f", f=DH3)))
                lr = ps[2][:, 0:GROUP * 2 * HEADS3].rearrange("p (j k h) -> p j k h", k=2, h=HEADS3)
                c.then(dve.tensor_copy(ht[:, :, :, DH3 + 1], lr[:, :, 0, :]))
                c.then(dve.tensor_copy(right[:, bass.ds(g * GROUP, GROUP), :], lr[:, :, 1, :]))
                dve.sem_inc(heads_ready, 1)
                dve.sem_inc(lin_used, 1)
                c.then(dve.tensor_tensor(grp(X, g), grp(X, g), rowbc(bias["out"][:, :]), ALU.add))
            c.close()
            c = Chain()
            c.then(dve.memset(run_src[96:P, :], 0))
            c.then(dve.memset(run_src[:, SPAN:SPAN + RING], 0))
            c.then(dve.memset(dst_xi, int(PAD_DST)))
            c.then(dve.memset(dst_xi[:, 0:1], -1))
            c.then(dve.memset(logw[96:P, :], 1.0))
            dve.sem_inc(runs_padded, 1)
            dve.wait_ge(runs_loaded, 16 * 8)
            c.then(dve.tensor_copy(dst0[:, :], dst_xi[:, 1:2]))
            dve.sem_inc(dst0_ready, 1)
            c.then(dve.tensor_scalar(logw, logw, 1e-8, None, ALU.max))
            dve.sem_inc(logw_ready, 1)
            dve.wait_ge(heads_stored, 16 * GROUPS)
            c.then(dve.tensor_copy(dst_x, dst_xi))
            c.then(dve.tensor_tensor(same, dst_x[:, 1:], dst_x[:, 0:SPAN + 1], ALU.is_equal))
            c.then(dve.tensor_scalar(keep, same, 0.5, 2 * BIG, ALU.subtract, ALU.mult))
            dve.wait_ge(logw_ready, 2)
            dve.wait_ge(right_loaded, 16)
            dve.wait_ge(right0_loaded, 16)
            dve.wait_ge(score_taken, 2 * SPAN_ITERS)
            for h in range(HEADS3):
                c.then(dve.tensor_tensor_scan(right_e[:, :, h], same[:, 0:SPAN], right_e[:, :, h], right0[:, h:h + 1],
                                              ALU.mult, ALU.add))
            sf, rf = (t.rearrange("p t h -> p (t h)") for t in (score, right_e))
            c.then(dve.tensor_tensor(sf, sf, rf, ALU.add))
            c.then(dve.scalar_tensor_tensor(out=sf, in0=sf, scalar=SLOPE, in1=sf, op0=ALU.mult, op1=ALU.max))
            c.then(dve.tensor_tensor(score, score, logw.rearrange("p (t a) -> p t a", a=1).to_broadcast([P, SPAN, HEADS3]), ALU.add))
            fwd, bwd = (scratch[:, i * SPAN:(i + 1) * SPAN] for i in range(2))

            def forward(h, initial):
                c.then(dve.tensor_tensor_scan(fwd, keep[:, 0:SPAN], score[:, :, h], initial, ALU.min, ALU.max))

            def backward(initial):
                c.then(dve.tensor_tensor_scan(bwd[:, ::-1], keep[:, 1:SPAN + 1][:, ::-1], fwd[:, ::-1], initial, ALU.min, ALU.max))

            for h in range(HEADS3):
                forward(h, -BIG)
                c.then(dve.tensor_copy(carry[:, 0, h:h + 1], fwd[:, SPAN - 1:SPAN]))
                backward(-BIG)
                c.then(dve.tensor_copy(carry[:, 3, h:h + 1], bwd[:, 0:1]))
            def flag(i, a, b):
                c.then(dve.tensor_tensor(carry_in[:, 0, 0:1], dst_x[:, a:a + 1], dst_x[:, b:b + 1], ALU.is_equal))
                c.then(dve.tensor_scalar(carry[:, i, :], carry_in[:, 0, 0:1].to_broadcast([P, HEADS3]), 0.5, 2 * BIG,
                                         ALU.subtract, ALU.mult))
            flag(1, 0, SPAN)
            flag(2, 0, 1)
            flag(4, 1, SPAN + 1)
            flag(5, SPAN, SPAN + 1)
            dve.sem_inc(carries_ready, 1)
            dve.wait_ge(carries_turned, 1)
            for i in range(6):
                c.then(dve.tensor_copy(chain[:, i, :], ps[1 + i // 4][0:HEADS3, (i % 4) * P:(i % 4 + 1) * P]))
            lo, hi = slice(0, P - 1), slice(1, P)
            c.then(dve.memset(chain_out[:, 0:2, :], -BIG))
            c.then(dve.tensor_tensor_scan(chain_out[:, 2, :], chain[:, 1, :], chain[:, 0, :], -BIG, ALU.min, ALU.max))
            c.then(dve.tensor_tensor(chain_out[:, 0, hi], chain_out[:, 2, lo], chain[:, 2, hi], ALU.min))
            c.then(dve.tensor_tensor_scan(chain_out[:, 3, ::-1], chain[:, 4, ::-1], chain[:, 3, ::-1], -BIG, ALU.min, ALU.max))
            c.then(dve.tensor_tensor(chain_out[:, 1, lo], chain_out[:, 3, hi], chain[:, 5, lo], ALU.min))
            dve.sem_inc(chains_ready, 1)
            dve.wait_ge(chains_turned, 1)
            c.then(dve.tensor_copy(carry_in[:, :, :].rearrange("p k h -> p (k h)"), ps[3][:, 0:2 * HEADS3]))
            for h in range(HEADS3):
                forward(h, carry_in[:, 0, h:h + 1])
                backward(carry_in[:, 1, h:h + 1])
                c.then(dve.tensor_tensor(score[:, :, h], score[:, :, h], bwd, ALU.subtract))
            dve.sem_inc(exponents_ready, 1)
            dve.wait_ge(alpha_copied, CHUNKS)
            sums(4, AGG_W, place2)
            agg3 = AGG.rearrange("p b (h f) -> p b h f", f=DH3 + 1)
            with dve.Fori(0, GROUPS) as g:
                c = Chain(5, g)
                a3 = agg3[:, bass.ds(g * GROUP, GROUP), :, :]
                r = small[:, 6, 0:GROUP * HEADS3].rearrange("p (j h) -> p j h", h=HEADS3)
                c.then(dve.tensor_copy(r, a3[:, :, :, DH3]))
                c.then(dve.tensor_scalar(small[:, 6, 0:GROUP * HEADS3], small[:, 6, 0:GROUP * HEADS3], 1e-8, None, ALU.add))
                c.then(dve.reciprocal(small[:, 6, 0:GROUP * HEADS3], small[:, 6, 0:GROUP * HEADS3]))
                c4 = cen.rearrange("p j (h f) -> p j h f", f=DH3)
                c.then(dve.tensor_tensor(c4, a3[:, :, :, 0:DH3],
                                         r.rearrange("p j (h a) -> p j h a", a=1).to_broadcast([P, GROUP, HEADS3, DH3]), ALU.mult))
                c.then(dve.tensor_tensor(grp(X, g), grp(X, g), cen, ALU.add))
                dve.sem_inc(out_ready, 1)
            c.close()


def kernel(**inputs):
    import numpy as np
    import concourse.bacc as bacc
    from concourse.bass_utils import run_bass_kernel_spmd

    def a(name):
        return np.asarray(inputs[name])

    arrays = {
        "x": a("x"), "src": a("src"), "dst": a("dst"), "edge_attr": a("edge_attr_16"), "edge_weight": a("edge_weight"),
        "q": a("L0_gnn_w_q"), "k": a("L0_gnn_w_k"), "v": a("L0_gnn_w_v"), "o": a("L0_gnn_w_o"),
        "rel": a("L1_gnn_W_rel").T, "root": a("L1_gnn_W_root").T,
        "self0": a("L2_gnn_W_self")[0].T, "self1": a("L2_gnn_W_self")[1].T,
        "neigh0": a("L2_gnn_W_neigh")[0].T, "neigh1": a("L2_gnn_W_neigh")[1].T, "agg": a("L2_gnn_W_agg").T,
        "b_o": a("L0_gnn_b_o"), "b_rel": a("L1_gnn_b_rel"),
        "b_self0": a("L2_gnn_b_self")[0], "b_self1": a("L2_gnn_b_self")[1],
        "b_neigh0": a("L2_gnn_b_neigh")[0], "b_neigh1": a("L2_gnn_b_neigh")[1],
        "b_layer0": a("L2_gnn_layer_bias")[0], "b_layer1": a("L2_gnn_layer_bias")[1], "b_agg": a("L2_gnn_b_agg"),
        "heads": a("L3_gnn_W").transpose(1, 0, 2).reshape(D, HEADS3 * DH3),
        "left": a("L3_gnn_a_l").reshape(-1), "right": a("L3_gnn_a_r").reshape(-1), "b_out": a("L3_gnn_bias"),
    }
    nc = bacc.Bacc("TRN2", target_bir_lowering=False, num_devices=1)
    arrays = {k: np.ascontiguousarray(v) for k, v in arrays.items()}
    aps = {k: nc.dram_tensor(f"in_{k}", v.shape, mybir.dt.from_np(v.dtype), kind="ExternalInput").ap()
           for k, v in arrays.items()}
    out = nc.dram_tensor("out", (N, D), F32, kind="ExternalOutput").ap()
    build(nc, aps["x"], aps["src"], aps["dst"], aps["edge_attr"], aps["edge_weight"], aps, out)
    r = run_bass_kernel_spmd(nc, [{f"in_{k}": v for k, v in arrays.items()}], core_ids=[0])
    return r.results[0]["out"]
```

```python
from contextlib import ExitStack

import concourse.bass as bass
from concourse import mybir

P = 128
N = 6250
E = 200000
D = 128
EDGE_ATTRS = 16
TILES = -(-E // P)
BLOCKS = -(-N // P)
GROUP = 7
GROUPS = BLOCKS // GROUP
RING = 16
HALF = RING // 2
STEPS = -(-(TILES + BLOCKS - 1) // RING) * RING
ITERS = STEPS // RING
CHUNKS = -(-(STEPS + RING) // P)
COLS = CHUNKS * P
AGG_W = 132
HEADS0, DH0 = 8, 16
HEADS3, DH3 = 4, 32
SCALE0 = DH0 ** -0.5
EPS = 1e-5
SLOPE = 0.2
ROW3 = HEADS3 * (DH3 + 2)
SPAN_ITERS = -(-E // (P * RING))
BIG = 1e38
CHUNK_ITERS = (30, 28, 24, SPAN_ITERS - 82)
NC = len(CHUNK_ITERS)
AT_STARTS, AT_QUADS = 40, 60
SPLIT = 6
SPAN = [RING * i for i in CHUNK_ITERS]
ITER0 = [sum(CHUNK_ITERS[:c]) for c in range(NC + 1)]
RUN0 = [RING * i for i in ITER0]
EDGE0 = [P * RING * i for i in ITER0]
E_PAD = EDGE0[NC]
QUAD = 4 * P
QUADS = [P * n // QUAD for n in SPAN]
QRING = 6
QITERS = [-(-(n + BLOCKS - 1) // QRING) for n in QUADS]
QSTEP0 = [QRING * sum(QITERS[:c]) for c in range(NC + 1)]
QCOLS = 2 * P
assert max(QITERS) * QRING <= QCOLS and all(n % 4 == 0 for n in SPAN)
REC = HEADS3 + 1
PAD_DST = 20000.0
assert GROUPS * GROUP == BLOCKS and TILES <= COLS

ALU = mybir.AluOpType
ACT = mybir.ActivationFunctionType
AX = mybir.AxisListType.X
F32 = mybir.dt.float32
I32 = mybir.dt.int32
DVE_ONLY = (mybir.EngineType.DVE,)
SP_ONLY = (mybir.EngineType.SP,)

(KV, QUERY, OUT0, ROOT, REL, SELF2A, NEIGH2A, SELF2B, NEIGH2B, AGG2, HEADS) = range(11)
PASSES = 11


def build(nc, x, src, dst, edge_attr, edge_weight, w, out, debug=None):
    ctx = ExitStack()
    with ctx:
        def sb(name, shape, dt=F32):
            return ctx.enter_context(nc.sbuf_tensor(name, shape, dt))

        def sem(name):
            return ctx.enter_context(nc.semaphore(name))

        def dram(name, shape, dt=F32):
            return nc.dram_tensor(name, shape, dt, kind="Internal").ap()

        tile_rows = dram("tile_rows", [COLS, 4 * P])
        step_block_d = dram("step_block_d", [1, COLS], I32)
        tables = [dram(f"table{i}", [BLOCKS * P, D]) for i in range(4)]
        head_table = dram("head_table", [BLOCKS * P, ROW3])
        right_table = dram("right_table", [BLOCKS * P, HEADS3])
        right_edges = dram("right_edges", [E_PAD, HEADS3])
        edge_rows = dram("edge_rows", [E_PAD, ROW3])
        edge_records = dram("edge_records", [E_PAD, REC])
        quad_d = [dram(f"quad_{n}_d", [1, NC * QCOLS], I32) for n in ("block", "tile")]

        X = sb("X", [P, BLOCKS, D])
        H = sb("H", [P, BLOCKS, D])
        scratch = sb("scratch", [P, BLOCKS * D + BLOCKS * AGG_W])
        R = scratch[:, 0:BLOCKS * D].rearrange("p (b f) -> p b f", f=D)
        AGG = scratch[:, BLOCKS * D:].rearrange("p (b f) -> p b f", f=AGG_W)
        step_table = sb("step_table", [P, 4, COLS])
        S_SRC, S_PLACE, S_W, S_W0 = range(4)
        step_block = sb("step_block", [1, COLS], I32)
        idx_stage = sb("idx_stage", [P, RING], I32)
        rows = sb("rows", [P, RING, ROW3])
        scaled = sb("scaled", [P, HALF, AGG_W])
        onehot = sb("onehot", [P, HALF, P])
        work = sb("work", [P, 4, GROUP * D])
        stage, turned, cen, sq = (work[:, i, :].rearrange("p (j f) -> p j f", f=D) for i in range(4))
        small = sb("small", [P, 8, GROUP * HEADS0])
        stats = sb("stats", [P, GROUP, 6])
        moments = sb("moments", [P, GROUP, 2])
        iota = sb("iota", [P, P])
        pidx = sb("pidx", [P, 1])
        ident = sb("ident", [P, P])
        ones = sb("ones", [P, P])
        epst = sb("epst", [P, 1])
        cnt = sb("cnt", [P, BLOCKS])
        inv_mean0 = sb("inv_mean0", [P, BLOCKS])
        inv_mean2 = sb("inv_mean2", [P, BLOCKS])
        W = {k: sb(f"w_{k}", [P, D]) for k in
             ("q", "k", "v", "o", "rel", "root", "self0", "self1", "neigh0", "neigh1", "agg", "heads", "left", "right")}
        bias = {k: sb(f"b_{k}", [P, D]) for k in
                ("o", "rel", "self0", "neigh0", "layer0", "self1", "neigh1", "layer1", "agg", "out")}
        bsum = sb("bsum", [P, 2, D])
        chunk_i = work[:, :, :].rearrange("p i f -> p (i f)")[:, 0:2 * COLS].bitcast(I32).rearrange("p (k e) -> p k e", k=2)
        block_edge = sb("block_edge", [P, BLOCKS - 1])
        block_no = sb("block_no", [P, BLOCKS - 1])
        step_no = sb("step_no", [P, CHUNKS])
        cmp = sb("cmp", [P, (BLOCKS - 1) * CHUNKS])
        first_tile = sb("first_tile", [P, BLOCKS - 1])
        step_b = sb("step_b", [P, CHUNKS])
        step_t = sb("step_t", [P, CHUNKS])
        step_off = sb("step_off", [P, CHUNKS])
        step_b_i = sb("step_b_i", [P, CHUNKS], I32)
        step_t_i = sb("step_t_i", [P, CHUNKS], I32)
        tri = sb("tri", [P, P])
        before = sb("before", [P, 3, BLOCKS])
        first_edge = sb("first_edge", [P, BLOCKS], I32)
        w_lr = sb("w_lr", [P, 2 * HEADS3])
        right = sb("right", [P, BLOCKS, HEADS3])
        right0 = sb("right0", [P, NC, HEADS3])
        zeros = sb("zeros", [P, E_PAD // P * HEADS3 // 16])
        dst0 = sb("dst0", [P, NC], I32)
        carry = sb("carry", [P, 6, HEADS3])
        carry_in = sb("carry_in", [P, 2, HEADS3])
        shift = sb("shift", [P, HEADS3])
        factor = sb("factor", [P, HEADS3])
        chain = sb("chain", [HEADS3, 6, P])
        chain_out = sb("chain_out", [HEADS3, 4, P])
        chain_end = sb("chain_end", [HEADS3, 1])
        block_start = sb("block_start", [P, BLOCKS - 1])
        quad_last_i = sb("quad_last_i", [P, NC], I32)
        quad_last = sb("quad_last", [P, NC])
        quad_count = sb("quad_count", [P, NC])
        quad_base = sb("quad_base", [P, NC])
        quad_b = sb("quad_b", [P, 2, NC])
        quad_t = sb("quad_t", [P, 2, NC])
        quad_over = sb("quad_over", [P, 2, NC])
        quad_i = sb("quad_i", [P, 2, 2, NC], I32)
        quad_row = sb("quad_row", [1, 2, NC * QCOLS], I32)
        quad_off = sb("quad_off", [P, NC, QCOLS])
        seam_i = sb("seam_i", [P, NC - 1], I32)
        seam = sb("seam", [P, 3, NC - 1])
        seam_b = sb("seam_b", [P, NC - 1], I32)
        seam_place = sb("seam_place", [P, NC - 1, P])
        quad_rec = sb("quad_rec", [P, QRING, 4 * REC])
        quad_place = sb("quad_place", [P, 2, 4])

        HT = scratch[:, 0:BLOCKS * ROW3].rearrange("p (b h f) -> p b h f", h=HEADS3, f=DH3 + 2)
        Hflat = H[:, :, :].rearrange("p b f -> p (b f)")
        SM = max(SPAN)

        def carve(base):
            at = [0]

            def piece(n):
                at[0] += n
                assert at[0] <= base.shape[-1], (at[0], base.shape)
                return base[:, at[0] - n:at[0]]
            return piece
        piece = carve(Hflat)
        record = [piece(SM * REC) for _ in range(2)]
        same_b, keep_b = piece(SM + 1), piece(SM + 1)
        piece = carve(scratch[:, 0:BLOCKS * D])
        quad_rows = piece(QRING * 4 * ROW3).rearrange("p (s q f) -> p s q f", s=QRING, q=4)
        quad_onehot = piece(3 * 4 * P).rearrange("p (s q d) -> p s q d", s=3, q=4)
        fwd_b, bwd_b, dst_b = piece(SM), piece(SM), piece(SM + 2)
        piece = carve(step_table[:, :, :].rearrange("p k c -> p (k c)"))
        run_src = piece(E_PAD // P + RING).bitcast(I32)
        run_dst = piece(E_PAD // P + 2 * NC).bitcast(I32)
        logw = piece(E_PAD // P)
        right_b = piece(SM * HEADS3)

        ps = [ctx.enter_context(nc.psum_tensor(f"ps{i}", [P, 1024], F32)) for i in range(4)]

        loaded_x = sem("loaded_x")
        loaded_edges = sem("loaded_edges")
        loaded_attr = [sem(f"loaded_attr{i}") for i in range(5)]
        loaded_w = sem("loaded_w")
        consts = sem("consts")
        cleared = sem("cleared")
        attr_used = sem("attr_used")
        logits_ready = sem("logits_ready")
        sigmoid_ready = sem("sigmoid_ready")
        tile_rows_ready = sem("tile_rows_ready")
        tile_rows_stored = sem("tile_rows_stored")
        counted = sem("counted")
        summed = sem("summed")
        step_index_ready = sem("step_index_ready")
        step_rows_landed = [sem(f"step_rows_landed{i}") for i in range(2)]
        step_rows_ready = sem("step_rows_ready")
        step_turned = sem("step_turned")
        step_table_ready = sem("step_table_ready")
        blocks_stored = sem("blocks_stored")
        blocks_loaded = sem("blocks_loaded")
        ve = sem("ve")
        norm_stats = sem("norm_stats")
        norm_sum = sem("norm_sum")
        norm_root = sem("norm_root")
        norm_scaled = sem("norm_scaled")
        normed = sem("normed")
        table_ready = sem("table_ready")
        table_stored = sem("table_stored")
        lin_staged = sem("lin_staged")
        lin_transposed = sem("lin_transposed")
        lin_turned = sem("lin_turned")
        lin_product = sem("lin_product")
        lin_used = sem("lin_used")
        idx_staged = sem("idx_staged")
        row_landed = [sem(f"row_landed{j}") for j in range(RING)]
        row_scaled = sem("row_scaled")
        onehot_ready = sem("onehot_ready")
        partial_ready = sem("partial_ready")
        block_added = sem("block_added")
        agg_cleared = sem("agg_cleared")
        agg_done = sem("agg_done")
        out_stored = sem("out_stored")
        out_ready = sem("out_ready")
        zeroed = sem("zeroed")
        right_cleared = sem("right_cleared")
        cnt_ready = sem("cnt_ready")
        starts_summed = sem("starts_summed")
        starts_ready = sem("starts_ready")
        heads_ready = sem("heads_ready")
        heads_stored = sem("heads_stored")
        right_stored = sem("right_stored")
        runs_padded = sem("runs_padded")
        runs_loaded = sem("runs_loaded")
        rows_stored = [sem(f"rows_stored{i}") for i in range(2)]
        score_taken = sem("score_taken")
        round_open = sem("round_open")
        right_scattered = sem("right_scattered")
        right0_loaded = sem("right0_loaded")
        right_loaded = sem("right_loaded")
        dst0_ready = sem("dst0_ready")
        logw_ready = sem("logw_ready")
        carries_ready = sem("carries_ready")
        carries_turned = sem("carries_turned")
        chains_ready = sem("chains_ready")
        chains_turned = sem("chains_turned")
        exponents_ready = sem("exponents_ready")
        alphas_ready = sem("alphas_ready")
        alphas_stored = sem("alphas_stored")
        right_used = sem("right_used")
        quads_padded = sem("quads_padded")
        quads_loaded = sem("quads_loaded")
        quads_counted = sem("quads_counted")
        quads_summed = sem("quads_summed")
        quads_ready = sem("quads_ready")
        offsets_ready = sem("offsets_ready")
        offsets_spread = sem("offsets_spread")
        quad_rows_stored = sem("quad_rows_stored")
        quad_row_loaded = sem("quad_row_loaded")
        shift_ready = sem("shift_ready")
        shift_placed = sem("shift_placed")
        factor_ready = sem("factor_ready")
        quad_landed = [sem(f"quad_landed{j}") for j in range(QRING)]
        quad_ready = sem("quad_ready")
        quad_partial = sem("quad_partial")
        quad_added = sem("quad_added")
        quad_placed = sem("quad_placed")
        quad_scaled = sem("quad_scaled")

        SCALED0, PARTIAL0, ADDED0 = RING, HALF, 2

        full_tiles = E // P
        fullc = full_tiles // P
        rest = full_tiles - fullc * P
        tail = E - full_tiles * P

        def tiled(a, width):
            yield slice(0, P), slice(0, fullc), a[0:fullc * P * P * width].rearrange("(c p e) -> p c e", p=P, e=P * width)
            yield slice(0, rest), fullc, a[fullc * P * P * width:full_tiles * P * width].rearrange("(p e) -> p e", e=P * width)
            yield slice(rest, rest + 1), fullc, a[full_tiles * P * width:].rearrange("(p e) -> p e", p=1)

        TR = step_table[:, :, :].rearrange("p k c -> p (k c)").rearrange("p (c k e) -> p c k e", k=4, e=P)
        WLOADS = len(W) + len(bias)
        attr = edge_attr.rearrange("e a -> (e a)")
        EAW = P * EDGE_ATTRS
        LOGITS = H[:, 0:CHUNKS, :]
        ATTR = [(slice(3 * i, 3 * i + 3), (i % 2) * 3 * EAW) for i in range(4)] + [(slice(12, 13), 0)]
        GATHER_STEPS = scratch[:, 0:CHUNKS * 4 * P].rearrange("p (c k e) -> p c k e", k=4, e=P)

        diag = work[:, 2:4, :].rearrange("p i f -> p (i f)")[:, 0:2 * NC * P].rearrange("p (i m) -> p i m", m=P)

        def step_sum(j, width):
            at = j % 2 * 512
            return ps[3][:, at:at + width]

        def grp_of(t, g):
            return t[:, bass.ds(g * GROUP, GROUP), :]

        def every(a, first, step, n):
            return bass.AP(tensor=a.tensor, offset=first, ap=[[step, n], [1, 1]])

        RUN_LOADS = sum(5 + 3 * (E < EDGE0[c + 1]) for c in range(NC))

        block = ctx.enter_context(nc.Block())

        @block.sync
        def _(sp):
            sp.wait_ge(cleared, 2)
            for k, a in ((0, src), (1, dst)):
                for pp, cc, s in tiled(a, 1):
                    n = s.shape[-1]
                    t = chunk_i[pp, k, :].rearrange("p (c e) -> p c e", e=P)
                    sp.dma_start(t[:, cc, 0:n], s).then_inc(loaded_edges, 16)
            for pp, cc, s in tiled(edge_weight, 1):
                sp.dma_start(TR[pp, cc, 2, 0:s.shape[-1]], s).then_inc(loaded_edges, 16)
            sp.dma_start(X[:, 0:BLOCKS - 1, :], x[0:(BLOCKS - 1) * P, :].rearrange("(b p) f -> p b f", p=P))\
                .then_inc(loaded_x, 16)
            last = N - (BLOCKS - 1) * P
            sp.dma_start(X[0:last, BLOCKS - 1, :], x[(BLOCKS - 1) * P:, :]).then_inc(loaded_x, 16)
            for i, (cc, at) in enumerate(ATTR):
                if i >= 2:
                    sp.wait_ge(attr_used, i - 1)
                dst_ = scratch[:, at:at + 3 * EAW].rearrange("p (c e) -> p c e", c=3)
                if i < 4:
                    s = attr[cc.start * P * EAW:cc.stop * P * EAW].rearrange("(c p e) -> p c e", p=P, e=EAW)
                    sp.dma_start(dst_, s).then_inc(loaded_attr[i], 16)
                else:
                    s = attr[fullc * P * EAW:full_tiles * EAW].rearrange("(p e) -> p e", e=EAW)
                    sp.dma_start(dst_[0:rest, 0, :], s).then_inc(loaded_attr[i], 16)
                    s = attr[full_tiles * EAW:].rearrange("(p e) -> p e", p=1)
                    sp.dma_start(dst_[rest:rest + 1, 0, 0:tail * EDGE_ATTRS], s).then_inc(loaded_attr[i], 16)
            for k in ("q", "k", "v", "o", "rel", "root", "self0", "self1", "neigh0", "neigh1", "agg", "heads"):
                sp.dma_start(W[k][:, :], w[k]).then_inc(loaded_w, 16)
            for k, t in (("left", W["left"]), ("right", W["right"])):
                sp.dma_start(t[:, :], w[k].rearrange("(a f) -> a f", a=1).to_broadcast([P, D])).then_inc(loaded_w, 16)
            for k in ("o", "rel", "self0", "neigh0", "layer0", "self1", "neigh1", "layer1", "agg", "out"):
                sp.dma_start(bias[k][:, :], w["b_" + k].rearrange("(a f) -> a f", a=1).to_broadcast([P, D]))\
                    .then_inc(loaded_w, 16)
            sp.wait_ge(zeroed, 1)
            sp.dma_start(right_edges.rearrange("(p r t) h -> p r (t h)", p=P, r=16),
                         zeros[:, :].rearrange("p (a t) -> p a t", a=1).to_broadcast([P, 16, zeros.shape[-1]]))\
                .then_inc(right_cleared, 16)
            sp.wait_ge(tile_rows_ready, 2)
            sp.wait_ge(loaded_edges, 16 * 9)
            sp.dma_start(tile_rows.rearrange("(c p) e -> p c e", p=P), TR.rearrange("p c k e -> p c (k e)"))\
                .then_inc(tile_rows_stored, 16)
            sp.wait_ge(step_index_ready, 1)
            sp.dma_start(step_block_d.rearrange("a (c p) -> p (a c)", p=P), step_b_i[:, :],
                         allow_slow_non_contiguous=True).then_inc(blocks_stored, 16)
            sp.wait_ge(blocks_stored, 16)
            sp.dma_start(step_block[:, :], step_block_d).then_inc(blocks_loaded, 16)

            sp.wait_ge(quads_padded, 1)
            for c in range(NC):
                n = min(QUADS[c], (E - EDGE0[c]) // QUAD)
                sp.dma_start(quad_last_i[0:n, c:c + 1], every(dst, EDGE0[c] + QUAD - 1, QUAD, n),
                             allow_slow_non_contiguous=True).then_inc(quads_loaded, 16)
            for c in range(1, NC):
                sp.dma_start(seam_i[:, c - 1:c], every(dst, EDGE0[c] - 1, 0, P), allow_slow_non_contiguous=True)\
                    .then_inc(quads_loaded, 16)

            for layer in range(4):
                if layer == 2:
                    sp.wait_ge(quads_ready, 1)
                    for i in range(2):
                        for c in range(NC):
                            sp.dma_start(quad_d[i][:, c * QCOLS:(c + 1) * QCOLS].rearrange("a (k p) -> p (a k)", p=P),
                                         quad_i[:, i, :, c], allow_slow_non_contiguous=True).then_inc(quad_rows_stored, 16)
                    sp.wait_ge(quad_rows_stored, 16 * 2 * NC)
                    for i in range(2):
                        sp.dma_start(quad_row[:, i, :], quad_d[i]).then_inc(quad_row_loaded, 16)
                rows_d = tables[layer].rearrange("(g j p) f -> g p j f", p=P, j=GROUP)
                with sp.Fori(0, GROUPS) as g:
                    if layer < 3:
                        sp.wait_ge(normed, g + (GROUPS * layer + 2))
                    else:
                        sp.wait_ge(table_ready, g + 1)
                    sp.dma_start(rows_d[bass.ds(g, 1), :, :, :].rearrange("a p j f -> (a p) j f"),
                                 H[:, bass.ds(g * GROUP, GROUP), :]).then_inc(table_stored, 16)
            sp.wait_ge(runs_padded, 1)
            for c in range(NC):
                full = min(P, (E - EDGE0[c]) // SPAN[c])
                more = min(E, EDGE0[c + 1]) - EDGE0[c] - full * SPAN[c]
                for a_, t_, o_ in ((src, run_src, RUN0[c]), (dst, run_dst, RUN0[c] + 2 * c + 1), (edge_weight, logw, RUN0[c])):
                    a_ = a_[EDGE0[c]:min(E, EDGE0[c + 1])]
                    sp.dma_start(t_[0:full, o_:o_ + SPAN[c]], a_[0:full * SPAN[c]].rearrange("(p t) -> p t", p=full)).then_inc(runs_loaded, 16)
                    if more:
                        sp.dma_start(t_[full:full + 1, o_:o_ + more], a_[full * SPAN[c]:].rearrange("(p t) -> p t", p=1)).then_inc(runs_loaded, 16)
                o_ = RUN0[c] + 2 * c
                p0 = 1 if c == 0 else 0
                n = min(P, -(-(E - EDGE0[c]) // SPAN[c])) - p0
                sp.dma_start(run_dst[p0:p0 + n, o_:o_ + 1], every(dst, EDGE0[c] + p0 * SPAN[c] - 1, SPAN[c], n),
                             allow_slow_non_contiguous=True).then_inc(runs_loaded, 16)
                n = min(P, (E - 1 - EDGE0[c]) // SPAN[c])
                sp.dma_start(run_dst[0:n, o_ + SPAN[c] + 1:o_ + SPAN[c] + 2], every(dst, EDGE0[c] + SPAN[c], SPAN[c], n),
                             allow_slow_non_contiguous=True).then_inc(runs_loaded, 16)
            heads_d = head_table.rearrange("(g j p) f -> g p j f", p=P, j=GROUP)
            with sp.Fori(0, GROUPS) as g:
                sp.wait_ge(heads_ready, g + 1)
                sp.dma_start(heads_d[bass.ds(g, 1), :, :, :].rearrange("a p j f -> (a p) j f"),
                             HT[:, bass.ds(g * GROUP, GROUP), :, :].rearrange("p j h f -> p j (h f)")).then_inc(heads_stored, 16)
            sp.wait_ge(heads_ready, GROUPS)
            sp.dma_start(right_table.rearrange("(b p) h -> p b h", p=P), right[:, :, :]).then_inc(right_stored, 16)
            sp.wait_ge(right_scattered, 16 * BLOCKS)
            sp.wait_ge(quad_row_loaded, 32)

            def load_right(c):
                sp.dma_start(right_b[:, 0:SPAN[c] * HEADS3],
                             right_edges[EDGE0[c]:EDGE0[c + 1], :].rearrange("(p t) h -> p (t h)", p=P)).then_inc(right_loaded, 16)

            load_right(0)
            for c in range(NC):
                sp.wait_ge(alphas_ready, c + 1)
                sp.dma_start(edge_records[EDGE0[c]:EDGE0[c + 1], :].rearrange("(p t) f -> p (t f)", p=P),
                             record[c % 2][:, 0:SPAN[c] * REC]).then_inc(alphas_stored, 16)
                if c < NC - 1:
                    sp.wait_ge(right_used, c + 1)
                    load_right(c + 1)
                sp.wait_ge(alphas_stored, 16 * (c + 1))
                for half in range(2):
                    sp.wait_ge(rows_stored[half], 16 * ITER0[c + 1])
                quad_rows_d = edge_rows.rearrange("(t p q) f -> t p (q f)", p=P, q=4)
                quad_rec_d = edge_records.rearrange("(t p q) f -> t p (q f)", p=P, q=4)
                with sp.Fori(0, QITERS[c]) as k:
                    _, at = nc.values_load_multi_w_load_instructions(
                        quad_row[0:1, 1, bass.ds(k * QRING + QCOLS * c, QRING)], engines=SP_ONLY, min_val=0,
                        max_val=E_PAD // QUAD - 1, skip_runtime_bounds_check_because="a quad step's quad is below by construction")
                    for j in range(QRING):
                        sp.wait_ge(quad_partial, k * QRING + (QSTEP0[c] + j + 1))
                        sp.dma_start(quad_rows[:, j, :, :].rearrange("p q f -> p (q f)"),
                                     quad_rows_d[bass.ds(at[j], 1), :, :].rearrange("a p f -> (a p) f")).then_inc(quad_landed[j], 16)
                        sp.dma_start(quad_rec[:, j, :], quad_rec_d[bass.ds(at[j], 1), :, :].rearrange("a p f -> (a p) f"))\
                            .then_inc(quad_landed[j], 16)
            with sp.Fori(0, GROUPS - 1) as g:
                sp.wait_ge(out_ready, g + 1)
                sp.dma_start(out[0:(BLOCKS - GROUP) * P, :].rearrange("(g j p) f -> g p j f", p=P, j=GROUP)[bass.ds(g, 1), :, :, :]
                             .rearrange("a p j f -> (a p) j f"), grp_of(X, g)).then_inc(out_stored, 16)
            sp.wait_ge(out_ready, GROUPS)
            sp.dma_start(out[(BLOCKS - GROUP) * P:(BLOCKS - 1) * P, :].rearrange("(b p) f -> p b f", p=P),
                         X[:, BLOCKS - GROUP:BLOCKS - 1, :]).then_inc(out_stored, 16)
            sp.dma_start(out[(BLOCKS - 1) * P:, :], X[0:last, BLOCKS - 1, :]).then_inc(out_stored, 16)
            sp.wait_ge(out_stored, 16 * (GROUPS + 1))

        @block.gpsimd
        def _(pool):
            pool.memset(chunk_i[:, 0, :], 0).then_inc(consts, 1)
            pool.iota(iota[:, :], [[1, P]], base=0, channel_multiplier=0,
                      allow_small_or_imprecise_dtypes=True).then_inc(consts, 1)
            pool.iota(pidx[:, :], [[1, 1]], base=0, channel_multiplier=1,
                      allow_small_or_imprecise_dtypes=True).then_inc(consts, 1)
            pool.iota(block_edge[:, :], [[P, BLOCKS - 1]], base=P, channel_multiplier=0,
                      allow_small_or_imprecise_dtypes=True).then_inc(consts, 1)
            pool.iota(block_start[:, :], [[P, BLOCKS - 1]], base=P, channel_multiplier=0,
                      allow_small_or_imprecise_dtypes=True).then_inc(consts, 1)
            pool.iota(block_no[:, :], [[1, BLOCKS - 1]], base=1, channel_multiplier=0,
                      allow_small_or_imprecise_dtypes=True).then_inc(consts, 1)
            pool.iota(step_no[:, :], [[P, CHUNKS]], base=0, channel_multiplier=1,
                      allow_small_or_imprecise_dtypes=True).then_inc(consts, 1)
            pool.memset(ones[:, :], 1.0).then_inc(consts, 1)
            pool.memset(epst[:, :], EPS).then_inc(consts, 1)
            pool.memset(zeros[:, :], 0.0).then_inc(zeroed, 1)
            pool.memset(scaled[:, :, D:AGG_W], 1.0).then_inc(consts, 1)
            pool.wait_ge(tile_rows_stored, 16)
            pool.wait_ge(step_index_ready, 1)
            pool.wait_ge(attr_used, 5)
            for c in range(CHUNKS):
                pool.indirect_dma_start(out=GATHER_STEPS[:, c, :, :].rearrange("p k e -> p (k e)"), out_offset=None,
                                        in_=tile_rows, in_offset=bass.IndirectOffsetOnAxis(ap=step_t_i[:, c:c + 1], axis=0))\
                    .then_inc(step_rows_landed[c >= 6], 16)

            def gathers(layer, table):
                pool.wait_ge(table_stored, 16 * GROUPS * (layer + 1))
                with pool.Fori(0, ITERS) as k:
                    for j in range(RING):
                        if j % HALF == 0:
                            pool.wait_ge(idx_staged, k * 2 + (2 * (ITERS + 1) * layer + j // HALF + 1))
                            pool.wait_ge(row_scaled, k * RING + (STEPS * layer + j + HALF))
                            pool.sem_inc(round_open, 1)
                        pool.indirect_dma_start(out=rows[:, j, 0:D], out_offset=None, in_=table,
                                                in_offset=bass.IndirectOffsetOnAxis(ap=idx_stage[:, j:j + 1], axis=0))\
                            .then_inc(row_landed[j], 16)

            for layer in range(4):
                gathers(layer, tables[layer])

            pool.wait_ge(right_cleared, 16)
            pool.wait_ge(starts_ready, 1)
            for b in range(BLOCKS):
                if b % GROUP == 0:
                    pool.wait_ge(heads_ready, b // GROUP + 1)
                pool.indirect_dma_start(out=right_edges, out_offset=bass.IndirectOffsetOnAxis(ap=first_edge[:, b:b + 1], axis=0),
                                        in_=right[:, b, :], in_offset=None, bounds_check=E_PAD - 1, oob_is_err=False)\
                    .then_inc(right_scattered, 16)
            pool.wait_ge(dst0_ready, 1)
            pool.wait_ge(right_stored, 16)
            for c in range(NC):
                pool.indirect_dma_start(out=right0[:, c, :], out_offset=None, in_=right_table,
                                        in_offset=bass.IndirectOffsetOnAxis(ap=dst0[:, c:c + 1], axis=0),
                                        bounds_check=BLOCKS * P - 1, oob_is_err=False).then_inc(right0_loaded, 16)
            pool.wait_ge(heads_stored, 16 * GROUPS)

            def run_gathers(k):
                for j in range(RING):
                    if j % HALF == 0:
                        half = j // HALF
                        pool.wait_ge(idx_staged, k * 2 + (2 * (ITERS + 1) * 4 + half + 1))
                        if not isinstance(k, int):
                            pool.wait_ge(rows_stored[half], k * 16)
                            pool.wait_ge(score_taken, k * 2 + (half - 1))
                        pool.sem_inc(round_open, 1)
                    pool.indirect_dma_start(out=rows[:, j, :], out_offset=None, in_=head_table,
                                            in_offset=bass.IndirectOffsetOnAxis(ap=idx_stage[:, j:j + 1], axis=0))\
                        .then_inc(row_landed[j], 16)

            run_gathers(0)
            with pool.Fori(1, SPAN_ITERS) as k:
                run_gathers(k)

        @block.scalar
        def _(act):
            act.sem_inc(row_scaled, SCALED0)
            for s in (lin_staged, lin_turned, normed):
                act.sem_inc(s, 1)

            def norm(g, n):
                act.wait_ge(norm_sum, g + (GROUPS * n + 1))
                act.activation(small[:, 3, 0:GROUP], moments[:, :, 1], ACT.Sqrt, bias=epst[:, 0:1]).then_inc(norm_root, 1)
                act.wait_ge(norm_scaled, g + (GROUPS * n + 1))
                for j in range(GROUP):
                    b = bass.ds(g * GROUP + j, 1)
                    ins = act.activation(H[:, b, :].rearrange("p a f -> p (a f)"), X[:, b, :].rearrange("p a f -> p (a f)"),
                                         ACT.Relu, bias=small[:, 5, j:j + 1], scale=small[:, 4, j:j + 1])
                ins.then_inc(normed, 1)

            def turn_group(g, p, source, ready, base):
                act.wait_ge(ready, g + (base + 1))
                act.wait_ge(lin_transposed, g + (GROUPS * p + 1))
                at = g * GROUP
                src_ = source[:, at:at + GROUP, 0:D] if isinstance(g, int) else source[:, bass.ds(at, GROUP), 0:D]
                act.copy(stage, src_).then_inc(lin_staged, 1)
                act.wait_ge(lin_transposed, g + (GROUPS * p + 2))
                act.wait_ge(lin_product, g + (GROUPS * p + 1))
                act.copy(turned.rearrange("p j f -> p (j f)"), ps[0][:, 0:GROUP * D]).then_inc(lin_turned, 1)

            def turn(p, source, ready, base, n=None):
                if n is None:
                    with act.Fori(0, GROUPS) as g:
                        turn_group(g, p, source, ready, base)
                    return
                turn_group(0, p, source, ready, base)
                with act.Fori(0, GROUPS - 1) as g:
                    turn_group(g + 1, p, source, ready, base)
                    norm(g, n)
                with act.Fori(GROUPS - 1, GROUPS) as g:
                    norm(g, n)

            def turn_agg(p, layers, n=None):
                act.wait_ge(agg_done, layers)
                turn(p, AGG, lin_used, GROUPS * p, n)

            def stage_indices(layer, k, half):
                act.copy(idx_stage[:, half * HALF:(half + 1) * HALF],
                         step_table[:, S_SRC, bass.ds(k * RING + half * HALF, HALF)] if not isinstance(k, int)
                         else step_table[:, S_SRC, k * RING + half * HALF:k * RING + (half + 1) * HALF])\
                    .then_inc(idx_staged, 1)

            def first_indices(layer):
                if layer:
                    act.wait_ge(idx_staged, 2 * (ITERS + 1) * layer)
                for half in range(2):
                    stage_indices(layer, 0, half)

            def scale(layer, weights, p, ready, base):
                def body(k):
                    for j in range(RING):
                        act.wait_ge(row_landed[j], k * 16 + (16 * (ITERS * layer + 1)))
                        act.wait_ge(partial_ready, k * RING + (STEPS * layer + j + 1))
                        by = 1.0 if weights is None else step_table[:, weights, bass.ds(k * RING + j, 1)]
                        act.activation(scaled[:, j % HALF, 0:D], rows[:, j, 0:D], ACT.Copy, scale=by)\
                            .then_inc(row_scaled, 1)
                        if j % HALF == HALF - 1:
                            stage_indices(layer, k + 1, j // HALF)

                with act.Fori(0, GROUPS) as k:
                    body(k)
                    turn_group(k, p, H, ready, base)
                with act.Fori(GROUPS, ITERS) as k:
                    body(k)

            act.wait_ge(logits_ready, 5)
            act.activation(TR[:, :, 3, :], LOGITS, ACT.Sigmoid).then_inc(sigmoid_ready, 1)
            act.wait_ge(sigmoid_ready, 1)
            act.sem_inc(tile_rows_ready, 1)
            with act.Fori(0, GROUPS) as g:
                norm(g, 0)
            act.wait_ge(tile_rows_stored, 16)
            for c in range(CHUNKS):
                act.wait_ge(step_turned, c + 1)
                act.copy(step_table[:, :, c * P:(c + 1) * P],
                         ps[c % 2][:, 0:4 * P].rearrange("p (k s) -> p k s", k=4)).then_inc(step_table_ready, 1)
            first_indices(0)
            scale(0, S_W0, KV, normed, 1)
            first_indices(1)
            turn_agg(QUERY, 1)
            turn(OUT0, H, lin_used, GROUPS * QUERY + 1, n=1)
            scale(1, None, ROOT, normed, GROUPS + 1)
            first_indices(2)
            turn_agg(REL, 2, n=2)
            scale(2, S_W, SELF2A, normed, 2 * GROUPS + 1)
            first_indices(3)
            turn_agg(NEIGH2A, 3)
            scale(3, S_W, SELF2B, lin_used, GROUPS * NEIGH2A + 1)
            turn_agg(NEIGH2B, 4)
            turn(AGG2, H, lin_used, GROUPS * NEIGH2B + 1, n=3)
            turn(HEADS, H, normed, 3 * GROUPS + 1)
            act.wait_ge(runs_loaded, 16 * RUN_LOADS)
            act.wait_ge(logw_ready, 1)
            act.activation(logw, logw, ACT.Ln).then_inc(logw_ready, 1)
            act.wait_ge(lin_used, GROUPS * PASSES + 1)

            def stage_run(n, half):
                n = n * RING + half * HALF
                act.copy(idx_stage[:, half * HALF:(half + 1) * HALF],
                         run_src[:, n:n + HALF] if isinstance(n, int) else run_src[:, bass.ds(n, HALF)]).then_inc(idx_staged, 1)

            def take_rows(c, k0, k1):
                score = record[c % 2].rearrange("p (t r) -> p t r", r=REC)
                rows_d = edge_rows[EDGE0[c]:EDGE0[c + 1], :].rearrange("(p t) f -> p t f", p=P)
                with act.Fori(k0, k1) as k:
                    for half in range(2):
                        for j in range(half * HALF, (half + 1) * HALF):
                            act.wait_ge(row_landed[j], k * 16 + (16 * (ITERS * 4 + ITER0[c] + 1)))
                        act.dma_start(rows_d[:, bass.ds(k * RING + half * HALF, HALF), :].rearrange("p t f -> p (t f)"),
                                      rows[:, half * HALF:(half + 1) * HALF, :].rearrange("p t f -> p (t f)"))\
                            .then_inc(rows_stored[half], 16)
                        act.copy(score[:, bass.ds(k * RING + half * HALF, HALF), 0:HEADS3],
                                 rows[:, half * HALF:(half + 1) * HALF, :].rearrange("p t (h f) -> p t h f", h=HEADS3)[:, :, :, DH3 + 1])\
                            .then_inc(score_taken, 1)
                        stage_run(k + (ITER0[c] + 1), half)

            def exponentials(c):
                act.wait_ge(exponents_ready, c + 1)
                w4 = record[c % 2].rearrange("p (t r) -> p t r", r=REC)[:, 0:SPAN[c], 0:HEADS3]
                act.activation(w4, w4, ACT.Exp).then_inc(alphas_ready, 1)
                if c > 0:
                    act.wait_ge(shift_placed, c)
                    act.activation(factor[:, :], ps[3][:, 512:512 + HEADS3], ACT.Exp).then_inc(factor_ready, 1)

            act.wait_ge(idx_staged, 2 * (ITERS + 1) * 4)
            stage_run(0, 0)
            stage_run(0, 1)
            take_rows(0, 0, CHUNK_ITERS[0])
            for c in range(1, NC):
                if c >= 2:
                    act.wait_ge(alphas_stored, 16 * (c - 1))
                take_rows(c, 0, SPLIT)
                exponentials(c - 1)
                take_rows(c, SPLIT, CHUNK_ITERS[c])
            exponentials(NC - 1)

        @block.tensor
        def _(pe):
            pe.sem_inc(partial_ready, PARTIAL0)
            for s in (lin_transposed, lin_product):
                pe.sem_inc(s, 1)
            pe.wait_ge(consts, 10)
            pe.wait_ge(counted, 1)
            pe.matmul(ps[2][:, 0:BLOCKS - 1], ones[:, :], first_tile[:, :], start=True, stop=True).then_inc(summed, 1)
            for c in range(CHUNKS):
                pe.wait_ge(step_rows_ready, c + 1)
                if c >= 2:
                    pe.wait_ge(step_table_ready, c - 1)
                for k in range(4):
                    mm = pe.transpose(ps[c % 2][:, k * P:(k + 1) * P], GATHER_STEPS[:, c, k, :], ident[:, :])
                mm.then_inc(step_turned, 1)

            pe.wait_ge(loaded_w, 16 * WLOADS)
            pe.wait_ge(step_table_ready, CHUNKS)

            def linear_group(g, p, weights):
                pe.wait_ge(lin_staged, g + (GROUPS * p + 2))
                pe.wait_ge(lin_turned, g + (GROUPS * p + 1))
                for j in range(GROUP):
                    mm = pe.transpose(ps[0][:, j * D:(j + 1) * D], stage[:, j, :], ident[:, :])
                mm.then_inc(lin_transposed, 1)
                pe.wait_ge(lin_turned, g + (GROUPS * p + 2))
                pe.wait_ge(lin_used, g + (GROUPS * p + 1))
                for j in range(GROUP):
                    for i, m in enumerate(weights):
                        n = m.shape[-1]
                        mm = pe.matmul(ps[1 + i][:, j * n:(j + 1) * n], turned[:, j, :], m[:, :], start=True, stop=True)
                mm.then_inc(lin_product, 1)

            def linear(p, weights):
                with pe.Fori(0, GROUPS) as g:
                    linear_group(g, p, weights)

            def partials(layer, width, p, weights, extras=()):
                def body(k):
                    for j in range(RING):
                        n = k * RING + (STEPS * layer + j + 1)
                        pe.wait_ge(onehot_ready, n)
                        pe.wait_ge(row_scaled, n + SCALED0)
                        pe.wait_ge(block_added, n)
                        pe.matmul(step_sum(j, width), onehot[:, j % HALF, :], scaled[:, j % HALF, 0:width],
                                  start=True, stop=True).then_inc(partial_ready, 1)

                with pe.Fori(0, GROUPS) as k:
                    body(k)
                    linear_group(k, p, weights)
                at = GROUPS
                for stop, extra in (*extras, (ITERS, None)):
                    with pe.Fori(at, stop) as k:
                        body(k)
                    if extra:
                        extra()
                    at = stop

            def starts():
                pe.wait_ge(cnt_ready, 1)
                pe.matmul(ps[1][:, 0:BLOCKS], tri[:, :], cnt[:, :], start=True, stop=True)
                pe.matmul(ps[2][:, 0:BLOCKS], ones[:, :], cnt[:, :], start=True, stop=True).then_inc(starts_summed, 1)

            def quads():
                pe.wait_ge(quads_counted, 1)
                pe.matmul(ps[1][:, 0:NC * (BLOCKS - 1)], ones[:, :], cmp[:, 0:NC * (BLOCKS - 1)], start=True, stop=True)\
                    .then_inc(quads_summed, 1)
                pe.wait_ge(offsets_ready, 1)
                for i in range(2 * NC):
                    mm = pe.matmul(ps[2][:, i * P:(i + 1) * P], ones[:, :], diag[:, i, :], start=True, stop=True)
                mm.then_inc(offsets_spread, 1)

            partials(0, D + 1, KV, [W["k"], W["v"]])
            pe.wait_ge(agg_done, 1)
            linear(QUERY, [W["q"]])
            linear(OUT0, [W["o"]])
            partials(1, D, ROOT, [W["root"]], [(AT_STARTS, starts), (AT_QUADS, quads)])
            pe.wait_ge(agg_done, 2)
            pe.wait_ge(offsets_spread, 2)
            linear(REL, [W["rel"]])
            partials(2, D, SELF2A, [W["neigh0"], W["self0"]])
            pe.wait_ge(agg_done, 3)
            linear(NEIGH2A, [W["neigh0"]])
            partials(3, D, SELF2B, [W["neigh1"], W["self1"]])
            pe.wait_ge(agg_done, 4)
            linear(NEIGH2B, [W["neigh1"]])
            linear(AGG2, [W["agg"]])
            pe.wait_ge(starts_ready, 1)
            linear(HEADS, [W["heads"], w_lr])
            pe.wait_ge(lin_used, GROUPS * PASSES + 1)
            pe.sem_inc(quad_partial, QRING)
            for c in range(NC):
                pe.wait_ge(carries_ready, c + 1)
                for i in range(6):
                    mm = pe.transpose(ps[1 + i // 4][0:HEADS3, (i % 4) * P:(i % 4 + 1) * P], carry[:, i, :], ident[:, :])
                mm.then_inc(carries_turned, 1)
                pe.wait_ge(chains_ready, c + 1)
                for i in range(2):
                    mm = pe.transpose(ps[3][:, i * HEADS3:(i + 1) * HEADS3], chain_out[:, i, :], ident[0:HEADS3, 0:HEADS3])
                mm.then_inc(chains_turned, 1)
                if c > 0:
                    pe.wait_ge(shift_ready, c)
                    pe.matmul(ps[3][:, 512:512 + HEADS3], seam_place[0:1, c - 1, :], shift[0:1, :], start=True, stop=True)\
                        .then_inc(shift_placed, 1)
                with pe.Fori(0, QITERS[c]) as k:
                    for j in range(QRING):
                        n = k * QRING + (QSTEP0[c] + j + 1)
                        pe.wait_ge(quad_ready, n)
                        pe.wait_ge(quad_scaled, n)
                        pe.wait_ge(quad_added, n)
                        for q in range(4):
                            mm = pe.matmul(ps[j % 3][:, 0:AGG_W], quad_onehot[:, j % 3, q, :],
                                           quad_rows[:, j, q, :].rearrange("p (h f) -> p h f", h=HEADS3)[:, :, 0:DH3 + 1],
                                           start=(q == 0), stop=(q == 3))
                        mm.then_inc(quad_partial, 1)

        @block.vector
        def _(dve):
            done = [0]

            class Chain:
                def __init__(self, per=0, g=None):
                    self.base, self.n, self.per, self.g = done[0], 0, per, g

                def then(self, ins):
                    ins.then_inc(ve, 1)
                    self.n += 1
                    if self.g is None:
                        done[0] += 1
                        dve.wait_ge(ve, self.base + self.n)
                    else:
                        dve.wait_ge(ve, self.g * self.per + (self.base + self.n))

                def close(self):
                    assert self.n == self.per
                    done[0] += self.per * GROUPS

            def bc(a, n):
                return a.rearrange("p (j a) -> p j a", a=1).to_broadcast([P, a.shape[-1], n])

            def flat(a):
                return a.rearrange("p j f -> p (j f)")

            def grp(t, g, w=D):
                return t[:, bass.ds(g * GROUP, GROUP), 0:w]

            def pg(i, w=D):
                return ps[i][:, 0:GROUP * w].rearrange("p (j f) -> p j f", f=w)

            def rowbc(t):
                return t.rearrange("p (a f) -> p a f", a=1).to_broadcast([P, GROUP, D])

            NORM_OPS = 4

            def norm(c, g, n):
                for j in range(GROUP):
                    ins = dve.bn_stats(stats[:, j, :], X[:, bass.ds(g * GROUP + j, 1), :].rearrange("p a f -> p (a f)"))
                c.then(ins)
                dve.sem_inc(norm_stats, 1)
                for j in range(GROUP):
                    ins = dve.bn_aggr(moments[:, j, :], stats[:, j, :])
                c.then(ins)
                dve.sem_inc(norm_sum, 1)
                dve.wait_ge(norm_root, g + (GROUPS * n + 1))
                dve.wait_ge(normed, g + (GROUPS * n + 1))
                c.then(dve.reciprocal(small[:, 4, 0:GROUP], small[:, 3, 0:GROUP]))
                c.then(dve.scalar_tensor_tensor(out=small[:, 5, 0:GROUP], in0=moments[:, :, 0], scalar=-1.0,
                                                in1=small[:, 4, 0:GROUP], op0=ALU.mult, op1=ALU.mult))
                dve.sem_inc(norm_scaled, 1)

            def sums(layer, width, other, extras=()):
                def body(k):
                    _, at = nc.values_load_multi_w_load_instructions(
                        step_block[0:1, bass.ds(k * RING, RING)], engines=DVE_ONLY, min_val=0, max_val=BLOCKS - 1,
                        skip_runtime_bounds_check_because="a step's block is below BLOCKS by construction")
                    for half in range(2):
                        for j in range(half * HALF, (half + 1) * HALF):
                            dve.wait_ge(partial_ready, k * RING + (STEPS * layer + j + 1))
                            dve.tensor_scalar(onehot[:, j % HALF, :], iota[:, :],
                                              step_table[:, S_PLACE, bass.ds(k * RING + j, 1)], None, ALU.is_equal)\
                                .then_inc(onehot_ready, 1)
                        for j in range(half * HALF, (half + 1) * HALF):
                            dve.wait_ge(partial_ready, k * RING + (STEPS * layer + j + 1 + PARTIAL0))
                            dve.wait_ge(block_added, k * RING + (STEPS * layer + j + ADDED0))
                            s = AGG[:, bass.ds(at[j], 1), 0:width].rearrange("p a f -> p (a f)")
                            dve.tensor_tensor(s, s, step_sum(j, width), ALU.add).then_inc(block_added, 1)

                dve.memset(AGG[:, :, :].rearrange("p b f -> p (b f)"), 0.0).then_inc(agg_cleared, 1)
                dve.wait_ge(agg_cleared, layer + 1)
                dve.wait_ge(step_table_ready, CHUNKS)
                dve.wait_ge(blocks_loaded, 16)
                per, group = other
                with dve.Fori(0, GROUPS) as k:
                    body(k)
                    c = Chain(per, k)
                    group(c, k)
                c.close()
                at = GROUPS
                for stop, extra in (*extras, (ITERS, None)):
                    with dve.Fori(at, stop) as k:
                        body(k)
                    if extra:
                        extra()
                    at = stop
                dve.wait_ge(block_added, STEPS * (layer + 1) + ADDED0)
                dve.sem_inc(agg_done, 1)

            dve.sem_inc(block_added, ADDED0)
            dve.sem_inc(lin_used, 1)
            c = Chain()
            c.then(dve.memset(chunk_i[:, 1, :], int(PAD_DST)))
            c.then(dve.memset(TR[:, :, 2, :], 0.0))
            c.then(dve.memset(LOGITS, 0.0))
            c.then(dve.memset(X[:, BLOCKS - 1, :], 0.0))
            dve.wait_ge(consts, 1)
            dve.sem_inc(cleared, 2)
            dve.wait_ge(consts, 10)
            c.then(dve.tensor_scalar(ident[:, :], iota[:, :], pidx[:, 0:1], None, ALU.is_equal))
            c.then(dve.tensor_scalar(tri[:, :], iota[:, :], pidx[:, 0:1], None, ALU.is_gt))
            c.then(dve.memset(quad_last_i[:, :], int(PAD_DST)))
            for i in range(NC):
                c.then(dve.memset(quad_count[:, i:i + 1], float(QUADS[i] - 1)))
                c.then(dve.memset(quad_base[:, i:i + 1], float(EDGE0[i] // QUAD)))
            dve.sem_inc(quads_padded, 1)
            dve.wait_ge(loaded_edges, 16 * 9)
            for k in range(2):
                c.then(dve.tensor_copy(TR[:, :, k, :], chunk_i[:, k, :].rearrange("p (c e) -> p c e", e=P)))
            dve.sem_inc(tile_rows_ready, 1)
            c.then(dve.tensor_tensor(cmp[:, :].rearrange("p (b c) -> p b c", c=CHUNKS),
                                     TR[:, :, 1, P - 1:P].rearrange("p c a -> p a c").to_broadcast([P, BLOCKS - 1, CHUNKS]),
                                     block_edge[:, :].rearrange("p (b a) -> p b a", a=1).to_broadcast([P, BLOCKS - 1, CHUNKS]),
                                     ALU.is_lt))
            c.then(dve.tensor_reduce(first_tile[:, :], cmp[:, :].rearrange("p (b c) -> p b c", c=CHUNKS), AX, ALU.add))
            dve.sem_inc(counted, 1)
            dve.wait_ge(summed, 1)
            c.then(dve.tensor_tensor(block_edge[:, :], ps[2][:, 0:BLOCKS - 1], block_no[:, :], ALU.add))
            c.then(dve.tensor_tensor(cmp[:, :].rearrange("p (c b) -> p c b", c=CHUNKS),
                                     block_edge[:, :].rearrange("p (a b) -> p a b", a=1).to_broadcast([P, CHUNKS, BLOCKS - 1]),
                                     step_no[:, :].rearrange("p (c a) -> p c a", a=1).to_broadcast([P, CHUNKS, BLOCKS - 1]),
                                     ALU.is_le))
            c.then(dve.tensor_reduce(step_b[:, :], cmp[:, :].rearrange("p (c b) -> p c b", c=CHUNKS), AX, ALU.add))
            c.then(dve.tensor_tensor(step_t[:, :], step_no[:, :], step_b[:, :], ALU.subtract))
            c.then(dve.tensor_scalar(step_off[:, :], step_b[:, :], -float(P), None, ALU.mult))
            c.then(dve.tensor_copy(step_b_i[:, :], step_b[:, :]))
            c.then(dve.tensor_copy(step_t_i[:, :], step_t[:, :]))
            dve.sem_inc(step_index_ready, 1)
            for i, (cc, at) in enumerate(ATTR):
                dve.wait_ge(loaded_attr[i], 16 if i < 4 else 32)
                n = cc.stop - cc.start
                a = scratch[:, at:at + n * EAW].rearrange("p (c e a) -> p c e a", c=n, a=EDGE_ATTRS)
                if i < 4:
                    dve.tensor_reduce(LOGITS[:, cc, :], a, AX, ALU.add).then_inc(logits_ready, 1)
                else:
                    c.then(dve.tensor_reduce(LOGITS[0:rest + 1, 12, 0:tail], a[0:rest + 1, 0, 0:tail, :], AX, ALU.add))
                    dve.tensor_reduce(LOGITS[0:rest, 12, tail:P], a[0:rest, 0, tail:P, :], AX, ALU.add)\
                        .then_inc(logits_ready, 1)
                dve.wait_ge(logits_ready, i + 1)
                dve.sem_inc(attr_used, 1)
            dve.wait_ge(loaded_x, 32)
            dve.wait_ge(sigmoid_ready, 1)
            with dve.Fori(0, GROUPS) as g:
                c = Chain(NORM_OPS, g)
                norm(c, g, 0)
            c.close()
            c = Chain()
            for ch in range(CHUNKS):
                dve.wait_ge(step_rows_landed[ch >= 6], 16 * (6 if ch < 6 else CHUNKS - 6))
                c.then(dve.tensor_scalar(GATHER_STEPS[:, ch, 1, :], GATHER_STEPS[:, ch, 1, :], step_off[:, ch:ch + 1],
                                         None, ALU.add))
                dve.sem_inc(step_rows_ready, 1)
            dve.wait_ge(loaded_w, 16 * WLOADS)
            for i in range(2):
                c.then(dve.tensor_tensor(bsum[:, i, :], bias[f"self{i}"][:, :], bias[f"neigh{i}"][:, :], ALU.add))
                c.then(dve.tensor_tensor(bsum[:, i, :], bsum[:, i, :], bias[f"layer{i}"][:, :], ALU.add))
            dve.wait_ge(step_turned, CHUNKS)
            dve.wait_ge(table_stored, 16 * GROUPS)

            def products(p, g):
                dve.wait_ge(lin_product, g + (GROUPS * p + 2))

            def keys_values(c, g):
                products(KV, g)
                c.then(dve.tensor_copy(grp(R, g), pg(1)))
                c.then(dve.tensor_copy(grp(H, g), pg(2)))
                dve.sem_inc(lin_used, 1)
                c.then(dve.tensor_tensor(grp(X, g), grp(X, g), rowbc(bias["o"][:, :]), ALU.add))

            sums(0, D + 1, (3, keys_values))
            c = Chain()
            c.then(dve.tensor_copy(cnt[:, :], AGG[:, :, D]))
            c.then(dve.tensor_scalar(inv_mean0[:, :], cnt[:, :], 1.0, None, ALU.max))
            c.then(dve.reciprocal(inv_mean0[:, :], inv_mean0[:, :]))
            c.then(dve.tensor_scalar(inv_mean0[:, :], inv_mean0[:, :], SCALE0, None, ALU.mult))
            c.then(dve.tensor_scalar(inv_mean2[:, :], cnt[:, :], 1.0, None, ALU.add))
            c.then(dve.reciprocal(inv_mean2[:, :], inv_mean2[:, :]))
            dve.sem_inc(cnt_ready, 1)
            with dve.Fori(0, GROUPS) as g:
                c = Chain(4, g)
                products(QUERY, g)
                c.then(dve.tensor_tensor(cen, pg(1), grp(R, g), ALU.mult))
                sc = small[:, 6, 0:GROUP * HEADS0]
                c.then(dve.tensor_reduce(sc, flat(cen).rearrange("p (h d) -> p h d", d=DH0), AX, ALU.add))
                c.then(dve.tensor_tensor(sc.rearrange("p (j h) -> p j h", h=HEADS0), sc.rearrange("p (j h) -> p j h", h=HEADS0),
                                         bc(inv_mean0[:, bass.ds(g * GROUP, GROUP)], HEADS0), ALU.mult))
                v = flat(grp(H, g)).rearrange("p (h d) -> p h d", d=DH0)
                c.then(dve.tensor_tensor(v, v, bc(sc, DH0), ALU.mult))
                dve.sem_inc(lin_used, 1)
            c.close()
            with dve.Fori(0, GROUPS) as g:
                c = Chain(1 + NORM_OPS, g)
                products(OUT0, g)
                c.then(dve.tensor_tensor(grp(X, g), grp(X, g), pg(1), ALU.add))
                dve.sem_inc(lin_used, 1)
                norm(c, g, 1)
            c.close()
            def root_terms(c, g):
                products(ROOT, g)
                c.then(dve.tensor_tensor(grp(R, g), pg(1), rowbc(bias["rel"][:, :]), ALU.add))
                dve.sem_inc(lin_used, 1)

            def starts():
                dve.wait_ge(starts_summed, 1)
                c = Chain()
                c.then(dve.tensor_copy(before[:, 0, :], ps[2][:, 0:BLOCKS]))
                c.then(dve.tensor_tensor_scan(before[:, 1, :], before[:, 0, :], zeros[:, 0:BLOCKS], 0.0, ALU.add, ALU.add))
                c.then(dve.tensor_tensor(before[:, 1, :], before[:, 1, :], before[:, 0, :], ALU.subtract))
                c.then(dve.tensor_tensor(before[:, 1, :], before[:, 1, :], ps[1][:, 0:BLOCKS], ALU.add))
                c.then(dve.tensor_scalar(before[:, 2, :], cnt[:, :], 0.0, float(2 * E_PAD), ALU.is_equal, ALU.mult))
                c.then(dve.tensor_tensor(first_edge[:, :], before[:, 1, :], before[:, 2, :], ALU.add))
                for i, k_ in enumerate(("left", "right")):
                    c.then(dve.tensor_tensor(W[k_][:, :], W[k_][:, :], W["heads"][:, :], ALU.mult))
                    c.then(dve.tensor_reduce(w_lr[:, i * HEADS3:(i + 1) * HEADS3], W[k_][:, :].rearrange("p (h o) -> p h o", o=DH3),
                                             AX, ALU.add))
                dve.sem_inc(starts_ready, 1)

            def quads():
                NB = BLOCKS - 1
                c = Chain()
                dve.wait_ge(quads_loaded, 16 * (2 * NC - 1))
                c.then(dve.tensor_copy(quad_last[:, :], quad_last_i[:, :]))
                quad_cmp = cmp[:, 0:NC * NB].rearrange("p (c b) -> p c b", c=NC)
                quad_cmp2 = cmp[:, NC * NB:2 * NC * NB].rearrange("p (c b) -> p c b", c=NC)
                c.then(dve.tensor_tensor(quad_cmp, quad_last[:, :].rearrange("p (c a) -> p c a", a=1).to_broadcast([P, NC, NB]),
                                         block_start[:, :].rearrange("p (a b) -> p a b", a=1).to_broadcast([P, NC, NB]), ALU.is_lt))
                dve.sem_inc(quads_counted, 1)
                dve.wait_ge(quads_summed, 1)
                c.then(dve.tensor_tensor(quad_cmp2, ps[1][:, 0:NC * NB].rearrange("p (c b) -> p c b", c=NC),
                                         block_no[:, :].rearrange("p (a b) -> p a b", a=1).to_broadcast([P, NC, NB]), ALU.add))
                for i in range(2):
                    c.then(dve.tensor_scalar(quad_cmp, quad_cmp2, step_no[:, i:i + 1], None, ALU.is_le))
                    c.then(dve.tensor_reduce(quad_b[:, i, :], quad_cmp, AX, ALU.add))
                    c.then(dve.tensor_scalar(quad_t[:, i, :], quad_b[:, i, :], -1.0, step_no[:, i:i + 1], ALU.mult, ALU.add))
                    c.then(dve.tensor_tensor(quad_over[:, i, :], quad_t[:, i, :], quad_count[:, :], ALU.is_gt))
                    c.then(dve.tensor_tensor(quad_t[:, i, :], quad_t[:, i, :], quad_count[:, :], ALU.min))
                    c.then(dve.tensor_tensor(quad_i[:, 1, i, :], quad_t[:, i, :], quad_base[:, :], ALU.add))
                    c.then(dve.tensor_copy(quad_i[:, 0, i, :], quad_b[:, i, :]))
                dve.sem_inc(quads_ready, 1)
                c.then(dve.tensor_scalar(quad_over[:, :, :], quad_over[:, :, :], 2 * PAD_DST, None, ALU.mult))
                c.then(dve.scalar_tensor_tensor(out=quad_over[:, :, :], in0=quad_b[:, :, :], scalar=float(P), in1=quad_over[:, :, :],
                                                op0=ALU.mult, op1=ALU.add))
                for i in range(2 * NC):
                    c.then(dve.tensor_scalar(diag[:, i, :], ident[:, :], quad_over[:, i % 2, i // 2:i // 2 + 1], None, ALU.mult))
                dve.sem_inc(offsets_ready, 1)
                dve.wait_ge(offsets_spread, 1)
                c.then(dve.tensor_copy(quad_off[:, :, :].rearrange("p c s -> p (c s)"), ps[2][:, :]))
                dve.sem_inc(offsets_spread, 1)
                c.then(dve.tensor_copy(seam[:, 0, :], seam_i[:, :]))
                ns = NC - 1
                seam_cmp = cmp[:, 0:ns * NB].rearrange("p (c b) -> p c b", c=ns)
                c.then(dve.tensor_tensor(seam_cmp, block_start[:, :].rearrange("p (a b) -> p a b", a=1).to_broadcast([P, ns, NB]),
                                         seam[:, 0, :].rearrange("p (c a) -> p c a", a=1).to_broadcast([P, ns, NB]), ALU.is_le))
                c.then(dve.tensor_reduce(seam[:, 1, :], seam_cmp, AX, ALU.add))
                c.then(dve.tensor_copy(seam_b[:, :], seam[:, 1, :]))
                c.then(dve.scalar_tensor_tensor(out=seam[:, 2, :], in0=seam[:, 1, :], scalar=-float(P), in1=seam[:, 0, :],
                                                op0=ALU.mult, op1=ALU.add))
                for i in range(ns):
                    c.then(dve.tensor_scalar(seam_place[:, i, :], iota[:, :], seam[:, 2, i:i + 1], None, ALU.is_equal))

            sums(1, D, (1, root_terms), [(AT_STARTS, starts), (AT_QUADS, quads)])
            with dve.Fori(0, GROUPS) as g:
                c = Chain(2 + NORM_OPS, g)
                products(REL, g)
                c.then(dve.tensor_tensor(cen, pg(1), grp(R, g), ALU.add))
                c.then(dve.scalar_tensor_tensor(out=grp(X, g), in0=cen, scalar=0.0, in1=grp(X, g), op0=ALU.max, op1=ALU.add))
                dve.sem_inc(lin_used, 1)
                norm(c, g, 2)
            c.close()

            def self_terms(p, i, with_bias):
                def group(c, g):
                    products(p, g)
                    c.then(dve.tensor_tensor(cen, pg(1), bc(inv_mean2[:, bass.ds(g * GROUP, GROUP)], D), ALU.mult))
                    c.then(dve.tensor_tensor(cen, cen, pg(2), ALU.add))
                    dve.sem_inc(lin_used, 1)
                    c.then(dve.tensor_tensor(grp(R, g), cen, rowbc(bsum[:, i, :]), ALU.add))
                    if with_bias:
                        c.then(dve.tensor_tensor(grp(X, g), grp(X, g), rowbc(bias["agg"][:, :]), ALU.add))
                return 3 + with_bias, group

            def neighbours(p, table):
                with dve.Fori(0, GROUPS) as g:
                    c = Chain(3, g)
                    products(p, g)
                    c.then(dve.tensor_tensor(cen, pg(1), bc(inv_mean2[:, bass.ds(g * GROUP, GROUP)], D), ALU.mult))
                    c.then(dve.tensor_tensor(cen, cen, grp(R, g), ALU.add))
                    c.then(dve.scalar_tensor_tensor(out=grp(H, g), in0=cen, scalar=SLOPE, in1=cen, op0=ALU.mult, op1=ALU.max))
                    dve.sem_inc(lin_used, 1)
                    if table:
                        dve.sem_inc(table_ready, 1)
                c.close()

            sums(2, D, self_terms(SELF2A, 0, 1))
            neighbours(NEIGH2A, True)
            sums(3, D, self_terms(SELF2B, 1, 0))
            dve.wait_ge(idx_staged, 2 * (ITERS + 1) * 4)
            c = Chain()
            c.then(dve.memset(run_src, 0))
            c.then(dve.memset(run_dst, int(PAD_DST)))
            c.then(dve.memset(run_dst[:, 0:1], -1))
            c.then(dve.memset(logw, 1.0))
            dve.sem_inc(runs_padded, 1)
            neighbours(NEIGH2B, False)
            with dve.Fori(0, GROUPS) as g:
                c = Chain(1 + NORM_OPS, g)
                products(AGG2, g)
                c.then(dve.tensor_tensor(grp(X, g), grp(X, g), pg(1), ALU.add))
                dve.sem_inc(lin_used, 1)
                norm(c, g, 3)
            c.close()

            c = Chain()
            c.then(dve.memset(HT[:, :, :, DH3:DH3 + 1], 1.0))
            with dve.Fori(0, GROUPS) as g:
                c = Chain(4, g)
                products(HEADS, g)
                ht = HT[:, bass.ds(g * GROUP, GROUP), :, :]
                c.then(dve.tensor_copy(ht[:, :, :, 0:DH3], pg(1).rearrange("p j (h f) -> p j h f", f=DH3)))
                lr = ps[2][:, 0:GROUP * 2 * HEADS3].rearrange("p (j k h) -> p j k h", k=2, h=HEADS3)
                c.then(dve.tensor_copy(ht[:, :, :, DH3 + 1], lr[:, :, 0, :]))
                c.then(dve.tensor_copy(right[:, bass.ds(g * GROUP, GROUP), :], lr[:, :, 1, :]))
                dve.sem_inc(heads_ready, 1)
                dve.sem_inc(lin_used, 1)
                c.then(dve.tensor_tensor(grp(X, g), grp(X, g), rowbc(bias["out"][:, :]), ALU.add))
            c.close()
            c = Chain()
            c.then(dve.memset(right0[:, :, :], 0.0))
            dve.wait_ge(runs_loaded, 16 * RUN_LOADS)
            for i in range(NC):
                c.then(dve.tensor_copy(dst0[:, i:i + 1], run_dst[:, RUN0[i] + 2 * i + 1:RUN0[i] + 2 * i + 2]))
            dve.sem_inc(dst0_ready, 1)
            c.then(dve.tensor_scalar(logw, logw, 1e-8, None, ALU.max))
            dve.sem_inc(logw_ready, 1)
            dve.wait_ge(heads_stored, 16 * GROUPS)
            c.then(dve.memset(AGG.rearrange("p b f -> p (b f)"), 0.0))
            dve.wait_ge(logw_ready, 2)
            dve.wait_ge(right0_loaded, 16 * NC)
            dve.wait_ge(quad_row_loaded, 32)
            dve.sem_inc(quad_added, 3)

            def softmax(i):
                S = SPAN[i]
                rec = record[i % 2].rearrange("p (t r) -> p t r", r=REC)[:, 0:S, :]
                score = rec[:, :, 0:HEADS3]
                right_e = right_b[:, 0:S * HEADS3].rearrange("p (t h) -> p t h", h=HEADS3)
                same, keep, fwd, bwd = same_b[:, 0:S + 1], keep_b[:, 0:S + 1], fwd_b[:, 0:S], bwd_b[:, 0:S]
                dst_x = dst_b[:, 0:S + 2]
                o = RUN0[i] + 2 * i
                c.then(dve.tensor_copy(dst_x, run_dst[:, o:o + S + 2]))
                c.then(dve.tensor_tensor(same, dst_x[:, 1:], dst_x[:, 0:S + 1], ALU.is_equal))
                c.then(dve.tensor_scalar(keep, same, 0.5, 2 * BIG, ALU.subtract, ALU.mult))
                dve.wait_ge(right_loaded, 16 * (i + 1))
                for h in range(HEADS3):
                    c.then(dve.tensor_tensor_scan(right_e[:, :, h], same[:, 0:S], right_e[:, :, h], right0[:, i, h:h + 1],
                                                  ALU.mult, ALU.add))
                dve.wait_ge(score_taken, 2 * ITER0[i + 1])
                c.then(dve.tensor_tensor(score, score, right_e, ALU.add))
                dve.sem_inc(right_used, 1)
                c.then(dve.scalar_tensor_tensor(out=score, in0=score, scalar=SLOPE, in1=score, op0=ALU.mult, op1=ALU.max))
                c.then(dve.tensor_tensor(score, score, logw[:, RUN0[i]:RUN0[i + 1]].rearrange("p (t a) -> p t a", a=1)
                                         .to_broadcast([P, S, HEADS3]), ALU.add))
                c.then(dve.tensor_copy(rec[:, :, HEADS3], dst_x[:, 1:S + 1]))

                def forward(h, initial):
                    c.then(dve.tensor_tensor_scan(fwd, keep[:, 0:S], score[:, :, h], initial, ALU.min, ALU.max))

                def backward(initial):
                    c.then(dve.tensor_tensor_scan(bwd[:, ::-1], keep[:, 1:S + 1][:, ::-1], fwd[:, ::-1], initial, ALU.min, ALU.max))

                for h in range(HEADS3):
                    forward(h, -BIG)
                    c.then(dve.tensor_copy(carry[:, 0, h:h + 1], fwd[:, S - 1:S]))
                    backward(-BIG)
                    c.then(dve.tensor_copy(carry[:, 3, h:h + 1], bwd[:, 0:1]))

                def flag(k, a, b):
                    c.then(dve.tensor_tensor(carry_in[:, 0, 0:1], dst_x[:, a:a + 1], dst_x[:, b:b + 1], ALU.is_equal))
                    c.then(dve.tensor_scalar(carry[:, k, :], carry_in[:, 0, 0:1].to_broadcast([P, HEADS3]), 0.5, 2 * BIG,
                                             ALU.subtract, ALU.mult))
                flag(1, 0, S)
                flag(2, 0, 1)
                flag(4, 1, S + 1)
                flag(5, S, S + 1)
                dve.sem_inc(carries_ready, 1)
                dve.wait_ge(carries_turned, i + 1)
                c.then(dve.tensor_copy(chain[:, 0:4, :].rearrange("h k p -> h (k p)"), ps[1][0:HEADS3, 0:4 * P]))
                c.then(dve.tensor_copy(chain[:, 4:6, :].rearrange("h k p -> h (k p)"), ps[2][0:HEADS3, 0:2 * P]))
                lo, hi = slice(0, P - 1), slice(1, P)
                c.then(dve.memset(chain_out[:, 0:2, :], -BIG))
                if i:
                    c.then(dve.tensor_tensor(chain_out[:, 0, 0:1], chain_end[:, :], chain[:, 2, 0:1], ALU.min))
                c.then(dve.tensor_tensor_scan(chain_out[:, 2, :], chain[:, 1, :], chain[:, 0, :], chain_end[:, 0:1] if i else -BIG,
                                              ALU.min, ALU.max))
                c.then(dve.tensor_tensor(chain_out[:, 0, hi], chain_out[:, 2, lo], chain[:, 2, hi], ALU.min))
                c.then(dve.tensor_tensor_scan(chain_out[:, 3, ::-1], chain[:, 4, ::-1], chain[:, 3, ::-1], -BIG, ALU.min, ALU.max))
                c.then(dve.tensor_tensor(chain_out[:, 1, lo], chain_out[:, 3, hi], chain[:, 5, lo], ALU.min))
                c.then(dve.tensor_copy(chain_end[:, :], chain_out[:, 2, P - 1:P]))
                dve.sem_inc(chains_ready, 1)
                dve.wait_ge(chains_turned, i + 1)
                c.then(dve.tensor_copy(carry_in[:, :, :].rearrange("p k h -> p (k h)"), ps[3][:, 0:2 * HEADS3]))
                for h in range(HEADS3):
                    forward(h, carry_in[:, 0, h:h + 1])
                    backward(carry_in[:, 1, h:h + 1])
                    c.then(dve.tensor_copy(shift[:, h:h + 1], bwd[:, 0:1]))
                    c.then(dve.tensor_tensor(score[:, :, h], score[:, :, h], bwd, ALU.subtract))
                dve.sem_inc(exponents_ready, 1)
                if i:
                    c.then(dve.tensor_tensor(shift[:, :], carry_in[:, 0, :], shift[:, :], ALU.subtract))
                    c.then(dve.tensor_scalar(shift[:, :], shift[:, :], same[:, 0:1], None, ALU.mult))
                    dve.sem_inc(shift_ready, 1)
                    dve.wait_ge(factor_ready, i)
                    _, at = nc.values_load_multi_w_load_instructions(
                        seam_b[0:1, i - 1:i], engines=DVE_ONLY, min_val=0, max_val=BLOCKS - 1,
                        skip_runtime_bounds_check_because="a node's block is below BLOCKS")
                    a = AGG[:, bass.ds(at[0], 1), :].rearrange("p a (h f) -> p (a h) f", h=HEADS3)
                    c.then(dve.tensor_tensor(a, a, factor[:, :].rearrange("p (h a) -> p h a", a=1)
                                             .to_broadcast([P, HEADS3, DH3 + 1]), ALU.mult))

            def quad_sums(i):
                with dve.Fori(0, QITERS[i]) as k:
                    _, at = nc.values_load_multi_w_load_instructions(
                        quad_row[0:1, 0, bass.ds(k * QRING + QCOLS * i, QRING)], engines=DVE_ONLY, min_val=0, max_val=BLOCKS - 1,
                        skip_runtime_bounds_check_because="a quad step's block is below BLOCKS by construction")

                    def prepare(j):
                        n = k * QRING + (QSTEP0[i] + j + 1)
                        rec = quad_rec[:, j, :].rearrange("p (q r) -> p q r", r=REC)
                        place = quad_place[:, j % 2, :]
                        dve.wait_ge(quad_landed[j], k * 32 + (32 * (QSTEP0[i] // QRING + 1)))
                        dve.tensor_scalar(place, rec[:, :, HEADS3], quad_off[:, i, bass.ds(k * QRING + j, 1)], None,
                                          ALU.subtract).then_inc(quad_placed, 1)
                        rows_ = quad_rows[:, j, :, :].rearrange("p q (h f) -> p q h f", h=HEADS3)[:, :, :, 0:DH3 + 1]
                        al = rec[:, :, 0:HEADS3].rearrange("p q (h a) -> p q h a", a=1).to_broadcast([P, 4, HEADS3, DH3 + 1])
                        dve.tensor_tensor(rows_, rows_, al, ALU.mult).then_inc(quad_scaled, 1)
                        dve.wait_ge(quad_placed, n)
                        dve.wait_ge(quad_partial, n + (QRING - 3))
                        dve.tensor_tensor(quad_onehot[:, j % 3, :, :],
                                          iota[:, :].rearrange("p (a d) -> p a d", a=1).to_broadcast([P, 4, P]),
                                          place.rearrange("p (q a) -> p q a", a=1).to_broadcast([P, 4, P]),
                                          ALU.is_equal).then_inc(quad_ready, 1)

                    def add(j):
                        n = k * QRING + (QSTEP0[i] + j)
                        dve.wait_ge(quad_partial, n + (1 + QRING))
                        dve.wait_ge(quad_added, n + 3)
                        a = AGG[:, bass.ds(at[j], 1), :].rearrange("p a f -> p (a f)")
                        dve.tensor_tensor(a, a, ps[j % 3][:, 0:AGG_W], ALU.add)\
                            .then_inc(quad_added, 1)

                    prepare(0)
                    for j in range(1, QRING):
                        prepare(j)
                        add(j - 1)
                    add(QRING - 1)
                dve.wait_ge(quad_added, QSTEP0[i + 1] + 3)

            for i in range(NC):
                softmax(i)
                quad_sums(i)
            agg3 = AGG.rearrange("p b (h f) -> p b h f", f=DH3 + 1)
            with dve.Fori(0, GROUPS) as g:
                c = Chain(5, g)
                a3 = agg3[:, bass.ds(g * GROUP, GROUP), :, :]
                r = small[:, 6, 0:GROUP * HEADS3].rearrange("p (j h) -> p j h", h=HEADS3)
                c.then(dve.tensor_copy(r, a3[:, :, :, DH3]))
                c.then(dve.tensor_scalar(small[:, 6, 0:GROUP * HEADS3], small[:, 6, 0:GROUP * HEADS3], 1e-8, None, ALU.add))
                c.then(dve.reciprocal(small[:, 6, 0:GROUP * HEADS3], small[:, 6, 0:GROUP * HEADS3]))
                c4 = cen.rearrange("p j (h f) -> p j h f", f=DH3)
                c.then(dve.tensor_tensor(c4, a3[:, :, :, 0:DH3],
                                         r.rearrange("p j (h a) -> p j h a", a=1).to_broadcast([P, GROUP, HEADS3, DH3]), ALU.mult))
                c.then(dve.tensor_tensor(grp(X, g), grp(X, g), cen, ALU.add))
                dve.sem_inc(out_ready, 1)
            c.close()


def kernel(**inputs):
    import numpy as np
    import concourse.bacc as bacc
    from concourse.bass_utils import run_bass_kernel_spmd

    def a(name):
        return np.asarray(inputs[name])

    arrays = {
        "x": a("x"), "src": a("src"), "dst": a("dst"), "edge_attr": a("edge_attr_16"), "edge_weight": a("edge_weight"),
        "q": a("L0_gnn_w_q"), "k": a("L0_gnn_w_k"), "v": a("L0_gnn_w_v"), "o": a("L0_gnn_w_o"),
        "rel": a("L1_gnn_W_rel").T, "root": a("L1_gnn_W_root").T,
        "self0": a("L2_gnn_W_self")[0].T, "self1": a("L2_gnn_W_self")[1].T,
        "neigh0": a("L2_gnn_W_neigh")[0].T, "neigh1": a("L2_gnn_W_neigh")[1].T, "agg": a("L2_gnn_W_agg").T,
        "b_o": a("L0_gnn_b_o"), "b_rel": a("L1_gnn_b_rel"),
        "b_self0": a("L2_gnn_b_self")[0], "b_self1": a("L2_gnn_b_self")[1],
        "b_neigh0": a("L2_gnn_b_neigh")[0], "b_neigh1": a("L2_gnn_b_neigh")[1],
        "b_layer0": a("L2_gnn_layer_bias")[0], "b_layer1": a("L2_gnn_layer_bias")[1], "b_agg": a("L2_gnn_b_agg"),
        "heads": a("L3_gnn_W").transpose(1, 0, 2).reshape(D, HEADS3 * DH3),
        "left": a("L3_gnn_a_l").reshape(-1), "right": a("L3_gnn_a_r").reshape(-1), "b_out": a("L3_gnn_bias"),
    }
    nc = bacc.Bacc("TRN2", target_bir_lowering=False, num_devices=1)
    arrays = {k: np.ascontiguousarray(v) for k, v in arrays.items()}
    aps = {k: nc.dram_tensor(f"in_{k}", v.shape, mybir.dt.from_np(v.dtype), kind="ExternalInput").ap()
           for k, v in arrays.items()}
    out = nc.dram_tensor("out", (N, D), F32, kind="ExternalOutput").ap()
    build(nc, aps["x"], aps["src"], aps["dst"], aps["edge_attr"], aps["edge_weight"], aps, out)
    r = run_bass_kernel_spmd(nc, [{f"in_{k}": v for k, v in arrays.items()}], core_ids=[0])
    return r.results[0]["out"]
```

```python
from contextlib import ExitStack

import concourse.bass as bass
from concourse import mybir

P = 128
N = 6250
E = 200000
D = 128
EDGE_ATTRS = 16
TILES = -(-E // P)
BLOCKS = -(-N // P)
GROUP = 7
GROUPS = BLOCKS // GROUP
RING = 16
HALF = RING // 2
STEPS = -(-(TILES + BLOCKS - 1) // RING) * RING
ITERS = STEPS // RING
CHUNKS = -(-(STEPS + RING) // P)
COLS = CHUNKS * P
AGG_W = 132
HEADS0, DH0 = 8, 16
HEADS3, DH3 = 4, 32
SCALE0 = DH0 ** -0.5
EPS = 1e-5
SLOPE = 0.2
ROW3 = HEADS3 * (DH3 + 2)
SPAN_ITERS = -(-E // (P * RING))
BIG = 1e38
CHUNK_ITERS = (30, 23, 18, 15, SPAN_ITERS - 86)
NC = len(CHUNK_ITERS)
AT_STAGE, AT_TRANSPOSES, AT_COPY, AT_PRODUCTS = 0, 1, 8, 9
AT_STARTS, AT_QUADS = 40, 60
SPLIT = 2
SPAN = [RING * i for i in CHUNK_ITERS]
ITER0 = [sum(CHUNK_ITERS[:c]) for c in range(NC + 1)]
RUN0 = [RING * i for i in ITER0]
EDGE0 = [P * RING * i for i in ITER0]
E_PAD = EDGE0[NC]
QUAD = 4 * P
QUADS = [P * n // QUAD for n in SPAN]
QRING = 6
QBODY = 2 * QRING
QITERS = [-(-(n + BLOCKS - 1) // QBODY) for n in QUADS]
QSTEP0 = [QBODY * sum(QITERS[:c]) for c in range(NC + 1)]
QCOLS = 2 * P
assert max(QITERS) * QBODY <= QCOLS and all(n % 4 == 0 for n in SPAN)
REC = HEADS3 + 1
PAD_DST = 20000.0
assert GROUPS * GROUP == BLOCKS and TILES <= COLS

ALU = mybir.AluOpType
ACT = mybir.ActivationFunctionType
AX = mybir.AxisListType.X
F32 = mybir.dt.float32
I32 = mybir.dt.int32
DVE_ONLY = (mybir.EngineType.DVE,)
SP_ONLY = (mybir.EngineType.SP,)

(KV, QUERY, OUT0, ROOT, REL, SELF2A, NEIGH2A, SELF2B, NEIGH2B, AGG2, HEADS) = range(11)
PASSES = 11
WRITING = (QUERY, REL, NEIGH2A, NEIGH2B)


def build(nc, x, src, dst, edge_attr, edge_weight, w, out):
    ctx = ExitStack()
    with ctx:
        def sb(name, shape, dt=F32):
            return ctx.enter_context(nc.sbuf_tensor(name, shape, dt))

        def sem(name):
            return ctx.enter_context(nc.semaphore(name))

        def dram(name, shape, dt=F32):
            return nc.dram_tensor(name, shape, dt, kind="Internal").ap()

        tile_rows = dram("tile_rows", [COLS, 4 * P])
        step_block_d = dram("step_block_d", [1, COLS], I32)
        tables = [dram(f"table{i}", [BLOCKS * P, D]) for i in range(4)]
        head_table = dram("head_table", [BLOCKS * P, ROW3])
        right_table = dram("right_table", [BLOCKS * P, HEADS3])
        right_edges = dram("right_edges", [E_PAD, HEADS3])
        edge_rows = dram("edge_rows", [E_PAD, ROW3])
        edge_records = dram("edge_records", [E_PAD, REC])
        quad_d = [dram(f"quad_{n}_d", [1, NC * QCOLS], I32) for n in ("block", "tile")]

        X = sb("X", [P, BLOCKS, D])
        H = sb("H", [P, BLOCKS, D])
        scratch = sb("scratch", [P, BLOCKS * D + BLOCKS * AGG_W])
        R = scratch[:, 0:BLOCKS * D].rearrange("p (b f) -> p b f", f=D)
        AGG = scratch[:, BLOCKS * D:].rearrange("p (b f) -> p b f", f=AGG_W)
        step_table = sb("step_table", [P, 4, COLS])
        S_SRC, S_PLACE, S_W, S_W0 = range(4)
        step_block = sb("step_block", [1, COLS], I32)
        idx_stage = sb("idx_stage", [P, RING], I32)
        rows = sb("rows", [P, RING, ROW3])
        scaled = sb("scaled", [P, HALF, AGG_W])
        onehot = sb("onehot", [P, HALF, P])
        work = sb("work", [P, 4, GROUP * D])
        stage, turned, cen = (work[:, i, :].rearrange("p (j f) -> p j f", f=D) for i in range(3))
        small = sb("small", [P, 8, GROUP * HEADS0])
        stats = sb("stats", [P, GROUP, 6])
        moments = sb("moments", [P, GROUP, 2])
        iota = sb("iota", [P, P])
        pidx = sb("pidx", [P, 1])
        ident = sb("ident", [P, P])
        ones = sb("ones", [P, P])
        epst = sb("epst", [P, 1])
        cnt = sb("cnt", [P, BLOCKS])
        inv_mean0 = sb("inv_mean0", [P, BLOCKS])
        inv_mean2 = sb("inv_mean2", [P, BLOCKS])
        W_NAMES = ("q", "k", "v", "o", "rel", "root", "self0", "self1", "neigh0", "neigh1", "agg", "heads", "left", "right")
        w_all = sb("w_all", [P, len(W_NAMES), D])
        W = {k: w_all[:, i, :] for i, k in enumerate(W_NAMES)}
        bias = {k: sb(f"b_{k}", [P, D]) for k in
                ("o", "rel", "self0", "neigh0", "layer0", "self1", "neigh1", "layer1", "agg", "out")}
        bsum = sb("bsum", [P, 2, D])
        chunk_i = work[:, :, :].rearrange("p i f -> p (i f)")[:, 0:2 * COLS].bitcast(I32).rearrange("p (k e) -> p k e", k=2)
        block_edge = sb("block_edge", [P, BLOCKS - 1])
        block_no = sb("block_no", [P, BLOCKS - 1])
        step_no = sb("step_no", [P, CHUNKS])
        cmp = sb("cmp", [P, (BLOCKS - 1) * CHUNKS])
        first_tile = sb("first_tile", [P, BLOCKS - 1])
        step_b = sb("step_b", [P, CHUNKS])
        step_t = sb("step_t", [P, CHUNKS])
        step_off = sb("step_off", [P, CHUNKS])
        step_b_i = sb("step_b_i", [P, CHUNKS], I32)
        step_t_i = sb("step_t_i", [P, CHUNKS], I32)
        tri = sb("tri", [P, P])
        before = sb("before", [P, 3, BLOCKS])
        first_edge = sb("first_edge", [P, BLOCKS], I32)
        w_lr = sb("w_lr", [P, 2 * HEADS3])
        right = sb("right", [P, BLOCKS, HEADS3])
        right0 = sb("right0", [P, NC, HEADS3])
        zeros = sb("zeros", [P, E_PAD // P * HEADS3 // 16])
        dst0 = sb("dst0", [P, NC], I32)
        carry = sb("carry", [P, 6, HEADS3])
        carry_in = sb("carry_in", [P, 2, HEADS3])
        shift = sb("shift", [P, HEADS3])
        factor = sb("factor", [P, HEADS3])
        chain = sb("chain", [HEADS3, 6, P])
        chain_out = sb("chain_out", [HEADS3, 4, P])
        chain_end = sb("chain_end", [HEADS3, 1])
        block_start = sb("block_start", [P, BLOCKS - 1])
        quad_last_i = sb("quad_last_i", [P, NC], I32)
        quad_last = sb("quad_last", [P, NC])
        quad_count = sb("quad_count", [P, NC])
        quad_base = sb("quad_base", [P, NC])
        quad_b = sb("quad_b", [P, 2, NC])
        quad_t = sb("quad_t", [P, 2, NC])
        quad_over = sb("quad_over", [P, 2, NC])
        quad_i = sb("quad_i", [P, 2, 2, NC], I32)
        quad_row = sb("quad_row", [1, 2, NC * QCOLS], I32)
        quad_off = sb("quad_off", [P, NC, QCOLS])
        seam_i = sb("seam_i", [P, NC - 1], I32)
        seam = sb("seam", [P, 3, NC - 1])
        seam_b = sb("seam_b", [P, NC - 1], I32)
        seam_place = w_all[:, 0:NC - 1, :]
        assert NC - 1 <= 4
        quad_rec = sb("quad_rec", [P, QRING, 4 * REC])
        quad_place = sb("quad_place", [P, 4, 4])

        HT = scratch[:, 0:BLOCKS * ROW3].rearrange("p (b h f) -> p b h f", h=HEADS3, f=DH3 + 2)
        Hflat = H[:, :, :].rearrange("p b f -> p (b f)")
        SM = max(SPAN)

        def carve(base):
            at = [0]

            def piece(n):
                at[0] += n
                assert at[0] <= base.shape[-1], (at[0], base.shape)
                return base[:, at[0] - n:at[0]]
            return piece
        piece = carve(Hflat)
        record = [piece(SM * REC) for _ in range(2)]
        same_b, keep_b = piece(SM + 1), piece(SM + 1)
        piece = carve(scratch[:, 0:BLOCKS * D])
        quad_rows = piece(QRING * 4 * ROW3).rearrange("p (s q f) -> p s q f", s=QRING, q=4)
        quad_onehot = piece(3 * 4 * P).rearrange("p (s q d) -> p s q d", s=3, q=4)
        fwd_b, bwd_b, dst_b = piece(SM), piece(SM), piece(SM + 2)
        piece = carve(step_table[:, :, :].rearrange("p k c -> p (k c)"))
        run_src = piece(E_PAD // P + RING).bitcast(I32)
        run_dst = piece(E_PAD // P + 2 * NC).bitcast(I32)
        logw = piece(E_PAD // P)
        right_b = piece(SM * HEADS3)

        ps = [ctx.enter_context(nc.psum_tensor(f"ps{i}", [P, 1024], F32)) for i in range(4)]

        loaded_x = sem("loaded_x")
        loaded_edges = sem("loaded_edges")
        loaded_attr = [sem(f"loaded_attr{i}") for i in range(5)]
        loaded_w = sem("loaded_w")
        consts = sem("consts")
        cleared = sem("cleared")
        attr_used = sem("attr_used")
        logits_ready = sem("logits_ready")
        sigmoid_ready = sem("sigmoid_ready")
        tile_rows_ready = sem("tile_rows_ready")
        tile_rows_stored = sem("tile_rows_stored")
        counted = sem("counted")
        summed = sem("summed")
        step_index_ready = sem("step_index_ready")
        step_rows_landed = [sem(f"step_rows_landed{i}") for i in range(2)]
        step_rows_ready = sem("step_rows_ready")
        step_turned = sem("step_turned")
        step_table_ready = sem("step_table_ready")
        blocks_stored = sem("blocks_stored")
        blocks_loaded = sem("blocks_loaded")
        ve = sem("ve")
        norm_stats = sem("norm_stats")
        sqrt_loaded = sem("sqrt_loaded")
        norm_sum = sem("norm_sum")
        norm_root = sem("norm_root")
        norm_scaled = sem("norm_scaled")
        normed = sem("normed")
        table_stored = sem("table_stored")
        lin_staged = sem("lin_staged")
        lin_transposed = sem("lin_transposed")
        lin_turned = sem("lin_turned")
        lin_product = sem("lin_product")
        lin_used = sem("lin_used")
        rows_written = sem("rows_written")
        idx_staged = sem("idx_staged")
        row_landed = [sem(f"row_landed{j}") for j in range(RING)]
        row_scaled = sem("row_scaled")
        onehot_ready = sem("onehot_ready")
        partial_ready = sem("partial_ready")
        block_added = sem("block_added")
        agg_cleared = sem("agg_cleared")
        agg_done = sem("agg_done")
        out_stored = sem("out_stored")
        out_ready = sem("out_ready")
        zeroed = sem("zeroed")
        right_cleared = sem("right_cleared")
        cnt_ready = sem("cnt_ready")
        starts_summed = sem("starts_summed")
        starts_ready = sem("starts_ready")
        head_values = sem("head_values")
        heads_ready = sem("heads_ready")
        heads_stored = sem("heads_stored")
        right_stored = sem("right_stored")
        runs_padded = sem("runs_padded")
        runs_loaded = sem("runs_loaded")
        rows_stored = [sem(f"rows_stored{i}") for i in range(2)]
        score_taken = sem("score_taken")
        round_open = sem("round_open")
        right_scattered = sem("right_scattered")
        right0_loaded = sem("right0_loaded")
        right_loaded = sem("right_loaded")
        dst0_ready = sem("dst0_ready")
        logw_ready = sem("logw_ready")
        carries_ready = sem("carries_ready")
        carries_turned = sem("carries_turned")
        chains_ready = sem("chains_ready")
        chains_turned = sem("chains_turned")
        exponents_ready = sem("exponents_ready")
        alphas_ready = sem("alphas_ready")
        alphas_stored = sem("alphas_stored")
        right_used = sem("right_used")
        quads_padded = sem("quads_padded")
        quads_loaded = sem("quads_loaded")
        quads_counted = sem("quads_counted")
        quads_summed = sem("quads_summed")
        quads_ready = sem("quads_ready")
        offsets_ready = sem("offsets_ready")
        offsets_spread = sem("offsets_spread")
        quad_rows_stored = sem("quad_rows_stored")
        quad_row_loaded = sem("quad_row_loaded")
        shift_ready = sem("shift_ready")
        shift_placed = sem("shift_placed")
        factor_ready = sem("factor_ready")
        quad_landed = [sem(f"quad_landed{j}") for j in range(QRING)]
        quad_ready = sem("quad_ready")
        quad_partial = sem("quad_partial")
        quad_added = sem("quad_added")
        quad_placed = sem("quad_placed")
        quad_scaled = sem("quad_scaled")
        quarter_scaled = sem("quarter_scaled")

        SCALED0, PARTIAL0, ADDED0 = RING, HALF, 2

        full_tiles = E // P
        fullc = full_tiles // P
        rest = full_tiles - fullc * P
        tail = E - full_tiles * P

        def tiled(a, width):
            yield slice(0, P), slice(0, fullc), a[0:fullc * P * P * width].rearrange("(c p e) -> p c e", p=P, e=P * width)
            yield slice(0, rest), fullc, a[fullc * P * P * width:full_tiles * P * width].rearrange("(p e) -> p e", e=P * width)
            yield slice(rest, rest + 1), fullc, a[full_tiles * P * width:].rearrange("(p e) -> p e", p=1)

        TR = step_table[:, :, :].rearrange("p k c -> p (k c)").rearrange("p (c k e) -> p c k e", k=4, e=P)
        WLOADS = len(W) + len(bias)
        attr = edge_attr.rearrange("e a -> (e a)")
        EAW = P * EDGE_ATTRS
        LOGITS = TR[:, :, 3, :]
        moments0 = cmp[:, 0:BLOCKS * 2].rearrange("p (b m) -> p b m", m=2)
        root0, scale0, shift0 = (cmp[:, BLOCKS * i:BLOCKS * (i + 1)] for i in (2, 3, 4))
        ATTR = [(slice(3 * i, 3 * i + 3), (i % 2) * 3 * EAW) for i in range(4)] + [(slice(12, 13), 0)]
        GATHER_STEPS = scratch[:, 0:CHUNKS * 4 * P].rearrange("p (c k e) -> p c k e", k=4, e=P)

        diag = work[:, 2:4, :].rearrange("p i f -> p (i f)")[:, 0:2 * NC * P].rearrange("p (i m) -> p i m", m=P)

        def step_sum(j, width):
            at = j % 2 * 512
            return ps[3][:, at:at + width]

        def grp_of(t, g):
            return t[:, bass.ds(g * GROUP, GROUP), :]

        def every(a, first, step, n):
            return bass.AP(tensor=a.tensor, offset=first, ap=[[step, n], [1, 1]])

        RUN_LOADS = sum(5 + 3 * ((min(E, EDGE0[c + 1]) - EDGE0[c]) % SPAN[c] > 0) for c in range(NC))

        block = ctx.enter_context(nc.Block())

        @block.sync
        def _(sp):
            sp.wait_ge(cleared, 2)
            for k, a in ((0, src), (1, dst)):
                for pp, cc, s in tiled(a, 1):
                    n = s.shape[-1]
                    t = chunk_i[pp, k, :].rearrange("p (c e) -> p c e", e=P)
                    sp.dma_start(t[:, cc, 0:n], s).then_inc(loaded_edges, 16)
            for pp, cc, s in tiled(edge_weight, 1):
                sp.dma_start(TR[pp, cc, 2, 0:s.shape[-1]], s).then_inc(loaded_edges, 16)
            sp.dma_start(X[:, 0:BLOCKS - 1, :], x[0:(BLOCKS - 1) * P, :].rearrange("(b p) f -> p b f", p=P))\
                .then_inc(loaded_x, 16)
            last = N - (BLOCKS - 1) * P
            sp.dma_start(X[0:last, BLOCKS - 1, :], x[(BLOCKS - 1) * P:, :]).then_inc(loaded_x, 16)
            for i, (cc, at) in enumerate(ATTR):
                if i == 2:
                    for k in ("q", "k", "v", "o", "rel", "root", "self0", "self1", "neigh0", "neigh1", "agg", "heads"):
                        sp.dma_start(W[k][:, :], w[k]).then_inc(loaded_w, 16)
                    for k, t in (("left", W["left"]), ("right", W["right"])):
                        sp.dma_start(t[:, :], w[k].rearrange("(a f) -> a f", a=1).to_broadcast([P, D])).then_inc(loaded_w, 16)
                    for k in ("o", "rel", "self0", "neigh0", "layer0", "self1", "neigh1", "layer1", "agg", "out"):
                        sp.dma_start(bias[k][:, :], w["b_" + k].rearrange("(a f) -> a f", a=1).to_broadcast([P, D]))\
                            .then_inc(loaded_w, 16)
                    sp.wait_ge(tile_rows_ready, 1)
                    sp.wait_ge(loaded_edges, 16 * 9)
                    sp.dma_start(tile_rows.rearrange("(c p) e -> p c e", p=P)[:, :, 0:3 * P],
                                 TR[:, :, 0:3, :].rearrange("p c k e -> p c (k e)")).then_inc(tile_rows_stored, 16)
                if i >= 2:
                    sp.wait_ge(attr_used, i - 1)
                dst_ = scratch[:, at:at + 3 * EAW].rearrange("p (c e) -> p c e", c=3)
                if i < 4:
                    s = attr[cc.start * P * EAW:cc.stop * P * EAW].rearrange("(c p e) -> p c e", p=P, e=EAW)
                    sp.dma_start(dst_, s).then_inc(loaded_attr[i], 16)
                else:
                    s = attr[fullc * P * EAW:full_tiles * EAW].rearrange("(p e) -> p e", e=EAW)
                    sp.dma_start(dst_[0:rest, 0, :], s).then_inc(loaded_attr[i], 16)
                    s = attr[full_tiles * EAW:].rearrange("(p e) -> p e", p=1)
                    sp.dma_start(dst_[rest:rest + 1, 0, 0:tail * EDGE_ATTRS], s).then_inc(loaded_attr[i], 16)
            def store_table(layer):
                rows_d = tables[layer].rearrange("(g j p) f -> g p j f", p=P, j=GROUP)
                with sp.Fori(0, GROUPS) as g:
                    if layer < 3:
                        sp.wait_ge(normed, g + (GROUPS * layer + 2))
                    else:
                        sp.wait_ge(rows_written, g + (GROUPS * WRITING.index(NEIGH2A) + 1))
                    sp.dma_start(rows_d[bass.ds(g, 1), :, :, :].rearrange("a p j f -> (a p) j f"),
                                 H[:, bass.ds(g * GROUP, GROUP), :]).then_inc(table_stored, 16)

            store_table(0)
            sp.wait_ge(sigmoid_ready, 1)
            sp.dma_start(tile_rows.rearrange("(c p) e -> p c e", p=P)[:, :, 3 * P:], TR[:, :, 3, :]).then_inc(tile_rows_stored, 16)
            sp.wait_ge(step_index_ready, 1)
            sp.dma_start(step_block_d.rearrange("a (c p) -> p (a c)", p=P), step_b_i[:, :],
                         allow_slow_non_contiguous=True).then_inc(blocks_stored, 16)
            sp.wait_ge(blocks_stored, 16)
            sp.dma_start(step_block[:, :], step_block_d).then_inc(blocks_loaded, 16)

            sp.wait_ge(quads_padded, 1)
            for c in range(NC):
                n = min(QUADS[c], (E - EDGE0[c]) // QUAD)
                sp.dma_start(quad_last_i[0:n, c:c + 1], every(dst, EDGE0[c] + QUAD - 1, QUAD, n),
                             allow_slow_non_contiguous=True).then_inc(quads_loaded, 16)
            for c in range(1, NC):
                sp.dma_start(seam_i[:, c - 1:c], every(dst, EDGE0[c] - 1, 0, P), allow_slow_non_contiguous=True)\
                    .then_inc(quads_loaded, 16)

            for layer in range(1, 4):
                if layer == 1:
                    sp.wait_ge(cnt_ready, 1)
                    sp.wait_ge(zeroed, 1)
                    sp.dma_start(right_edges.rearrange("(p r t) h -> p r (t h)", p=P, r=16),
                                 zeros[:, :].rearrange("p (a t) -> p a t", a=1).to_broadcast([P, 16, zeros.shape[-1]]))\
                        .then_inc(right_cleared, 16)
                if layer == 2:
                    sp.wait_ge(quads_ready, 1)
                    for i in range(2):
                        for c in range(NC):
                            sp.dma_start(quad_d[i][:, c * QCOLS:(c + 1) * QCOLS].rearrange("a (k p) -> p (a k)", p=P),
                                         quad_i[:, i, :, c], allow_slow_non_contiguous=True).then_inc(quad_rows_stored, 16)
                    sp.wait_ge(quad_rows_stored, 16 * 2 * NC)
                    for i in range(2):
                        sp.dma_start(quad_row[:, i, :], quad_d[i]).then_inc(quad_row_loaded, 16)
                store_table(layer)
            sp.wait_ge(runs_padded, 1)
            for c in range(NC):
                full = min(P, (E - EDGE0[c]) // SPAN[c])
                more = min(E, EDGE0[c + 1]) - EDGE0[c] - full * SPAN[c]
                for a_, t_, o_ in ((src, run_src, RUN0[c]), (dst, run_dst, RUN0[c] + 2 * c + 1), (edge_weight, logw, RUN0[c])):
                    a_ = a_[EDGE0[c]:min(E, EDGE0[c + 1])]
                    sp.dma_start(t_[0:full, o_:o_ + SPAN[c]], a_[0:full * SPAN[c]].rearrange("(p t) -> p t", p=full))\
                        .then_inc(runs_loaded, 16)
                    if more:
                        sp.dma_start(t_[full:full + 1, o_:o_ + more], a_[full * SPAN[c]:].rearrange("(p t) -> p t", p=1))\
                            .then_inc(runs_loaded, 16)
                o_ = RUN0[c] + 2 * c
                p0 = 1 if c == 0 else 0
                n = min(P, -(-(E - EDGE0[c]) // SPAN[c])) - p0
                sp.dma_start(run_dst[p0:p0 + n, o_:o_ + 1], every(dst, EDGE0[c] + p0 * SPAN[c] - 1, SPAN[c], n),
                             allow_slow_non_contiguous=True).then_inc(runs_loaded, 16)
                n = min(P, (E - 1 - EDGE0[c]) // SPAN[c])
                sp.dma_start(run_dst[0:n, o_ + SPAN[c] + 1:o_ + SPAN[c] + 2], every(dst, EDGE0[c] + SPAN[c], SPAN[c], n),
                             allow_slow_non_contiguous=True).then_inc(runs_loaded, 16)
            heads_d = head_table.rearrange("(g j p) f -> g p j f", p=P, j=GROUP)
            with sp.Fori(0, GROUPS) as g:
                sp.wait_ge(heads_ready, g + 1)
                sp.dma_start(heads_d[bass.ds(g, 1), :, :, :].rearrange("a p j f -> (a p) j f"),
                             HT[:, bass.ds(g * GROUP, GROUP), :, :].rearrange("p j h f -> p j (h f)")).then_inc(heads_stored, 16)
            sp.wait_ge(heads_ready, GROUPS)
            sp.dma_start(right_table.rearrange("(b p) h -> p b h", p=P), right[:, :, :]).then_inc(right_stored, 16)
            sp.wait_ge(right_scattered, 16 * BLOCKS)
            sp.wait_ge(quad_row_loaded, 32)

            def load_right(c):
                sp.dma_start(right_b[:, 0:SPAN[c] * HEADS3],
                             right_edges[EDGE0[c]:EDGE0[c + 1], :].rearrange("(p t) h -> p (t h)", p=P)).then_inc(right_loaded, 16)

            load_right(0)
            for c in range(NC):
                sp.wait_ge(alphas_ready, c + 1)
                sp.dma_start(edge_records[EDGE0[c]:EDGE0[c + 1], :].rearrange("(p t) f -> p (t f)", p=P),
                             record[c % 2][:, 0:SPAN[c] * REC]).then_inc(alphas_stored, 16)
                if c < NC - 1:
                    sp.wait_ge(right_used, c + 1)
                    load_right(c + 1)
                sp.wait_ge(alphas_stored, 16 * (c + 1))
                for half in range(2):
                    sp.wait_ge(rows_stored[half], 16 * ITER0[c + 1])
                quad_rows_d = edge_rows.rearrange("(t p q) f -> t p (q f)", p=P, q=4)
                quad_rec_d = edge_records.rearrange("(t p q) f -> t p (q f)", p=P, q=4)
                with sp.Fori(0, QITERS[c]) as k:
                    _, at = nc.values_load_multi_w_load_instructions(
                        quad_row[0:1, 1, bass.ds(k * QBODY + QCOLS * c, QBODY)], engines=SP_ONLY, min_val=0,
                        max_val=E_PAD // QUAD - 1, skip_runtime_bounds_check_because="a quad step's quad is below by construction")
                    for j in range(QBODY):
                        slot = j % QRING
                        sp.wait_ge(quad_partial, k * QBODY + (QSTEP0[c] + j + 1))
                        sp.dma_start(quad_rows[:, slot, :, :].rearrange("p q f -> p (q f)"),
                                     quad_rows_d[bass.ds(at[j], 1), :, :].rearrange("a p f -> (a p) f")).then_inc(quad_landed[slot], 16)
                        sp.dma_start(quad_rec[:, slot, :], quad_rec_d[bass.ds(at[j], 1), :, :].rearrange("a p f -> (a p) f"))\
                            .then_inc(quad_landed[slot], 16)
            with sp.Fori(0, GROUPS - 1) as g:
                sp.wait_ge(out_ready, g + 1)
                sp.dma_start(out[0:(BLOCKS - GROUP) * P, :].rearrange("(g j p) f -> g p j f", p=P, j=GROUP)[bass.ds(g, 1), :, :, :]
                             .rearrange("a p j f -> (a p) j f"), grp_of(X, g)).then_inc(out_stored, 16)
            sp.wait_ge(out_ready, GROUPS)
            sp.dma_start(out[(BLOCKS - GROUP) * P:(BLOCKS - 1) * P, :].rearrange("(b p) f -> p b f", p=P),
                         X[:, BLOCKS - GROUP:BLOCKS - 1, :]).then_inc(out_stored, 16)
            sp.dma_start(out[(BLOCKS - 1) * P:, :], X[0:last, BLOCKS - 1, :]).then_inc(out_stored, 16)
            sp.wait_ge(out_stored, 16 * (GROUPS + 1))

        @block.gpsimd
        def _(pool):
            pool.memset(chunk_i[:, 0, :], 0).then_inc(consts, 1)
            pool.iota(iota[:, :], [[1, P]], base=0, channel_multiplier=0,
                      allow_small_or_imprecise_dtypes=True).then_inc(consts, 1)
            pool.iota(pidx[:, :], [[1, 1]], base=0, channel_multiplier=1,
                      allow_small_or_imprecise_dtypes=True).then_inc(consts, 1)
            pool.iota(block_edge[:, :], [[P, BLOCKS - 1]], base=P, channel_multiplier=0,
                      allow_small_or_imprecise_dtypes=True).then_inc(consts, 1)
            pool.iota(block_start[:, :], [[P, BLOCKS - 1]], base=P, channel_multiplier=0,
                      allow_small_or_imprecise_dtypes=True).then_inc(consts, 1)
            pool.iota(block_no[:, :], [[1, BLOCKS - 1]], base=1, channel_multiplier=0,
                      allow_small_or_imprecise_dtypes=True).then_inc(consts, 1)
            pool.iota(step_no[:, :], [[P, CHUNKS]], base=0, channel_multiplier=1,
                      allow_small_or_imprecise_dtypes=True).then_inc(consts, 1)
            pool.memset(ones[:, :], 1.0).then_inc(consts, 1)
            pool.memset(epst[:, :], EPS).then_inc(consts, 1)
            pool.memset(zeros[:, :], 0.0).then_inc(zeroed, 1)
            pool.memset(scaled[:, :, D:AGG_W], 1.0).then_inc(consts, 1)
            pool.wait_ge(tile_rows_stored, 32)
            pool.wait_ge(step_index_ready, 1)
            pool.wait_ge(attr_used, 5)
            for c in range(CHUNKS):
                pool.indirect_dma_start(out=GATHER_STEPS[:, c, :, :].rearrange("p k e -> p (k e)"), out_offset=None,
                                        in_=tile_rows, in_offset=bass.IndirectOffsetOnAxis(ap=step_t_i[:, c:c + 1], axis=0))\
                    .then_inc(step_rows_landed[c >= 6], 16)

            def gathers(layer, table):
                pool.wait_ge(table_stored, 16 * GROUPS * (layer + 1))
                with pool.Fori(0, ITERS) as k:
                    for j in range(RING):
                        if j % HALF == 0:
                            pool.wait_ge(idx_staged, k * 2 + (2 * (ITERS + 1) * layer + j // HALF + 1))
                            pool.wait_ge(row_scaled, k * RING + (STEPS * layer + j + HALF))
                            pool.sem_inc(round_open, 1)
                        pool.indirect_dma_start(out=rows[:, j, 0:D], out_offset=None, in_=table,
                                                in_offset=bass.IndirectOffsetOnAxis(ap=idx_stage[:, j:j + 1], axis=0))\
                            .then_inc(row_landed[j], 16)

            for layer in range(4):
                gathers(layer, tables[layer])

            pool.wait_ge(right_cleared, 16)
            pool.wait_ge(starts_ready, 1)
            for b in range(BLOCKS):
                if b % GROUP == 0:
                    pool.wait_ge(heads_ready, b // GROUP + 1)
                pool.indirect_dma_start(out=right_edges, out_offset=bass.IndirectOffsetOnAxis(ap=first_edge[:, b:b + 1], axis=0),
                                        in_=right[:, b, :], in_offset=None, bounds_check=E_PAD - 1, oob_is_err=False)\
                    .then_inc(right_scattered, 16)
            pool.wait_ge(dst0_ready, 1)
            pool.wait_ge(right_stored, 16)
            for c in range(NC):
                pool.indirect_dma_start(out=right0[:, c, :], out_offset=None, in_=right_table,
                                        in_offset=bass.IndirectOffsetOnAxis(ap=dst0[:, c:c + 1], axis=0),
                                        bounds_check=BLOCKS * P - 1, oob_is_err=False).then_inc(right0_loaded, 16)
            pool.wait_ge(heads_stored, 16 * GROUPS)

            def run_gathers(k):
                for j in range(RING):
                    if j % HALF == 0:
                        half = j // HALF
                        pool.wait_ge(idx_staged, k * 2 + (2 * (ITERS + 1) * 4 + half + 1))
                        if not isinstance(k, int):
                            pool.wait_ge(rows_stored[half], k * 16)
                            pool.wait_ge(score_taken, k * 2 + (half - 1))
                        pool.sem_inc(round_open, 1)
                    pool.indirect_dma_start(out=rows[:, j, :], out_offset=None, in_=head_table,
                                            in_offset=bass.IndirectOffsetOnAxis(ap=idx_stage[:, j:j + 1], axis=0))\
                        .then_inc(row_landed[j], 16)

            run_gathers(0)
            with pool.Fori(1, SPAN_ITERS) as k:
                run_gathers(k)

        @block.scalar
        def _(act):
            act.sem_inc(row_scaled, SCALED0)
            for s in (lin_staged, lin_turned, normed):
                act.sem_inc(s, 1)

            def root_of(g, n):
                act.wait_ge(norm_sum, g + (GROUPS * n + 1))
                act.activation(small[:, 3, 0:GROUP], moments[:, :, 1], ACT.Sqrt, bias=epst[:, 0:1]).then_inc(norm_root, 1)

            def normalise(g, n):
                act.wait_ge(norm_scaled, g + (GROUPS * n + 1))
                for j in range(GROUP):
                    b = bass.ds(g * GROUP + j, 1)
                    ins = act.activation(H[:, b, :].rearrange("p a f -> p (a f)"), X[:, b, :].rearrange("p a f -> p (a f)"),
                                         ACT.Relu, bias=small[:, 5, j:j + 1], scale=small[:, 4, j:j + 1])
                ins.then_inc(normed, 1)

            def stage_group(g, p, source, ready, base):
                if ready:
                    act.wait_ge(ready, g + (base + 1))
                act.wait_ge(lin_transposed, g + (GROUPS * p + 1))
                at = g * GROUP
                src_ = source[:, at:at + GROUP, 0:D] if isinstance(g, int) else source[:, bass.ds(at, GROUP), 0:D]
                act.copy(stage, src_).then_inc(lin_staged, 1)

            def copy_turned(g, p):
                act.wait_ge(lin_transposed, g + (GROUPS * p + 2))
                act.wait_ge(lin_product, g + (GROUPS * p + 1))
                act.copy(turned.rearrange("p j f -> p (j f)"), ps[0][:, 0:GROUP * D]).then_inc(lin_turned, 1)

            def turn(p, source, ready, base, n=None):
                if n is None:
                    with act.Fori(0, GROUPS) as g:
                        stage_group(g, p, source, ready, base)
                        copy_turned(g, p)
                    return
                stage_group(0, p, source, ready, base)
                copy_turned(0, p)
                stage_group(1, p, source, ready, base)
                with act.Fori(0, GROUPS - 2) as g:
                    copy_turned(g + 1, p)
                    stage_group(g + 2, p, source, ready, base)
                    root_of(g, n)
                    normalise(g, n)
                copy_turned(GROUPS - 1, p)
                root_of(GROUPS - 2, n)
                normalise(GROUPS - 2, n)
                root_of(GROUPS - 1, n)
                normalise(GROUPS - 1, n)

            def turn_agg(p, layers, n=None):
                act.wait_ge(agg_done, layers)
                turn(p, AGG, None, 0, n)

            def stage_indices(layer, k, half):
                act.copy(idx_stage[:, half * HALF:(half + 1) * HALF],
                         step_table[:, S_SRC, bass.ds(k * RING + half * HALF, HALF)] if not isinstance(k, int)
                         else step_table[:, S_SRC, k * RING + half * HALF:k * RING + (half + 1) * HALF])\
                    .then_inc(idx_staged, 1)

            def first_indices(layer):
                if layer:
                    act.wait_ge(idx_staged, 2 * (ITERS + 1) * layer)
                for half in range(2):
                    stage_indices(layer, 0, half)

            def scale(layer, weights, p, ready, base):
                def body(k, linear=False):
                    for j in range(RING):
                        if linear and j == AT_STAGE:
                            stage_group(k, p, H, ready, base)
                        if linear and j == AT_COPY:
                            copy_turned(k, p)
                        act.wait_ge(row_landed[j], k * 16 + (16 * (ITERS * layer + 1)))
                        act.wait_ge(partial_ready, k * RING + (STEPS * layer + j + 1))
                        by = 1.0 if weights is None else step_table[:, weights, bass.ds(k * RING + j, 1)]
                        act.activation(scaled[:, j % HALF, 0:D], rows[:, j, 0:D], ACT.Copy, scale=by)\
                            .then_inc(row_scaled, 1)
                        if j % HALF == HALF - 1:
                            stage_indices(layer, k + 1, j // HALF)

                with act.Fori(0, GROUPS) as k:
                    body(k, linear=True)
                with act.Fori(GROUPS, ITERS) as k:
                    body(k)

            act.wait_ge(norm_sum, GROUPS)
            act.activation(root0, moments0[:, :, 1], ACT.Sqrt, bias=epst[:, 0:1]).then_inc(norm_root, GROUPS)
            act.wait_ge(norm_scaled, GROUPS)
            with act.Fori(0, GROUPS) as g:
                for j in range(GROUP):
                    b = bass.ds(g * GROUP + j, 1)
                    ins = act.activation(H[:, b, :].rearrange("p a f -> p (a f)"), X[:, b, :].rearrange("p a f -> p (a f)"),
                                         ACT.Relu, bias=shift0[:, b], scale=scale0[:, b])
                ins.then_inc(normed, 1)
            act.wait_ge(logits_ready, 5)
            act.activation(TR[:, :, 3, :], LOGITS, ACT.Sigmoid).then_inc(sigmoid_ready, 1)
            act.activation(small[:, 3, 0:1], epst[:, 0:1], ACT.Sqrt).then_inc(sqrt_loaded, 1)
            act.wait_ge(sqrt_loaded, 1)
            act.wait_ge(tile_rows_stored, 32)
            for c in range(CHUNKS):
                act.wait_ge(step_turned, c + 1)
                act.copy(step_table[:, :, c * P:(c + 1) * P],
                         ps[c % 2][:, 0:4 * P].rearrange("p (k s) -> p k s", k=4)).then_inc(step_table_ready, 1)
                if c == 0:
                    act.wait_ge(step_table_ready, 1)
                    first_indices(0)
            scale(0, S_W0, KV, normed, 1)
            first_indices(1)
            turn_agg(QUERY, 1)
            turn(OUT0, H, rows_written, GROUPS * WRITING.index(QUERY), n=1)
            scale(1, None, ROOT, normed, GROUPS + 1)
            first_indices(2)
            turn_agg(REL, 2, n=2)
            scale(2, S_W, SELF2A, normed, 2 * GROUPS + 1)
            first_indices(3)
            turn_agg(NEIGH2A, 3)
            scale(3, S_W, SELF2B, rows_written, GROUPS * WRITING.index(NEIGH2A))
            turn_agg(NEIGH2B, 4)
            turn(AGG2, H, rows_written, GROUPS * WRITING.index(NEIGH2B), n=3)
            turn(HEADS, H, normed, 3 * GROUPS + 1)
            act.wait_ge(runs_loaded, 16 * RUN_LOADS)
            act.wait_ge(logw_ready, 1)
            act.activation(logw, logw, ACT.Ln).then_inc(logw_ready, 1)
            act.wait_ge(lin_used, GROUPS * PASSES + 1)

            def stage_run(n, half):
                n = n * RING + half * HALF
                act.copy(idx_stage[:, half * HALF:(half + 1) * HALF],
                         run_src[:, n:n + HALF] if isinstance(n, int) else run_src[:, bass.ds(n, HALF)]).then_inc(idx_staged, 1)

            def take_rows(c, k0, k1):
                score = record[c % 2].rearrange("p (t r) -> p t r", r=REC)
                rows_d = edge_rows[EDGE0[c]:EDGE0[c + 1], :].rearrange("(p t) f -> p t f", p=P)
                with act.Fori(k0, k1) as k:
                    for half in range(2):
                        for j in range(half * HALF, (half + 1) * HALF):
                            act.wait_ge(row_landed[j], k * 16 + (16 * (ITERS * 4 + ITER0[c] + 1)))
                        act.dma_start(rows_d[:, bass.ds(k * RING + half * HALF, HALF), :].rearrange("p t f -> p (t f)"),
                                      rows[:, half * HALF:(half + 1) * HALF, :].rearrange("p t f -> p (t f)"))\
                            .then_inc(rows_stored[half], 16)
                        act.copy(score[:, bass.ds(k * RING + half * HALF, HALF), 0:HEADS3],
                                 rows[:, half * HALF:(half + 1) * HALF, :].rearrange("p t (h f) -> p t h f", h=HEADS3)[:, :, :, DH3 + 1])\
                            .then_inc(score_taken, 1)
                        stage_run(k + (ITER0[c] + 1), half)

            def exponentials(c):
                act.wait_ge(exponents_ready, c + 1)
                w4 = record[c % 2].rearrange("p (t r) -> p t r", r=REC)[:, 0:SPAN[c], 0:HEADS3]
                act.activation(w4, w4, ACT.Exp).then_inc(alphas_ready, 1)
                if c > 0:
                    act.wait_ge(shift_placed, c)
                    act.activation(factor[:, :], ps[3][:, 512:512 + HEADS3], ACT.Exp).then_inc(factor_ready, 1)

            act.wait_ge(idx_staged, 2 * (ITERS + 1) * 4)
            stage_run(0, 0)
            stage_run(0, 1)
            take_rows(0, 0, CHUNK_ITERS[0])
            for c in range(1, NC):
                if c >= 2:
                    act.wait_ge(alphas_stored, 16 * (c - 1))
                take_rows(c, 0, SPLIT)
                exponentials(c - 1)
                take_rows(c, SPLIT, CHUNK_ITERS[c])
            exponentials(NC - 1)
            with act.Fori(0, QITERS[NC - 1]) as k:
                for j in range(QBODY):
                    n = k * QBODY + (QSTEP0[NC - 1] + j + 1)
                    slot = j % QRING
                    rec = quad_rec[:, slot, :].rearrange("p (q r) -> p q r", r=REC)
                    act.wait_ge(quad_landed[slot], k * 64 + (32 * (QSTEP0[NC - 1] // QRING + j // QRING + 1)))
                    act.wait_ge(quad_ready, n - 4)
                    act.activation(quad_place[:, j % 4, :], rec[:, :, HEADS3], ACT.Identity,
                                   bias=quad_off[:, NC - 1, bass.ds(k * QBODY + j, 1)]).then_inc(quad_placed, 1)
                    for h in range(HEADS3):
                        at = h * (DH3 + 2)
                        row = quad_rows[:, slot, 3, at:at + DH3 + 1]
                        ins = act.activation(row, row, ACT.Copy, scale=rec[:, 3, h:h + 1])
                    ins.then_inc(quarter_scaled, 1)

        @block.tensor
        def _(pe):
            pe.sem_inc(partial_ready, PARTIAL0)
            for s in (lin_transposed, lin_product):
                pe.sem_inc(s, 1)
            pe.wait_ge(consts, 10)
            pe.wait_ge(counted, 1)
            pe.matmul(ps[2][:, 0:BLOCKS - 1], ones[:, :], first_tile[:, :], start=True, stop=True).then_inc(summed, 1)
            for c in range(CHUNKS):
                pe.wait_ge(step_rows_ready, c + 1)
                if c >= 2:
                    pe.wait_ge(step_table_ready, c - 1)
                for k in range(4):
                    mm = pe.transpose(ps[c % 2][:, k * P:(k + 1) * P], GATHER_STEPS[:, c, k, :], ident[:, :])
                mm.then_inc(step_turned, 1)

            pe.wait_ge(loaded_w, 16 * WLOADS)
            pe.wait_ge(step_table_ready, CHUNKS)

            def transposes(g, p, blocks=range(GROUP)):
                if blocks[0] == 0:
                    pe.wait_ge(lin_staged, g + (GROUPS * p + 2))
                    pe.wait_ge(lin_turned, g + (GROUPS * p + 1))
                for j in blocks:
                    mm = pe.transpose(ps[0][:, j * D:(j + 1) * D], stage[:, j, :], ident[:, :])
                if blocks[-1] == GROUP - 1:
                    mm.then_inc(lin_transposed, 1)

            def products(g, p, weights, blocks=range(GROUP)):
                if blocks[0] == 0:
                    pe.wait_ge(lin_turned, g + (GROUPS * p + 2))
                    pe.wait_ge(lin_used, g + (GROUPS * p + 1))
                for i, m in enumerate(weights):
                    n = m.shape[-1]
                    for j in blocks:
                        mm = pe.matmul(ps[1 + i][:, j * n:(j + 1) * n], turned[:, j, :], m[:, :], start=True, stop=True)
                    if p == HEADS and i == 0:
                        mm.then_inc(head_values, 1)
                if blocks[-1] == GROUP - 1:
                    mm.then_inc(lin_product, 1)

            def linear(p, weights):
                with pe.Fori(0, GROUPS) as g:
                    transposes(g, p)
                    products(g, p, weights)

            def partials(layer, width, p, weights, extras=()):
                def body(k, linear=False):
                    for j in range(RING):
                        b = j - AT_TRANSPOSES
                        if linear and 0 <= b < GROUP:
                            transposes(k, p, [b])
                        b = j - AT_PRODUCTS
                        if linear and 0 <= b < GROUP:
                            products(k, p, weights, [b])
                        n = k * RING + (STEPS * layer + j + 1)
                        pe.wait_ge(onehot_ready, n)
                        pe.wait_ge(row_scaled, n + SCALED0)
                        pe.wait_ge(block_added, n)
                        pe.matmul(step_sum(j, width), onehot[:, j % HALF, :], scaled[:, j % HALF, 0:width],
                                  start=True, stop=True).then_inc(partial_ready, 1)

                with pe.Fori(0, GROUPS) as k:
                    body(k, linear=True)
                at = GROUPS
                for stop, extra in (*extras, (ITERS, None)):
                    with pe.Fori(at, stop) as k:
                        body(k)
                    if extra:
                        extra()
                    at = stop

            def starts():
                pe.wait_ge(cnt_ready, 1)
                pe.matmul(ps[1][:, 0:BLOCKS], tri[:, :], cnt[:, :], start=True, stop=True)
                pe.matmul(ps[2][:, 0:BLOCKS], ones[:, :], cnt[:, :], start=True, stop=True).then_inc(starts_summed, 1)

            def quads():
                pe.wait_ge(quads_counted, 1)
                pe.matmul(ps[1][:, 0:NC * (BLOCKS - 1)], ones[:, :], cmp[:, 0:NC * (BLOCKS - 1)], start=True, stop=True)\
                    .then_inc(quads_summed, 1)
                pe.wait_ge(offsets_ready, 1)
                for i in range(2 * NC):
                    mm = pe.matmul(ps[2 - i // 8][:, i % 8 * P:(i % 8 + 1) * P], ones[:, :], diag[:, i, :], start=True, stop=True)
                mm.then_inc(offsets_spread, 1)

            partials(0, D + 1, KV, [W["k"], W["v"]])
            pe.wait_ge(agg_done, 1)
            linear(QUERY, [W["q"]])
            linear(OUT0, [W["o"]])
            partials(1, D, ROOT, [W["root"]], [(AT_STARTS, starts), (AT_QUADS, quads)])
            pe.wait_ge(agg_done, 2)
            pe.wait_ge(offsets_spread, 2)
            linear(REL, [W["rel"]])
            partials(2, D, SELF2A, [W["neigh0"], W["self0"]])
            pe.wait_ge(agg_done, 3)
            linear(NEIGH2A, [W["neigh0"]])
            partials(3, D, SELF2B, [W["neigh1"], W["self1"]])
            pe.wait_ge(agg_done, 4)
            linear(NEIGH2B, [W["neigh1"]])
            linear(AGG2, [W["agg"]])
            pe.wait_ge(starts_ready, 1)
            linear(HEADS, [W["heads"], w_lr])
            pe.wait_ge(lin_used, GROUPS * PASSES + 1)
            pe.sem_inc(quad_partial, QRING)
            for c in range(NC):
                pe.wait_ge(carries_ready, c + 1)
                for i in range(6):
                    mm = pe.transpose(ps[1 + i // 4][0:HEADS3, (i % 4) * P:(i % 4 + 1) * P], carry[:, i, :], ident[:, :])
                mm.then_inc(carries_turned, 1)
                pe.wait_ge(chains_ready, c + 1)
                for i in range(2):
                    mm = pe.transpose(ps[3][:, i * HEADS3:(i + 1) * HEADS3], chain_out[:, i, :], ident[0:HEADS3, 0:HEADS3])
                mm.then_inc(chains_turned, 1)
                if c > 0:
                    pe.wait_ge(shift_ready, c)
                    pe.matmul(ps[3][:, 512:512 + HEADS3], seam_place[0:1, c - 1, :], shift[0:1, :], start=True, stop=True)\
                        .then_inc(shift_placed, 1)
                with pe.Fori(0, QITERS[c]) as k:
                    for j in range(QBODY):
                        n = k * QBODY + (QSTEP0[c] + j + 1)
                        pe.wait_ge(quad_ready, n)
                        pe.wait_ge(quad_scaled, n)
                        if c == NC - 1:
                            pe.wait_ge(quarter_scaled, k * QBODY + (j + 1))
                        pe.wait_ge(quad_added, n)
                        for q in range(4):
                            mm = pe.matmul(ps[j % 3][:, 0:AGG_W], quad_onehot[:, j % 3, q, :],
                                           quad_rows[:, j % QRING, q, :].rearrange("p (h f) -> p h f", h=HEADS3)[:, :, 0:DH3 + 1],
                                           start=(q == 0), stop=(q == 3))
                        mm.then_inc(quad_partial, 1)

        @block.vector
        def _(dve):
            done = [0]

            class Chain:
                def __init__(self, per=0, g=None, first=0):
                    self.base, self.n, self.per, self.g = done[0] - per * first, 0, per, g

                def then(self, ins):
                    ins.then_inc(ve, 1)
                    self.n += 1
                    if self.g is None:
                        done[0] += 1
                        dve.wait_ge(ve, self.base + self.n)
                    else:
                        dve.wait_ge(ve, self.g * self.per + (self.base + self.n))

                def close(self, rounds=GROUPS):
                    assert self.n == self.per
                    done[0] += self.per * rounds

            def bc(a, n):
                return a.rearrange("p (j a) -> p j a", a=1).to_broadcast([P, a.shape[-1], n])

            def flat(a):
                return a.rearrange("p j f -> p (j f)")

            def grp(t, g, w=D):
                return t[:, bass.ds(g * GROUP, GROUP), 0:w]

            def pg(i, w=D):
                return ps[i][:, 0:GROUP * w].rearrange("p (j f) -> p j f", f=w)

            def rowbc(t):
                return t.rearrange("p (a f) -> p a f", a=1).to_broadcast([P, GROUP, D])

            NORM_OPS = 4

            def norm(c, g, n):
                for j in range(GROUP):
                    ins = dve.bn_stats(stats[:, j, :], X[:, bass.ds(g * GROUP + j, 1), :].rearrange("p a f -> p (a f)"))
                c.then(ins)
                dve.sem_inc(norm_stats, 1)
                for j in range(GROUP):
                    ins = dve.bn_aggr(moments[:, j, :], stats[:, j, :])
                c.then(ins)
                dve.sem_inc(norm_sum, 1)
                dve.wait_ge(norm_root, g + (GROUPS * n + 1))
                dve.wait_ge(normed, g + (GROUPS * n + 1))
                c.then(dve.reciprocal(small[:, 4, 0:GROUP], small[:, 3, 0:GROUP]))
                c.then(dve.scalar_tensor_tensor(out=small[:, 5, 0:GROUP], in0=moments[:, :, 0], scalar=-1.0,
                                                in1=small[:, 4, 0:GROUP], op0=ALU.mult, op1=ALU.mult))
                dve.sem_inc(norm_scaled, 1)

            def sums(layer, width, other, extras=()):
                def body(k):
                    _, at = nc.values_load_multi_w_load_instructions(
                        step_block[0:1, bass.ds(k * RING, RING)], engines=DVE_ONLY, min_val=0, max_val=BLOCKS - 1,
                        skip_runtime_bounds_check_because="a step's block is below BLOCKS by construction")
                    for half in range(2):
                        for j in range(half * HALF, (half + 1) * HALF):
                            dve.wait_ge(partial_ready, k * RING + (STEPS * layer + j + 1))
                            dve.tensor_scalar(onehot[:, j % HALF, :], iota[:, :],
                                              step_table[:, S_PLACE, bass.ds(k * RING + j, 1)], None, ALU.is_equal)\
                                .then_inc(onehot_ready, 1)
                        for j in range(half * HALF, (half + 1) * HALF):
                            dve.wait_ge(partial_ready, k * RING + (STEPS * layer + j + 1 + PARTIAL0))
                            dve.wait_ge(block_added, k * RING + (STEPS * layer + j + ADDED0))
                            s = AGG[:, bass.ds(at[j], 1), 0:width].rearrange("p a f -> p (a f)")
                            dve.tensor_tensor(s, s, step_sum(j, width), ALU.add).then_inc(block_added, 1)

                dve.memset(AGG[:, :, :].rearrange("p b f -> p (b f)"), 0.0).then_inc(agg_cleared, 1)
                dve.wait_ge(agg_cleared, layer + 1)
                dve.wait_ge(step_table_ready, CHUNKS)
                dve.wait_ge(blocks_loaded, 16)
                per, group = other
                with dve.Fori(0, GROUPS) as k:
                    body(k)
                    c = Chain(per, k)
                    group(c, k)
                c.close()
                at = GROUPS
                for stop, extra in (*extras, (ITERS, None)):
                    with dve.Fori(at, stop) as k:
                        body(k)
                    if extra:
                        extra()
                    at = stop
                dve.wait_ge(block_added, STEPS * (layer + 1) + ADDED0)
                dve.sem_inc(agg_done, 1)

            dve.sem_inc(block_added, ADDED0)
            dve.sem_inc(lin_used, 1)
            c = Chain()
            c.then(dve.memset(chunk_i[:, 1, :], int(PAD_DST)))
            c.then(dve.memset(TR[:, :, 2, :], 0.0))
            c.then(dve.memset(LOGITS, 0.0))
            c.then(dve.memset(X[:, BLOCKS - 1, :], 0.0))
            dve.wait_ge(consts, 1)
            dve.sem_inc(cleared, 2)
            dve.wait_ge(consts, 10)
            c.then(dve.tensor_scalar(ident[:, :], iota[:, :], pidx[:, 0:1], None, ALU.is_equal))
            c.then(dve.tensor_scalar(tri[:, :], iota[:, :], pidx[:, 0:1], None, ALU.is_gt))
            c.then(dve.memset(quad_last_i[:, :], int(PAD_DST)))
            for i in range(NC):
                c.then(dve.memset(quad_count[:, i:i + 1], float(QUADS[i] - 1)))
                c.then(dve.memset(quad_base[:, i:i + 1], float(EDGE0[i] // QUAD)))
            dve.sem_inc(quads_padded, 1)
            dve.wait_ge(loaded_edges, 16 * 9)
            for k in range(2):
                c.then(dve.tensor_copy(TR[:, :, k, :], chunk_i[:, k, :].rearrange("p (c e) -> p c e", e=P)))
            dve.sem_inc(tile_rows_ready, 1)
            c.then(dve.tensor_tensor(cmp[:, :].rearrange("p (b c) -> p b c", c=CHUNKS),
                                     TR[:, :, 1, P - 1:P].rearrange("p c a -> p a c").to_broadcast([P, BLOCKS - 1, CHUNKS]),
                                     block_edge[:, :].rearrange("p (b a) -> p b a", a=1).to_broadcast([P, BLOCKS - 1, CHUNKS]),
                                     ALU.is_lt))
            c.then(dve.tensor_reduce(first_tile[:, :], cmp[:, :].rearrange("p (b c) -> p b c", c=CHUNKS), AX, ALU.add))
            dve.sem_inc(counted, 1)
            dve.wait_ge(summed, 1)
            c.then(dve.tensor_tensor(block_edge[:, :], ps[2][:, 0:BLOCKS - 1], block_no[:, :], ALU.add))
            c.then(dve.tensor_tensor(cmp[:, :].rearrange("p (c b) -> p c b", c=CHUNKS),
                                     block_edge[:, :].rearrange("p (a b) -> p a b", a=1).to_broadcast([P, CHUNKS, BLOCKS - 1]),
                                     step_no[:, :].rearrange("p (c a) -> p c a", a=1).to_broadcast([P, CHUNKS, BLOCKS - 1]),
                                     ALU.is_le))
            c.then(dve.tensor_reduce(step_b[:, :], cmp[:, :].rearrange("p (c b) -> p c b", c=CHUNKS), AX, ALU.add))
            c.then(dve.tensor_tensor(step_t[:, :], step_no[:, :], step_b[:, :], ALU.subtract))
            c.then(dve.tensor_scalar(step_off[:, :], step_b[:, :], -float(P), None, ALU.mult))
            c.then(dve.tensor_copy(step_b_i[:, :], step_b[:, :]))
            c.then(dve.tensor_copy(step_t_i[:, :], step_t[:, :]))
            dve.sem_inc(step_index_ready, 1)

            def stats_of(first, end):
                with dve.Fori(first, end) as g:
                    c = Chain(3, g, first)
                    for j in range(GROUP):
                        ins = dve.bn_stats(stats[:, j, :], X[:, bass.ds(g * GROUP + j, 1), :].rearrange("p a f -> p (a f)"))
                    c.then(ins)
                    dve.sem_inc(norm_stats, 1)
                    for j in range(GROUP):
                        ins = dve.bn_aggr(moments[:, j, :], stats[:, j, :])
                    c.then(ins)
                    c.then(dve.tensor_copy(moments0[:, bass.ds(g * GROUP, GROUP), :], moments[:, :, :]))
                    dve.sem_inc(norm_sum, 1)
                c.close(end - first)

            dve.wait_ge(loaded_x, 32)
            dve.sem_inc(norm_stats, 1)
            stats_of(0, GROUPS // 2 + 1)
            c = Chain()
            for i, (cc, at) in enumerate(ATTR):
                dve.wait_ge(loaded_attr[i], 16 if i < 4 else 32)
                n = cc.stop - cc.start
                a = scratch[:, at:at + n * EAW].rearrange("p (c e a) -> p c e a", c=n, a=EDGE_ATTRS)
                if i < 4:
                    dve.tensor_reduce(LOGITS[:, cc, :], a, AX, ALU.add).then_inc(logits_ready, 1)
                else:
                    c.then(dve.tensor_reduce(LOGITS[0:rest + 1, 12, 0:tail], a[0:rest + 1, 0, 0:tail, :], AX, ALU.add))
                    dve.tensor_reduce(LOGITS[0:rest, 12, tail:P], a[0:rest, 0, tail:P, :], AX, ALU.add)\
                        .then_inc(logits_ready, 1)
                dve.wait_ge(logits_ready, i + 1)
                dve.sem_inc(attr_used, 1)
                if i == 1:
                    stats_of(GROUPS // 2 + 1, GROUPS)
                    dve.wait_ge(norm_root, GROUPS)
                    c = Chain()
                    c.then(dve.reciprocal(scale0, root0))
                    c.then(dve.scalar_tensor_tensor(out=shift0, in0=moments0[:, :, 0], scalar=-1.0, in1=scale0,
                                                    op0=ALU.mult, op1=ALU.mult))
                    dve.sem_inc(norm_scaled, GROUPS)
            c = Chain()
            for ch in range(CHUNKS):
                dve.wait_ge(step_rows_landed[ch >= 6], 16 * (6 if ch < 6 else CHUNKS - 6))
                c.then(dve.tensor_scalar(GATHER_STEPS[:, ch, 1, :], GATHER_STEPS[:, ch, 1, :], step_off[:, ch:ch + 1],
                                         None, ALU.add))
                dve.sem_inc(step_rows_ready, 1)
            dve.wait_ge(loaded_w, 16 * WLOADS)
            for i in range(2):
                c.then(dve.tensor_tensor(bsum[:, i, :], bias[f"self{i}"][:, :], bias[f"neigh{i}"][:, :], ALU.add))
                c.then(dve.tensor_tensor(bsum[:, i, :], bsum[:, i, :], bias[f"layer{i}"][:, :], ALU.add))
            dve.wait_ge(step_turned, CHUNKS)
            dve.wait_ge(table_stored, 16 * GROUPS)

            def products(p, g):
                dve.wait_ge(lin_product, g + (GROUPS * p + 2))

            def keys_values(c, g):
                products(KV, g)
                c.then(dve.tensor_copy(grp(R, g), pg(1)))
                c.then(dve.tensor_copy(grp(H, g), pg(2)))
                dve.sem_inc(lin_used, 1)
                c.then(dve.tensor_tensor(grp(X, g), grp(X, g), rowbc(bias["o"][:, :]), ALU.add))

            sums(0, D + 1, (3, keys_values))
            c = Chain()
            c.then(dve.tensor_copy(cnt[:, :], AGG[:, :, D]))
            c.then(dve.tensor_scalar(inv_mean0[:, :], cnt[:, :], 1.0, None, ALU.max))
            c.then(dve.reciprocal(inv_mean0[:, :], inv_mean0[:, :]))
            c.then(dve.tensor_scalar(inv_mean0[:, :], inv_mean0[:, :], SCALE0, None, ALU.mult))
            c.then(dve.tensor_scalar(inv_mean2[:, :], cnt[:, :], 1.0, None, ALU.add))
            c.then(dve.reciprocal(inv_mean2[:, :], inv_mean2[:, :]))
            dve.sem_inc(cnt_ready, 1)
            with dve.Fori(0, GROUPS) as g:
                c = Chain(4, g)
                products(QUERY, g)
                c.then(dve.tensor_tensor(cen, pg(1), grp(R, g), ALU.mult))
                dve.sem_inc(lin_used, 1)
                sc = small[:, 6, 0:GROUP * HEADS0]
                c.then(dve.tensor_reduce(sc, flat(cen).rearrange("p (h d) -> p h d", d=DH0), AX, ALU.add))
                c.then(dve.tensor_tensor(sc.rearrange("p (j h) -> p j h", h=HEADS0), sc.rearrange("p (j h) -> p j h", h=HEADS0),
                                         bc(inv_mean0[:, bass.ds(g * GROUP, GROUP)], HEADS0), ALU.mult))
                v = flat(grp(H, g)).rearrange("p (h d) -> p h d", d=DH0)
                c.then(dve.tensor_tensor(v, v, bc(sc, DH0), ALU.mult))
                dve.sem_inc(rows_written, 1)
            c.close()
            with dve.Fori(0, GROUPS) as g:
                c = Chain(1 + NORM_OPS, g)
                products(OUT0, g)
                c.then(dve.tensor_tensor(grp(X, g), grp(X, g), pg(1), ALU.add))
                dve.sem_inc(lin_used, 1)
                norm(c, g, 1)
            c.close()
            def root_terms(c, g):
                products(ROOT, g)
                c.then(dve.tensor_tensor(grp(R, g), pg(1), rowbc(bias["rel"][:, :]), ALU.add))
                dve.sem_inc(lin_used, 1)

            def starts():
                dve.wait_ge(starts_summed, 1)
                c = Chain()
                c.then(dve.tensor_copy(before[:, 0, :], ps[2][:, 0:BLOCKS]))
                c.then(dve.tensor_tensor_scan(before[:, 1, :], before[:, 0, :], zeros[:, 0:BLOCKS], 0.0, ALU.add, ALU.add))
                c.then(dve.tensor_tensor(before[:, 1, :], before[:, 1, :], before[:, 0, :], ALU.subtract))
                c.then(dve.tensor_tensor(before[:, 1, :], before[:, 1, :], ps[1][:, 0:BLOCKS], ALU.add))
                c.then(dve.tensor_scalar(before[:, 2, :], cnt[:, :], 0.0, float(2 * E_PAD), ALU.is_equal, ALU.mult))
                c.then(dve.tensor_tensor(first_edge[:, :], before[:, 1, :], before[:, 2, :], ALU.add))
                for i, k_ in enumerate(("left", "right")):
                    c.then(dve.tensor_tensor(W[k_][:, :], W[k_][:, :], W["heads"][:, :], ALU.mult))
                    c.then(dve.tensor_reduce(w_lr[:, i * HEADS3:(i + 1) * HEADS3], W[k_][:, :].rearrange("p (h o) -> p h o", o=DH3),
                                             AX, ALU.add))
                dve.sem_inc(starts_ready, 1)

            def quads():
                NB = BLOCKS - 1
                c = Chain()
                dve.wait_ge(quads_loaded, 16 * (2 * NC - 1))
                c.then(dve.tensor_copy(quad_last[:, :], quad_last_i[:, :]))
                quad_cmp = cmp[:, 0:NC * NB].rearrange("p (c b) -> p c b", c=NC)
                quad_cmp2 = cmp[:, NC * NB:2 * NC * NB].rearrange("p (c b) -> p c b", c=NC)
                c.then(dve.tensor_tensor(quad_cmp, quad_last[:, :].rearrange("p (c a) -> p c a", a=1).to_broadcast([P, NC, NB]),
                                         block_start[:, :].rearrange("p (a b) -> p a b", a=1).to_broadcast([P, NC, NB]), ALU.is_lt))
                dve.sem_inc(quads_counted, 1)
                dve.wait_ge(quads_summed, 1)
                c.then(dve.tensor_tensor(quad_cmp2, ps[1][:, 0:NC * NB].rearrange("p (c b) -> p c b", c=NC),
                                         block_no[:, :].rearrange("p (a b) -> p a b", a=1).to_broadcast([P, NC, NB]), ALU.add))
                for i in range(2):
                    c.then(dve.tensor_scalar(quad_cmp, quad_cmp2, step_no[:, i:i + 1], None, ALU.is_le))
                    c.then(dve.tensor_reduce(quad_b[:, i, :], quad_cmp, AX, ALU.add))
                    c.then(dve.tensor_scalar(quad_t[:, i, :], quad_b[:, i, :], -1.0, step_no[:, i:i + 1], ALU.mult, ALU.add))
                    c.then(dve.tensor_tensor(quad_over[:, i, :], quad_t[:, i, :], quad_count[:, :], ALU.is_gt))
                    c.then(dve.tensor_tensor(quad_t[:, i, :], quad_t[:, i, :], quad_count[:, :], ALU.min))
                    c.then(dve.tensor_tensor(quad_i[:, 1, i, :], quad_t[:, i, :], quad_base[:, :], ALU.add))
                    c.then(dve.tensor_copy(quad_i[:, 0, i, :], quad_b[:, i, :]))
                dve.sem_inc(quads_ready, 1)
                c.then(dve.tensor_scalar(quad_over[:, :, :], quad_over[:, :, :], -2 * PAD_DST, None, ALU.mult))
                c.then(dve.scalar_tensor_tensor(out=quad_over[:, :, :], in0=quad_b[:, :, :], scalar=-float(P),
                                                in1=quad_over[:, :, :], op0=ALU.mult, op1=ALU.add))
                for i in range(2 * NC):
                    c.then(dve.tensor_scalar(diag[:, i, :], ident[:, :], quad_over[:, i % 2, i // 2:i // 2 + 1], None, ALU.mult))
                dve.sem_inc(offsets_ready, 1)
                dve.wait_ge(offsets_spread, 1)
                c.then(dve.tensor_copy(quad_off[:, 0:4, :].rearrange("p c s -> p (c s)"), ps[2][:, :]))
                c.then(dve.tensor_copy(quad_off[:, 4:, :].rearrange("p c s -> p (c s)"), ps[1][:, 0:(NC - 4) * QCOLS]))
                dve.sem_inc(offsets_spread, 1)
                c.then(dve.tensor_copy(seam[:, 0, :], seam_i[:, :]))
                ns = NC - 1
                seam_cmp = cmp[:, 0:ns * NB].rearrange("p (c b) -> p c b", c=ns)
                c.then(dve.tensor_tensor(seam_cmp, block_start[:, :].rearrange("p (a b) -> p a b", a=1).to_broadcast([P, ns, NB]),
                                         seam[:, 0, :].rearrange("p (c a) -> p c a", a=1).to_broadcast([P, ns, NB]), ALU.is_le))
                c.then(dve.tensor_reduce(seam[:, 1, :], seam_cmp, AX, ALU.add))
                c.then(dve.tensor_copy(seam_b[:, :], seam[:, 1, :]))
                c.then(dve.scalar_tensor_tensor(out=seam[:, 2, :], in0=seam[:, 1, :], scalar=-float(P), in1=seam[:, 0, :],
                                                op0=ALU.mult, op1=ALU.add))
                for i in range(ns):
                    c.then(dve.tensor_scalar(seam_place[:, i, :], iota[:, :], seam[:, 2, i:i + 1], None, ALU.is_equal))

            sums(1, D, (1, root_terms), [(AT_STARTS, starts), (AT_QUADS, quads)])
            with dve.Fori(0, GROUPS) as g:
                c = Chain(2 + NORM_OPS, g)
                products(REL, g)
                c.then(dve.tensor_tensor(cen, pg(1), grp(R, g), ALU.add))
                dve.sem_inc(lin_used, 1)
                c.then(dve.scalar_tensor_tensor(out=grp(X, g), in0=cen, scalar=0.0, in1=grp(X, g), op0=ALU.max, op1=ALU.add))
                dve.sem_inc(rows_written, 1)
                norm(c, g, 2)
            c.close()

            def self_terms(p, i, with_bias):
                def group(c, g):
                    products(p, g)
                    c.then(dve.tensor_tensor(cen, pg(1), bc(inv_mean2[:, bass.ds(g * GROUP, GROUP)], D), ALU.mult))
                    c.then(dve.tensor_tensor(cen, cen, pg(2), ALU.add))
                    dve.sem_inc(lin_used, 1)
                    c.then(dve.tensor_tensor(grp(R, g), cen, rowbc(bsum[:, i, :]), ALU.add))
                    if with_bias:
                        c.then(dve.tensor_tensor(grp(X, g), grp(X, g), rowbc(bias["agg"][:, :]), ALU.add))
                return 3 + with_bias, group

            def neighbours(p):
                with dve.Fori(0, GROUPS) as g:
                    c = Chain(3, g)
                    products(p, g)
                    c.then(dve.tensor_tensor(cen, pg(1), bc(inv_mean2[:, bass.ds(g * GROUP, GROUP)], D), ALU.mult))
                    dve.sem_inc(lin_used, 1)
                    c.then(dve.tensor_tensor(cen, cen, grp(R, g), ALU.add))
                    c.then(dve.scalar_tensor_tensor(out=grp(H, g), in0=cen, scalar=SLOPE, in1=cen, op0=ALU.mult, op1=ALU.max))
                    dve.sem_inc(rows_written, 1)
                c.close()

            sums(2, D, self_terms(SELF2A, 0, 1))
            neighbours(NEIGH2A)
            sums(3, D, self_terms(SELF2B, 1, 0))
            dve.wait_ge(idx_staged, 2 * (ITERS + 1) * 4)
            c = Chain()
            c.then(dve.memset(run_src, 0))
            c.then(dve.memset(run_dst, int(PAD_DST)))
            c.then(dve.memset(run_dst[:, 0:1], -1))
            c.then(dve.memset(logw, 1.0))
            dve.sem_inc(runs_padded, 1)
            neighbours(NEIGH2B)
            with dve.Fori(0, GROUPS) as g:
                c = Chain(1 + NORM_OPS, g)
                products(AGG2, g)
                c.then(dve.tensor_tensor(grp(X, g), grp(X, g), pg(1), ALU.add))
                dve.sem_inc(lin_used, 1)
                norm(c, g, 3)
            c.close()

            c = Chain()
            c.then(dve.memset(HT[:, :, :, DH3:DH3 + 1], 1.0))
            with dve.Fori(0, GROUPS) as g:
                c = Chain(4, g)
                dve.wait_ge(head_values, g + 1)
                ht = HT[:, bass.ds(g * GROUP, GROUP), :, :]
                c.then(dve.tensor_copy(ht[:, :, :, 0:DH3], pg(1).rearrange("p j (h f) -> p j h f", f=DH3)))
                products(HEADS, g)
                lr = ps[2][:, 0:GROUP * 2 * HEADS3].rearrange("p (j k h) -> p j k h", k=2, h=HEADS3)
                c.then(dve.tensor_copy(ht[:, :, :, DH3 + 1], lr[:, :, 0, :]))
                c.then(dve.tensor_copy(right[:, bass.ds(g * GROUP, GROUP), :], lr[:, :, 1, :]))
                dve.sem_inc(heads_ready, 1)
                dve.sem_inc(lin_used, 1)
                c.then(dve.tensor_tensor(grp(X, g), grp(X, g), rowbc(bias["out"][:, :]), ALU.add))
            c.close()
            c = Chain()
            c.then(dve.memset(right0[:, :, :], 0.0))
            dve.wait_ge(runs_loaded, 16 * RUN_LOADS)
            for i in range(NC):
                c.then(dve.tensor_copy(dst0[:, i:i + 1], run_dst[:, RUN0[i] + 2 * i + 1:RUN0[i] + 2 * i + 2]))
            dve.sem_inc(dst0_ready, 1)
            c.then(dve.tensor_scalar(logw, logw, 1e-8, None, ALU.max))
            dve.sem_inc(logw_ready, 1)
            dve.wait_ge(heads_stored, 16 * GROUPS)
            c.then(dve.memset(AGG.rearrange("p b f -> p (b f)"), 0.0))
            dve.wait_ge(logw_ready, 2)
            dve.wait_ge(right0_loaded, 16 * NC)
            dve.wait_ge(quad_row_loaded, 32)
            dve.sem_inc(quad_added, 3)

            def softmax(i):
                S = SPAN[i]
                rec = record[i % 2].rearrange("p (t r) -> p t r", r=REC)[:, 0:S, :]
                score = rec[:, :, 0:HEADS3]
                right_e = right_b[:, 0:S * HEADS3].rearrange("p (t h) -> p t h", h=HEADS3)
                same, keep, fwd, bwd = same_b[:, 0:S + 1], keep_b[:, 0:S + 1], fwd_b[:, 0:S], bwd_b[:, 0:S]
                dst_x = dst_b[:, 0:S + 2]
                o = RUN0[i] + 2 * i
                c.then(dve.tensor_copy(dst_x, run_dst[:, o:o + S + 2]))
                c.then(dve.tensor_tensor(same, dst_x[:, 1:], dst_x[:, 0:S + 1], ALU.is_equal))
                c.then(dve.tensor_scalar(keep, same, 0.5, 2 * BIG, ALU.subtract, ALU.mult))
                dve.wait_ge(right_loaded, 16 * (i + 1))
                for h in range(HEADS3):
                    c.then(dve.tensor_tensor_scan(right_e[:, :, h], same[:, 0:S], right_e[:, :, h], right0[:, i, h:h + 1],
                                                  ALU.mult, ALU.add))
                dve.wait_ge(score_taken, 2 * ITER0[i + 1])
                c.then(dve.tensor_tensor(score, score, right_e, ALU.add))
                dve.sem_inc(right_used, 1)
                c.then(dve.scalar_tensor_tensor(out=score, in0=score, scalar=SLOPE, in1=score, op0=ALU.mult, op1=ALU.max))
                c.then(dve.tensor_tensor(score, score, logw[:, RUN0[i]:RUN0[i + 1]].rearrange("p (t a) -> p t a", a=1)
                                         .to_broadcast([P, S, HEADS3]), ALU.add))
                c.then(dve.tensor_copy(rec[:, :, HEADS3], dst_x[:, 1:S + 1]))

                def forward(h, initial):
                    c.then(dve.tensor_tensor_scan(fwd, keep[:, 0:S], score[:, :, h], initial, ALU.min, ALU.max))

                def backward(initial):
                    c.then(dve.tensor_tensor_scan(bwd[:, ::-1], keep[:, 1:S + 1][:, ::-1], fwd[:, ::-1], initial, ALU.min, ALU.max))

                for h in range(HEADS3):
                    forward(h, -BIG)
                    c.then(dve.tensor_copy(carry[:, 0, h:h + 1], fwd[:, S - 1:S]))
                    backward(-BIG)
                    c.then(dve.tensor_copy(carry[:, 3, h:h + 1], bwd[:, 0:1]))

                def flag(k, a, b):
                    c.then(dve.tensor_tensor(carry_in[:, 0, 0:1], dst_x[:, a:a + 1], dst_x[:, b:b + 1], ALU.is_equal))
                    c.then(dve.tensor_scalar(carry[:, k, :], carry_in[:, 0, 0:1].to_broadcast([P, HEADS3]), 0.5, 2 * BIG,
                                             ALU.subtract, ALU.mult))
                flag(1, 0, S)
                flag(2, 0, 1)
                flag(4, 1, S + 1)
                flag(5, S, S + 1)
                dve.sem_inc(carries_ready, 1)
                dve.wait_ge(carries_turned, i + 1)
                c.then(dve.tensor_copy(chain[:, 0:4, :].rearrange("h k p -> h (k p)"), ps[1][0:HEADS3, 0:4 * P]))
                c.then(dve.tensor_copy(chain[:, 4:6, :].rearrange("h k p -> h (k p)"), ps[2][0:HEADS3, 0:2 * P]))
                lo, hi = slice(0, P - 1), slice(1, P)
                c.then(dve.memset(chain_out[:, 0:2, :], -BIG))
                if i:
                    c.then(dve.tensor_tensor(chain_out[:, 0, 0:1], chain_end[:, :], chain[:, 2, 0:1], ALU.min))
                c.then(dve.tensor_tensor_scan(chain_out[:, 2, :], chain[:, 1, :], chain[:, 0, :], chain_end[:, 0:1] if i else -BIG,
                                              ALU.min, ALU.max))
                c.then(dve.tensor_tensor(chain_out[:, 0, hi], chain_out[:, 2, lo], chain[:, 2, hi], ALU.min))
                c.then(dve.tensor_tensor_scan(chain_out[:, 3, ::-1], chain[:, 4, ::-1], chain[:, 3, ::-1], -BIG, ALU.min, ALU.max))
                c.then(dve.tensor_tensor(chain_out[:, 1, lo], chain_out[:, 3, hi], chain[:, 5, lo], ALU.min))
                c.then(dve.tensor_copy(chain_end[:, :], chain_out[:, 2, P - 1:P]))
                dve.sem_inc(chains_ready, 1)
                dve.wait_ge(chains_turned, i + 1)
                c.then(dve.tensor_copy(carry_in[:, :, :].rearrange("p k h -> p (k h)"), ps[3][:, 0:2 * HEADS3]))
                for h in range(HEADS3):
                    forward(h, carry_in[:, 0, h:h + 1])
                    backward(carry_in[:, 1, h:h + 1])
                    c.then(dve.tensor_copy(shift[:, h:h + 1], bwd[:, 0:1]))
                    c.then(dve.tensor_tensor(score[:, :, h], score[:, :, h], bwd, ALU.subtract))
                dve.sem_inc(exponents_ready, 1)
                if i:
                    c.then(dve.tensor_tensor(shift[:, :], carry_in[:, 0, :], shift[:, :], ALU.subtract))
                    c.then(dve.tensor_scalar(shift[:, :], shift[:, :], same[:, 0:1], None, ALU.mult))
                    dve.sem_inc(shift_ready, 1)
                    dve.wait_ge(factor_ready, i)
                    _, at = nc.values_load_multi_w_load_instructions(
                        seam_b[0:1, i - 1:i], engines=DVE_ONLY, min_val=0, max_val=BLOCKS - 1,
                        skip_runtime_bounds_check_because="a node's block is below BLOCKS")
                    a = AGG[:, bass.ds(at[0], 1), :].rearrange("p a (h f) -> p (a h) f", h=HEADS3)
                    c.then(dve.tensor_tensor(a, a, factor[:, :].rearrange("p (h a) -> p h a", a=1)
                                             .to_broadcast([P, HEADS3, DH3 + 1]), ALU.mult))

            def quad_sums(i):
                def prepare(k, j):
                    n = k * QBODY + (QSTEP0[i] + j + 1)
                    slot = j % QRING
                    rec = quad_rec[:, slot, :].rearrange("p (q r) -> p q r", r=REC)
                    place = quad_place[:, j % 4, :]
                    dve.wait_ge(quad_landed[slot], k * 64 + (32 * (QSTEP0[i] // QRING + j // QRING + 1)))
                    last_chunk = i == NC - 1
                    Q = 3 if last_chunk else 4
                    if not last_chunk:
                        dve.tensor_scalar(place, rec[:, :, HEADS3], quad_off[:, i, bass.ds(k * QBODY + j, 1)], None,
                                          ALU.add).then_inc(quad_placed, 1)
                    rows_ = quad_rows[:, slot, 0:Q, :].rearrange("p q (h f) -> p q h f", h=HEADS3)[:, :, :, 0:DH3 + 1]
                    al = rec[:, 0:Q, 0:HEADS3].rearrange("p q (h a) -> p q h a", a=1).to_broadcast([P, Q, HEADS3, DH3 + 1])
                    dve.tensor_tensor(rows_, rows_, al, ALU.mult).then_inc(quad_scaled, 1)
                    dve.wait_ge(quad_placed, n)
                    dve.wait_ge(quad_partial, n + (QRING - 3))
                    dve.tensor_tensor(quad_onehot[:, j % 3, :, :],
                                      iota[:, :].rearrange("p (a d) -> p a d", a=1).to_broadcast([P, 4, P]),
                                      place.rearrange("p (q a) -> p q a", a=1).to_broadcast([P, 4, P]),
                                      ALU.is_equal).then_inc(quad_ready, 1)

                def add(k, j, at):
                    n = k * QBODY + (QSTEP0[i] + j)
                    dve.wait_ge(quad_partial, n + (1 + QRING))
                    dve.wait_ge(quad_added, n + 3)
                    a = AGG[:, bass.ds(at[j], 1), :].rearrange("p a f -> p (a f)")
                    dve.tensor_tensor(a, a, ps[j % 3][:, 0:AGG_W], ALU.add)\
                        .then_inc(quad_added, 1)

                def body(k, ahead):
                    _, at = nc.values_load_multi_w_load_instructions(
                        quad_row[0:1, 0, bass.ds(k * QBODY + QCOLS * i, QBODY)], engines=DVE_ONLY, min_val=0, max_val=BLOCKS - 1,
                        skip_runtime_bounds_check_because="a quad step's block is below BLOCKS by construction")
                    for j in range(QBODY):
                        if j + 2 < QBODY or ahead:
                            prepare(k, j + 2)
                        add(k, j, at)

                prepare(0, 0)
                prepare(0, 1)
                with dve.Fori(0, QITERS[i] - 1) as k:
                    body(k, True)
                body(QITERS[i] - 1, False)
                dve.wait_ge(quad_added, QSTEP0[i + 1] + 3)

            for i in range(NC):
                softmax(i)
                quad_sums(i)
            agg3 = AGG.rearrange("p b (h f) -> p b h f", f=DH3 + 1)
            c = Chain()
            weight_sum = quad_off[:, :, :].rearrange("p c s -> p (c s)")[:, 0:BLOCKS * HEADS3]
            ws4 = weight_sum.rearrange("p (b h) -> p b h", h=HEADS3)
            c.then(dve.tensor_copy(ws4, agg3[:, :, :, DH3]))
            c.then(dve.tensor_scalar(weight_sum, weight_sum, 1e-8, None, ALU.add))
            c.then(dve.reciprocal(weight_sum, weight_sum))
            with dve.Fori(0, GROUPS) as g:
                c = Chain(2, g)
                at = bass.ds(g * GROUP, GROUP)
                c.then(dve.tensor_tensor(cen.rearrange("p j (h f) -> p j h f", f=DH3), agg3[:, at, :, 0:DH3],
                                         ws4[:, at, :].rearrange("p j (h a) -> p j h a", a=1).to_broadcast([P, GROUP, HEADS3, DH3]),
                                         ALU.mult))
                c.then(dve.tensor_tensor(grp(X, g), grp(X, g), cen, ALU.add))
                dve.sem_inc(out_ready, 1)
            c.close()


def kernel(**inputs):
    import numpy as np
    import concourse.bacc as bacc
    from concourse.bass_utils import run_bass_kernel_spmd

    def a(name):
        return np.asarray(inputs[name])

    arrays = {
        "x": a("x"), "src": a("src"), "dst": a("dst"), "edge_attr": a("edge_attr_16"), "edge_weight": a("edge_weight"),
        "q": a("L0_gnn_w_q"), "k": a("L0_gnn_w_k"), "v": a("L0_gnn_w_v"), "o": a("L0_gnn_w_o"),
        "rel": a("L1_gnn_W_rel").T, "root": a("L1_gnn_W_root").T,
        "self0": a("L2_gnn_W_self")[0].T, "self1": a("L2_gnn_W_self")[1].T,
        "neigh0": a("L2_gnn_W_neigh")[0].T, "neigh1": a("L2_gnn_W_neigh")[1].T, "agg": a("L2_gnn_W_agg").T,
        "b_o": a("L0_gnn_b_o"), "b_rel": a("L1_gnn_b_rel"),
        "b_self0": a("L2_gnn_b_self")[0], "b_self1": a("L2_gnn_b_self")[1],
        "b_neigh0": a("L2_gnn_b_neigh")[0], "b_neigh1": a("L2_gnn_b_neigh")[1],
        "b_layer0": a("L2_gnn_layer_bias")[0], "b_layer1": a("L2_gnn_layer_bias")[1], "b_agg": a("L2_gnn_b_agg"),
        "heads": a("L3_gnn_W").transpose(1, 0, 2).reshape(D, HEADS3 * DH3),
        "left": a("L3_gnn_a_l").reshape(-1), "right": a("L3_gnn_a_r").reshape(-1), "b_out": a("L3_gnn_bias"),
    }
    nc = bacc.Bacc("TRN2", target_bir_lowering=False, num_devices=1)
    arrays = {k: np.ascontiguousarray(v) for k, v in arrays.items()}
    aps = {k: nc.dram_tensor(f"in_{k}", v.shape, mybir.dt.from_np(v.dtype), kind="ExternalInput").ap()
           for k, v in arrays.items()}
    out = nc.dram_tensor("out", (N, D), F32, kind="ExternalOutput").ap()
    build(nc, aps["x"], aps["src"], aps["dst"], aps["edge_attr"], aps["edge_weight"], aps, out)
    r = run_bass_kernel_spmd(nc, [{f"in_{k}": v for k, v in arrays.items()}], core_ids=[0])
    return r.results[0]["out"]
```
